# Optimizing a Trainium2 kernel written in Bass

```python
import numpy as np
import jax
import jax.numpy as jnp

def _softmax(x, axis=-1):
    return jax.nn.softmax(x, axis=axis)

def _gelu(x):
    return jax.nn.gelu(x, approximate=True)

def _silu(x):
    return jax.nn.silu(x)

def _sigmoid(x):
    return jax.nn.sigmoid(x)

def _layernorm(x, axis=-1, eps=1e-05):
    m = jnp.mean(x, axis=axis, keepdims=True)
    v = jnp.var(x, axis=axis, keepdims=True)
    return (x - m) / jnp.sqrt(v + eps)

def _scatter_add(tgt, idx, src, axis=0):
    return tgt.at[idx].add(src)

def _segment_sum(src, seg, n):
    return jax.ops.segment_sum(src, seg, n)
kernel_name = 'mk_gnn_resnorm_d4_gnn_r16_346903'

def setup_inputs(seed: int=0):
    np.random.seed(seed)
    _w = jnp.asarray

    def _rec_inputs():
        import jax
        import jax.numpy as jnp
        _gk = jax.random.key(seed)
        x = -0.000202 + 1 * jax.random.normal(jax.random.fold_in(_gk, 1), (6250, 128), jnp.float32)
        _s = jax.random.randint(jax.random.fold_in(_gk, 2), (50000,), 0, 6250, jnp.int32)
        _d = jax.random.randint(jax.random.fold_in(_gk, 3), (50000,), 0, 6250, jnp.int32)
        _loop = jnp.arange(6250, dtype=jnp.int32)
        src = jnp.concatenate([_s, _d, _loop])
        dst = jnp.concatenate([_d, _s, _loop])
        _o = jnp.argsort(dst, stable=True)
        src = src[_o]
        dst = dst[_o]
        edge_attr_128 = -8.16379e-05 + 0.999858 * jax.random.normal(jax.random.fold_in(_gk, 12), (106250, 128), jnp.float32)
        edge_weight = jax.random.uniform(jax.random.fold_in(_gk, 14), (106250,), jnp.float32, 0.0, 0.999998)
        return (x, src, dst, edge_attr_128, edge_weight)
    x, src, dst, edge_attr_128, edge_weight = _rec_inputs()

    def _L0_gnn_setup():
        import jax, jax.numpy as jnp
        import numpy as np
        N_NODES = 3125
        N_EDGES = 50000
        DIM = 128
        N_LAYERS = 3
        BN_EPS = 1e-05

        def _batchnorm(h, gamma, beta):
            mu = jnp.mean(h, axis=0)
            var = jnp.var(h, axis=0)
            return gamma * (h - mu) * jax.lax.rsqrt(var + BN_EPS) + beta
        key = jax.random.key(seed)
        ks = jax.random.split(key, 12)
        x = jax.random.normal(ks[0], (N_NODES, DIM), dtype=jnp.float32)
        edge_index = jax.random.randint(ks[1], (2, N_EDGES), 0, N_NODES, dtype=jnp.int64)
        W1 = jax.random.normal(ks[2], (N_LAYERS, DIM, DIM), dtype=jnp.float32) * 0.05
        b1 = jnp.zeros((N_LAYERS, DIM), dtype=jnp.float32)
        g1 = jnp.ones((N_LAYERS, DIM), dtype=jnp.float32)
        be1 = jnp.zeros((N_LAYERS, DIM), dtype=jnp.float32)
        W2 = jax.random.normal(ks[3], (N_LAYERS, DIM, DIM), dtype=jnp.float32) * 0.05
        b2 = jnp.zeros((N_LAYERS, DIM), dtype=jnp.float32)
        gbn = jnp.ones((N_LAYERS - 1, DIM), dtype=jnp.float32)
        bbn = jnp.zeros((N_LAYERS - 1, DIM), dtype=jnp.float32)
        return {'x': x, 'edge_index': edge_index, 'W1': W1, 'b1': b1, 'g1': g1, 'be1': be1, 'W2': W2, 'b2': b2, 'gbn': gbn, 'bbn': bbn}
    _L0_gnn_all = _L0_gnn_setup()
    _L0_gnn_in = {k: v for k, v in _L0_gnn_all.items() if k in ('W1', 'b1', 'g1', 'be1', 'W2', 'b2', 'gbn', 'bbn')}
    del _L0_gnn_all

    def _L1_gnn_setup():
        import jax, jax.numpy as jnp
        import numpy as np
        N_NODES = 6250
        DIM = 128
        N_EDGES = 40000
        key = jax.random.key(seed)
        k_x, k_e, k_w1, k_b1, k_w2, k_b2 = jax.random.split(key, 6)
        x = jax.random.normal(k_x, (N_NODES, DIM), dtype=jnp.float32)
        edge_index = jax.random.randint(k_e, (2, N_EDGES), 0, N_NODES, dtype=jnp.int64)
        s = 1.0 / np.sqrt(DIM)
        W1 = jax.random.uniform(k_w1, (DIM, DIM), minval=-s, maxval=s, dtype=jnp.float32)
        b1 = jax.random.uniform(k_b1, (DIM,), minval=-s, maxval=s, dtype=jnp.float32)
        W2 = jax.random.uniform(k_w2, (DIM, DIM), minval=-s, maxval=s, dtype=jnp.float32)
        b2 = jax.random.uniform(k_b2, (DIM,), minval=-s, maxval=s, dtype=jnp.float32)
        return {'x': x, 'edge_index': edge_index, 'W1': W1, 'b1': b1, 'W2': W2, 'b2': b2}
    _L1_gnn_all = _L1_gnn_setup()
    _L1_gnn_in = {k: v for k, v in _L1_gnn_all.items() if k in ('W1', 'b1', 'W2', 'b2')}
    del _L1_gnn_all

    def _L2_gnn_setup():
        import jax, jax.numpy as jnp
        import numpy as np
        N_NODES = 6250
        N_EDGES = 37500
        DIM = 128
        BN_EPS = 1e-05
        key = jax.random.key(seed)
        k = jax.random.split(key, 6)
        x = jax.random.normal(k[0], (N_NODES, DIM), dtype=jnp.float32)
        ei = jax.random.randint(k[1], (2, N_EDGES), 0, N_NODES, dtype=jnp.int64)
        W_l = jax.random.normal(k[2], (DIM, DIM), dtype=jnp.float32) * 0.05
        b_l = jnp.zeros((DIM,), dtype=jnp.float32)
        W_r = jax.random.normal(k[3], (DIM, DIM), dtype=jnp.float32) * 0.05
        gamma = jnp.ones((DIM,), dtype=jnp.float32)
        beta = jnp.zeros((DIM,), dtype=jnp.float32)
        return {'x': x, 'ei': ei, 'W_l': W_l, 'b_l': b_l, 'W_r': W_r, 'gamma': gamma, 'beta': beta}
    _L2_gnn_all = _L2_gnn_setup()
    _L2_gnn_in = {k: v for k, v in _L2_gnn_all.items() if k in ('W_l', 'b_l', 'W_r', 'gamma', 'beta')}
    del _L2_gnn_all

    def _L3_gnn_setup():
        import jax, jax.numpy as jnp
        import numpy as np
        N_NODES = 3125
        N_EDGES = 50000
        D = 128
        EPS = 1e-12
        key = jax.random.key(seed)
        ks = jax.random.split(key, 12)
        s = 1.0 / np.sqrt(D)
        return {'node_features': jax.random.normal(ks[0], (N_NODES, D), jnp.float32), 'edge_features': jax.random.normal(ks[1], (N_EDGES, D), jnp.float32), 'src': jax.random.randint(ks[2], (N_EDGES,), 0, N_NODES, jnp.int32), 'dst': jax.random.randint(ks[3], (N_EDGES,), 0, N_NODES, jnp.int32), 'edge_weight_raw': jax.random.uniform(ks[4], (N_EDGES,), jnp.float32), 'W_pool': jax.random.normal(ks[5], (D, D), jnp.float32) * s, 'b_pool': jnp.zeros((D,), jnp.float32), 'W1_self': jax.random.normal(ks[6], (D, D), jnp.float32) * s, 'W1_neigh': jax.random.normal(ks[7], (D, D), jnp.float32) * s, 'b1': jnp.zeros((D,), jnp.float32), 'W2_self': jax.random.normal(ks[8], (D, D), jnp.float32) * s, 'W2_neigh': jax.random.normal(ks[9], (D, D), jnp.float32) * s, 'b2': jnp.zeros((D,), jnp.float32)}
    _L3_gnn_all = _L3_gnn_setup()
    _L3_gnn_in = {k: v for k, v in _L3_gnn_all.items() if k in ('W_pool', 'b_pool', 'W1_self', 'W1_neigh', 'b1', 'W2_self', 'W2_neigh', 'b2')}
    del _L3_gnn_all
    return {'x': x, 'src': src, 'dst': dst, 'edge_attr_128': edge_attr_128, 'edge_weight': edge_weight, 'L0_gnn_W1': _L0_gnn_in['W1'], 'L0_gnn_b1': _L0_gnn_in['b1'], 'L0_gnn_g1': _L0_gnn_in['g1'], 'L0_gnn_be1': _L0_gnn_in['be1'], 'L0_gnn_W2': _L0_gnn_in['W2'], 'L0_gnn_b2': _L0_gnn_in['b2'], 'L0_gnn_gbn': _L0_gnn_in['gbn'], 'L0_gnn_bbn': _L0_gnn_in['bbn'], 'L1_gnn_W1': _L1_gnn_in['W1'], 'L1_gnn_b1': _L1_gnn_in['b1'], 'L1_gnn_W2': _L1_gnn_in['W2'], 'L1_gnn_b2': _L1_gnn_in['b2'], 'L2_gnn_W_l': _L2_gnn_in['W_l'], 'L2_gnn_b_l': _L2_gnn_in['b_l'], 'L2_gnn_W_r': _L2_gnn_in['W_r'], 'L2_gnn_gamma': _L2_gnn_in['gamma'], 'L2_gnn_beta': _L2_gnn_in['beta'], 'L3_gnn_W_pool': _L3_gnn_in['W_pool'], 'L3_gnn_b_pool': _L3_gnn_in['b_pool'], 'L3_gnn_W1_self': _L3_gnn_in['W1_self'], 'L3_gnn_W1_neigh': _L3_gnn_in['W1_neigh'], 'L3_gnn_b1': _L3_gnn_in['b1'], 'L3_gnn_W2_self': _L3_gnn_in['W2_self'], 'L3_gnn_W2_neigh': _L3_gnn_in['W2_neigh'], 'L3_gnn_b2': _L3_gnn_in['b2']}

def reference(x, src, dst, edge_attr_128, edge_weight, L0_gnn_W1, L0_gnn_b1, L0_gnn_g1, L0_gnn_be1, L0_gnn_W2, L0_gnn_b2, L0_gnn_gbn, L0_gnn_bbn, L1_gnn_W1, L1_gnn_b1, L1_gnn_W2, L1_gnn_b2, L2_gnn_W_l, L2_gnn_b_l, L2_gnn_W_r, L2_gnn_gamma, L2_gnn_beta, L3_gnn_W_pool, L3_gnn_b_pool, L3_gnn_W1_self, L3_gnn_W1_neigh, L3_gnn_b1, L3_gnn_W2_self, L3_gnn_W2_neigh, L3_gnn_b2):
    import jax
    import jax.numpy as jnp

    def _L0_gnn_ref(x, edge_index, W1, b1, g1, be1, W2, b2, gbn, bbn):
        import jax, jax.numpy as jnp
        import numpy as np
        N_NODES = 3125
        N_EDGES = 50000
        DIM = 128
        N_LAYERS = 3
        BN_EPS = 1e-05

        def _batchnorm(h, gamma, beta):
            mu = jnp.mean(h, axis=0)
            var = jnp.var(h, axis=0)
            return gamma * (h - mu) * jax.lax.rsqrt(var + BN_EPS) + beta
        src, dst = (edge_index[0], edge_index[1])
        n = x.shape[0]
        h = x
        for i in range(N_LAYERS):
            agg = jax.ops.segment_sum(h[src], dst, num_segments=n)
            z = h + agg
            z = z @ W1[i] + b1[i]
            z = jax.nn.relu(_batchnorm(z, g1[i], be1[i]))
            z = z @ W2[i] + b2[i]
            if i < N_LAYERS - 1:
                z = jax.nn.relu(_batchnorm(z, gbn[i], bbn[i]))
            h = z
        norm = jnp.linalg.norm(h, axis=-1, keepdims=True)
        return h / jnp.maximum(norm, 1e-12)

    def _L1_gnn_ref(x, edge_index, W1, b1, W2, b2):
        import jax, jax.numpy as jnp
        import numpy as np
        N_NODES = 6250
        DIM = 128
        N_EDGES = 40000
        row, col = (edge_index[0], edge_index[1])
        n = x.shape[0]
        msg = x[col]
        summed = jax.ops.segment_sum(msg, row, num_segments=n)
        deg = jax.ops.segment_sum(jnp.ones((row.shape[0],), x.dtype), row, num_segments=n)
        agg = summed / jnp.maximum(deg, 1.0)[:, None]
        h = jax.nn.relu(agg @ W1.T + b1)
        return h @ W2.T + b2

    def _L2_gnn_ref(x, ei, W_l, b_l, W_r, gamma, beta):
        import jax, jax.numpy as jnp
        import numpy as np
        N_NODES = 6250
        N_EDGES = 37500
        DIM = 128
        BN_EPS = 1e-05
        src, dst = (ei[0], ei[1])
        n = x.shape[0]
        msg_sum = jax.ops.segment_sum(x[src], dst, num_segments=n)
        deg = jax.ops.segment_sum(jnp.ones_like(dst, dtype=x.dtype), dst, num_segments=n)
        agg = msg_sum / jnp.clip(deg, 1.0, None)[:, None]
        h = agg @ W_l.T + b_l + x @ W_r.T
        mu = jnp.mean(h, axis=0)
        var = jnp.mean(jnp.square(h - mu), axis=0)
        hn = (h - mu) * jax.lax.rsqrt(var + BN_EPS) * gamma + beta
        return jax.nn.relu(hn) + x

    def _L3_gnn_ref(node_features, edge_features, src, dst, edge_weight_raw, W_pool, b_pool, W1_self, W1_neigh, b1, W2_self, W2_neigh, b2):
        import jax, jax.numpy as jnp
        import numpy as np
        N_NODES = 3125
        N_EDGES = 50000
        D = 128
        EPS = 1e-12
        N = node_features.shape[0]
        deg = jax.ops.segment_sum(jnp.ones_like(edge_weight_raw), dst, num_segments=N)
        wsum = jax.ops.segment_sum(edge_weight_raw, dst, num_segments=N)
        w = edge_weight_raw / jnp.maximum(wsum, EPS)[dst]
        feat = jax.nn.relu(node_features @ W_pool + b_pool)
        msg = feat[src] * w[:, None]
        neigh = jax.ops.segment_max(msg, dst, num_segments=N)
        neigh = jnp.where(deg[:, None] > 0, neigh, 0.0)
        rst = node_features @ W1_self + neigh @ W1_neigh + b1
        nrm = jnp.linalg.norm(rst, axis=1, keepdims=True)
        rst = rst / jnp.maximum(nrm, EPS)
        h = jax.nn.relu(rst)
        msg2 = h[src] * w[:, None]
        neigh2 = jax.ops.segment_sum(msg2, dst, num_segments=N) / jnp.maximum(deg, 1.0)[:, None]
        out = jax.nn.relu(h @ W2_self + neigh2 @ W2_neigh + b2)
        return out
    edge_index = jnp.stack([src, dst])
    x = _layernorm(x + _L0_gnn_ref(x, edge_index, L0_gnn_W1, L0_gnn_b1, L0_gnn_g1, L0_gnn_be1, L0_gnn_W2, L0_gnn_b2, L0_gnn_gbn, L0_gnn_bbn), axis=-1)
    x = _layernorm(x + _L1_gnn_ref(x, edge_index, L1_gnn_W1, L1_gnn_b1, L1_gnn_W2, L1_gnn_b2), axis=-1)
    x = _layernorm(x + _L2_gnn_ref(x, edge_index, L2_gnn_W_l, L2_gnn_b_l, L2_gnn_W_r, L2_gnn_gamma, L2_gnn_beta), axis=-1)
    x = _layernorm(x + _L3_gnn_ref(x, edge_attr_128, src, dst, edge_weight, L3_gnn_W_pool, L3_gnn_b_pool, L3_gnn_W1_self, L3_gnn_W1_neigh, L3_gnn_b1, L3_gnn_W2_self, L3_gnn_W2_neigh, L3_gnn_b2), axis=-1)
    return x

_drawn_inputs = setup_inputs


def setup_inputs(seed=0):
    import zlib

    import numpy as np

    out = dict(_drawn_inputs(seed))
    spreads = {'L0_gnn_b1': (0.0, 2.0),
     'L0_gnn_g1': (1.0, 0.6),
     'L0_gnn_be1': (0.0, 0.549),
     'L0_gnn_b2': (0.0, 0.34),
     'L0_gnn_gbn': (1.0, 0.569),
     'L0_gnn_bbn': (0.0, 0.665),
     'L2_gnn_b_l': (0.0, 2.0),
     'L2_gnn_gamma': (1.0, 0.2),
     'L2_gnn_beta': (0.0, 0.1),
     'L3_gnn_b_pool': (0.0, 2.0),
     'L3_gnn_b1': (0.0, 2.0),
     'L3_gnn_b2': (0.0, 0.1)}
    factors = {'edge_weight': 38.92,
     'L1_gnn_b1': 3.089,
     'L3_gnn_W_pool': 28.875,
     'L3_gnn_W1_neigh': 8.0,
     'L3_gnn_W2_neigh': 21.384,
     'L3_gnn_W1_self': 8.0}
    for name, (base, spread) in spreads.items():
        noise = np.random.default_rng([zlib.crc32(name.encode()), seed]).standard_normal(out[name].shape)
        drawn = base * np.exp(spread * noise) if base else spread * noise
        out[name] = jnp.asarray(drawn.astype(out[name].dtype))
    for name, factor in factors.items():
        out[name] = (out[name] * factor).astype(out[name].dtype)
    return out
```

```python
import numpy as np
from contextlib import ExitStack
import concourse.bass as bass
from concourse import mybir

N = 6250
E = 106250
D = 128
GT = 8
G = 104
T = G * GT
EP = T * 128
GE = GT * 128
W = 128
NR = 6400
BLK = 625
NBLK = N // BLK
TN = 125
TPB = BLK // TN
YW = D + 1
BIG = 3.0e38
MAX_PASS = 4
BN_EPS = 1e-5
NORM_EPS = 1e-12


def build_program(nc, a, out):
    F32, I32, BF16 = mybir.dt.float32, mybir.dt.int32, mybir.dt.bfloat16
    ALU, ACT, AX = mybir.AluOpType, mybir.ActivationFunctionType, mybir.AxisListType
    ctx = ExitStack()
    with ctx:
        def sb(name, shape, dt=F32):
            return ctx.enter_context(nc.sbuf_tensor(name, shape, dt))

        def sem(name):
            return ctx.enter_context(nc.semaphore(name))

        table = nc.dram_tensor("table", [NR, D], F32).ap()
        ysum = [nc.dram_tensor(f"ysum{k}", [NR, YW], F32).ap() for k in range(GT)]
        start_penalty = nc.dram_tensor("start_penalty", [G, GE], F32).ap()

        X = sb("X", [128, N])
        H = sb("H", [128, N + W])
        A = sb("A", [128, N + W])
        B = sb("B", [128, N])
        DEG = sb("DEG", [128, N + W])
        WS = H
        gbuf = [sb(f"gbuf{b}", [128, GT, D]) for b in range(2)]
        sel = [sb(f"sel{b}", [128, GT, W]) for b in range(2)]
        SS = [sb(f"SS{b}", [128, BLK]) for b in range(2)]
        ST = [sb(f"ST{b}", [128, TPB, D]) for b in range(2)]
        src_i = sb("src_i", [128, T + 2 * GT], I32)
        dst_f = sb("dst_f", [128, T])
        src_f = sb("src_f", [128, T + 2 * GT])
        keyloc = sb("keyloc", [128, T + GT])
        ew = sb("ew", [128, T + GT])
        is_end = sb("is_end", [128, T + GT])
        idx_slot = [sb(f"idx_slot{b}", [128, GT], I32) for b in range(2)]
        col_slot = [sb(f"col_slot{b}", [128, GT]) for b in range(2)]
        ident = sb("ident", [128, 128])
        iota = sb("iota", [128, W])
        ones = sb("ones", [128, 128])
        mean_m = sb("mean_m", [128, 128])
        base_i = sb("base_i", [1, G], I32)
        lohi = sb("lohi", [128, 2])
        eps_bn = sb("eps_bn", [128, 1])
        zero_c = sb("zero_c", [128, 1])
        stats = sb("stats", [128, 2 * NBLK, 6])
        mv = sb("mv", [128, 2])
        cf = sb("cf", [128, 5])
        wnames = list(WEIGHTS)
        weights = sb("weights", [128, len(wnames), 128])
        vnames = list(VECTORS)
        vectors = sb("vectors", [128, len(vnames)])
        wt = {n: weights[:, i, :] for i, n in enumerate(wnames)}
        vec = {n: vectors[:, i:i + 1] for i, n in enumerate(vnames)}
        scan = [B[:, b * GE:(b + 1) * GE] for b in range(2)]
        pen = [B[:, (2 + b) * GE:(3 + b) * GE] for b in range(2)]
        scan_rows_flat = B[:, 4 * GE:5 * GE]
        scan_rows = scan_rows_flat.rearrange("p (k f) -> p k f", k=GT)
        diag = B[:, 5 * GE:6 * GE].rearrange("p (k e) -> p k e", k=GT)
        same = A[:, 0:GE // 2].bitcast(BF16).rearrange("p (k e) -> p k e", k=GT)
        onehot = [A[:, (1 + b) * GE // 2:(2 + b) * GE // 2].bitcast(BF16).rearrange("p (k e) -> p k e", k=GT)
                  for b in range(2)]
        before = B[:, 0:GE].rearrange("p (k e) -> p k e", k=GT)
        earlier = sb("earlier", [128, 128])
        mcount = B[:, 2 * GE:3 * GE].rearrange("p (k e) -> p k e", k=GT)
        rank = B[:, 3 * GE:3 * GE + GT]
        to_row = B[:, 3 * GE + 16:3 * GE + 16 + GT]
        trash = sb("trash", [128, 1])
        xwin = [B[:, 3 * GE + 64 + 132 * b:3 * GE + 64 + 132 * b + YW] for b in range(2)]
        summed_rows = [A[:, 3 * GE // 2 + b * GT * YW:3 * GE // 2 + (b + 1) * GT * YW]
                       .rearrange("p (k f) -> p k f", k=GT) for b in range(2)]
        dst_i = B[:, 0:T].bitcast(I32)
        next_i = B[:, T:2 * T].bitcast(I32)
        next_f = B[:, 2 * T:3 * T]
        least = B[:, 3 * T:3 * T + G]
        row_i = A[0:G, 0:GE].bitcast(I32)
        prev_i = A[0:G, GE:2 * GE].bitcast(I32)
        row_pen = B[0:G, 4 * T:4 * T + GE]
        parts = [[B, H][b][0:TN, 0:GT * TPB * YW] for b in range(2)]
        ytot = [gbuf[b][0:TN, :, :].rearrange("p k f -> p (k f)")[:, 0:TPB * YW] for b in range(2)]
        ydeg = sb("ydeg", [128, 2, TPB])
        yrow = ST

        PS = ctx.enter_context(nc.psum_tensor("PS", [128, 4096], F32))
        blk_ps = [PS[:, 1024 * b:1024 * b + BLK] for b in range(2)]
        row_ps = [PS[:, 2048 + 1024 * b:2048 + 1024 * b + TPB * 128] for b in range(2)]
        agg_ps = [PS[:, 512 * b:512 * b + W] for b in range(2)]
        extra_ps = [PS[:, 1024 + 512 * b:1024 + 512 * b + W] for b in range(2)]
        msg_ps = [PS[:, 1024:2048], PS[:, 3072:4096]]
        rev_ps = PS[:, 2048:3072]
        keyrow_ps = PS[:, 0:1024]
        m_ps = PS[:, 1024:2048]
        v_ps = PS[:, 2048:4096].rearrange("p (k f) -> p k f", k=GT)

        loaded = sem("loaded")
        dve_chain = sem("dve_chain")
        const_ready = sem("const_ready")
        lohi_ps = sem("lohi_ps")
        lohi_done = sem("lohi_done")
        base_ps = sem("base_ps")
        setup_done = sem("setup_done")
        pen_out = sem("pen_out")
        ysum_zeroed = sem("ysum_zeroed")
        stood = sem("stood")
        idx_ready = sem("idx_ready")
        gathered = [sem(f"gathered{b}") for b in range(2)]
        sel_ready = sem("sel_ready")
        summed = sem("summed")
        placed = sem("placed")
        pass_clear = sem("pass_clear")
        msg_full = sem("msg_full")
        pen_in = [sem(f"pen_in{b}") for b in range(2)]
        diag_ready = sem("diag_ready")
        scanned = sem("scanned")
        rev_full = sem("rev_full")
        rev_kept = sem("rev_kept")
        lin_src = sem("lin_src")
        lin_full = sem("lin_full")
        lin_taken = sem("lin_taken")
        aff_done = sem("aff_done")
        stats_done = sem("stats_done")
        bn_var = sem("bn_var")
        bn_sd = sem("bn_sd")
        bn_coef = sem("bn_coef")
        ss_ready = sem("ss_ready")
        ss_kept = sem("ss_kept")
        rows_full = sem("rows_full")
        rows_staged = sem("rows_staged")
        rows_out = [sem(f"rows_out{b}") for b in range(2)]
        added = sem("added")
        mean_full = sem("mean_full")
        centered = sem("centered")
        sq_ready = sem("sq_ready")
        norm_full = sem("norm_full")
        sd_ready = sem("sd_ready")
        blk_chain = sem("blk_chain")
        scaled = sem("scaled")
        kr_full = sem("kr_full")
        same_ready = sem("same_ready")
        m_full = sem("m_full")
        m_kept = sem("m_kept")
        v_full = sem("v_full")
        v_kept = sem("v_kept")
        xwin_in = [sem(f"xwin_in{b}") for b in range(2)]
        row_idx = sem("row_idx")
        col_ready = sem("col_ready")
        hot_ready = sem("hot_ready")
        rank_chain = sem("rank_chain")
        scattered = [sem(f"scattered{k}") for k in range(GT)]
        parts_in = [sem(f"parts_in{b}") for b in range(2)]
        parts_used = sem("parts_used")
        yrow_ready = sem("yrow_ready")
        y_chain = sem("y_chain")
        yT_full = sem("yT_full")
        yT_kept = sem("yT_kept")

        tick = sb("tick", [128, 4])
        block = ctx.enter_context(nc.Block())

        def cols(i, b):
            return bass.ds(i * (2 * BLK) + b * BLK, BLK)

        def tiles(i, b, ahead=0):
            return bass.ds(i * (2 * GT) + (b + ahead) * GT, GT)

        def bc(col, n):
            return col.to_broadcast([128, n])

        def rows_written(eng, n):
            for b in range(2):
                eng.wait_ge(rows_out[b], 16 * (NBLK // 2) * n)

        def pool_stands(pool, before):
            pool.wait_ge(stood, before)
            nc.gpsimd.tensor_tensor(out=tick[:, 1:2], in0=tick[:, 0:1], in1=tick[:, 0:1],
                                    op=ALU.add).then_inc(stood, 1)

        def pool_gather(pool, q, source):
            with pool.Fori(0, G // 2) as i:
                for b in range(2):
                    free, used = gather_free(q, i, b)
                    used = pool.snap(used)
                    indices = pool.snap(q * (G + 2) + i * 2 + (b + 1))
                    pool.wait_ge(free, used)
                    pool.wait_ge(idx_ready, indices)
                    pool_stands(pool, (q if q < 3 else q + 2) * G + i * 2 + b)
                    for k in range(GT):
                        nc.gpsimd.indirect_dma_start(
                            out=gbuf[b][:, k, :], out_offset=None, in_=source,
                            in_offset=bass.IndirectOffsetOnAxis(ap=idx_slot[b][:, k:k + 1], axis=0),
                        ).then_inc(gathered[b], 16)

        def gather_free(q, i, b):
            return (msg_full, i * 2 + b) if q == MAX_PASS else (summed, q * G + i * 2 + b)

        def q_sel(q):
            return q * (G + 1) - (1 if q > MAX_PASS else 0)

        def gathered_value(q, i):
            return i * (16 * GT) + 16 * GT * (1 + q * (G // 2))

        def pe_sum(pe, q, extra=None):
            with pe.Fori(0, G // 2) as i:
                for b in range(2):
                    pe.wait_ge(gathered[b], gathered_value(q, i))
                    pe.wait_ge(sel_ready, q_sel(q) + i * 2 + (b + 1))
                    pe.wait_ge(placed, q * G + i * 2 + b)
                    for k in range(GT):
                        last = nc.tensor.matmul(agg_ps[b], gbuf[b][:, k, :], sel[b][:, k, :],
                                                start=(k == 0), stop=(k == GT - 1))
                    if extra is not None:
                        for k in range(GT):
                            left = ones[:, :] if extra == "degree" else bc(col_slot[b][:, k:k + 1], 128)
                            last = nc.tensor.matmul(extra_ps[b], left, sel[b][:, k, :],
                                                    start=(k == 0), stop=(k == GT - 1))
                    last.then_inc(summed, 1)
            pe.wait_ge(placed, G * (q + 1) + 1)

        def pe_max(pe, q):
            def weigh(i, b):
                pe.wait_ge(gathered[b], gathered_value(q, i))
                pe.wait_ge(diag_ready, i * 2 + (b + 1))
                pe.wait_ge(scanned, i * 2 + b)
                for k in range(GT):
                    last = nc.tensor.matmul(msg_ps[b][:, k * 128:(k + 1) * 128], gbuf[b][:, k, :],
                                            diag[:, k, :], start=True, stop=True)
                last.then_inc(msg_full, 1)

            def ends(i, b):
                pe.wait_ge(scanned, i * 2 + (b + 2))
                pe.wait_ge(rev_kept, i * 2 + b)
                for k in range(GT):
                    last = nc.tensor.transpose(rev_ps[:, k * 128:(k + 1) * 128],
                                               scan[b][:, k * 128:(k + 1) * 128], ident[:, :])
                last.then_inc(rev_full, 1)
                pe.wait_ge(rev_kept, i * 2 + (b + 1))
                pe.wait_ge(sel_ready, q_sel(q) + i * 2 + (b + 1))
                pe.wait_ge(placed, q * G + i * 2 + b)
                for k in range(GT):
                    last = nc.tensor.matmul(agg_ps[b], scan_rows[:, k, :], sel[b][:, k, :],
                                            start=(k == 0), stop=(k == GT - 1))
                last.then_inc(summed, 1)

            weigh(0, 0)
            with pe.Fori(0, G // 2 - 1) as i:
                weigh(i, 1)
                ends(i, 0)
                weigh(i + 1, 0)
                ends(i, 1)
            weigh(G // 2 - 1, 1)
            ends(G // 2 - 1, 0)
            ends(G // 2 - 1, 1)
            pe.wait_ge(placed, G * (q + 1) + 1)

        def act_max(act):
            def diagonals(i, b):
                act.wait_ge(msg_full, i * 2 + (b + 1))
                for k in range(GT):
                    last = nc.scalar.activation(diag[:, k, :], ident[:, :], ACT.Copy,
                                                scale=ew[:, bass.ds(i * (2 * GT) + (b * GT + k), 1)])
                last.then_inc(diag_ready, 1)

            def keep(i, b):
                act.wait_ge(rev_full, i * 2 + (b + 1))
                act.wait_ge(summed, MAX_PASS * G + i * 2 + (b + 1))
                nc.scalar.activation(scan_rows_flat, rev_ps, ACT.Copy).then_inc(rev_kept, 1)

            diagonals(0, 0)
            with act.Fori(0, G // 2 - 1) as i:
                diagonals(i, 1)
                keep(i, 0)
                diagonals(i + 1, 0)
                keep(i, 1)
            diagonals(G // 2 - 1, 1)
            keep(G // 2 - 1, 0)
            keep(G // 2 - 1, 1)

        def dve_max(dve, q, clears):
            dve.wait_ge(pass_clear, clears)
            with dve.Fori(0, G // 2) as i:
                for b in range(2):
                    base = dve.value_load(base_i[0:1, bass.ds(i * 2 + b, 1)], min_val=0, max_val=N)
                    at = lambda k, n: bass.ds(i * (2 * GT) + (b * GT + k), n)
                    dve.wait_ge(msg_full, i * 2 + (b + 2))
                    dve.wait_ge(pen_in[b], i * 16 + 16)
                    dve.wait_ge(scanned, i * 2 + (b + 1))
                    nc.vector.tensor_tensor_scan(scan[b], pen[b], msg_ps[b], scan[1 - b][:, GE - 1:GE],
                                                 ALU.add, ALU.max).then_inc(scanned, 1)
                    fill_slots(dve, i, b, 2)
                    build_sel(dve, sel[b], at, is_end).then_inc(sel_ready, 1)
                    dve.wait_ge(summed, q * G + i * 2 + (b + 2))
                    dve.wait_ge(placed, q * G + i * 2 + (b + 1))
                    nc.vector.tensor_tensor(out=A[:, bass.ds(base, W)], in0=A[:, bass.ds(base, W)],
                                            in1=agg_ps[b], op=ALU.add).then_inc(placed, 1)

        def sp_max(sp):
            with sp.Fori(0, G // 2) as i:
                for b in range(2):
                    sp.wait_ge(scanned, i * 2 + b)
                    sp.dma_start(pen[b], start_penalty[bass.ds(i * 2 + b, 1), :].to_broadcast([128, GE])
                                 ).then_inc(pen_in[b], 16)

        def dve_clear(dve, extra=None):
            nc.vector.memset(A[:, :], 0.0).then_inc(pass_clear, 1)
            if extra is not None:
                nc.vector.memset(extra[:, :], 0.0).then_inc(pass_clear, 1)

        def fill_slots(dve, i, b, ahead):
            nc.vector.tensor_copy(idx_slot[b][:, :], src_i[:, tiles(i, b, ahead)]).then_inc(idx_ready, 1)

        def fill_first(dve):
            for b in range(2):
                nc.vector.tensor_copy(idx_slot[b][:, :], src_i[:, b * GT:(b + 1) * GT]).then_inc(idx_ready, 1)

        def build_sel(dve, where, at, scale=None):
            if scale is None:
                return nc.vector.tensor_tensor(
                    out=where[:, :, :], in0=iota[:, :].unsqueeze(1).to_broadcast([128, GT, W]),
                    in1=keyloc[:, at(0, GT)].unsqueeze(2).to_broadcast([128, GT, W]), op=ALU.is_equal)
            for k in range(GT):
                last = nc.vector.tensor_scalar(where[:, k, :], iota[:, :], keyloc[:, at(k, 1)],
                                               scale[:, at(k, 1)], ALU.is_equal, ALU.mult)
            return last

        def dve_sum(dve, q, extra=None, scale=None, extra_cols=None, clears=0):
            def one_group(i, b, ahead):
                g = b + ahead
                at = lambda k, n: bass.ds(i * (2 * GT) + (g * GT + k), n)
                if extra_cols is not None:
                    nc.vector.tensor_copy(col_slot[g % 2][:, :], extra_cols[:, at(0, GT)])
                build_sel(dve, sel[g % 2], at, scale).then_inc(sel_ready, 1)
            one_group(0, 0, 0)
            dve.wait_ge(pass_clear, clears)
            with dve.Fori(0, G // 2) as i:
                for b in range(2):
                    base = dve.value_load(base_i[0:1, bass.ds(i * 2 + b, 1)], min_val=0, max_val=N)
                    one_group(i, b, 1)
                    dve.wait_ge(summed, q * G + i * 2 + (b + 2))
                    fill_slots(dve, i, b, 2)
                    dve.wait_ge(placed, q * G + i * 2 + (b + 1))
                    last = nc.vector.tensor_tensor(out=A[:, bass.ds(base, W)], in0=A[:, bass.ds(base, W)],
                                                   in1=agg_ps[b], op=ALU.add)
                    if extra is not None:
                        last = nc.vector.tensor_tensor(out=extra[:, bass.ds(base, W)],
                                                       in0=extra[:, bass.ds(base, W)],
                                                       in1=extra_ps[b], op=ALU.add)
                    last.then_inc(placed, 1)

        def block_matmul(ps, left, src, i, b, start, stop):
            nc.tensor.matmul(ps[:, 0:512], left, src[:, bass.ds(i * (2 * BLK) + b * BLK, 512)],
                             start=start, stop=stop)
            return nc.tensor.matmul(ps[:, 512:BLK], left,
                                    src[:, bass.ds(i * (2 * BLK) + (b * BLK + 512), BLK - 512)],
                                    start=start, stop=stop)

        def pe_linear(pe, n, terms, after_src=None, free=None):
            with pe.Fori(0, NBLK // 2) as i:
                for b in range(2):
                    if after_src is not None:
                        pe.wait_ge(after_src[0], after_src[1] + i * 2 + (b + 1))
                    if free is not None:
                        pe.wait_ge(free[0], free[1])
                    pe.wait_ge(lin_taken, NBLK * n + i * 2 + b)
                    for j, (w, src) in enumerate(terms):
                        last = block_matmul(blk_ps[b], wt[w], src, i, b, j == 0, j == len(terms) - 1)
                    last.then_inc(lin_full, 1)
            pe.wait_ge(lin_taken, NBLK * (n + 1) + 1)

        def act_linear(act, n, func, bias, dst):
            with act.Fori(0, NBLK // 2) as i:
                for b in range(2):
                    act.wait_ge(lin_full, NBLK * n + i * 2 + (b + 1))
                    nc.scalar.activation(dst[:, cols(i, b)], blk_ps[b], func, bias=vec[bias]).then_inc(lin_taken, 1)

        def act_rows_of(act, r, src, after):
            with act.Fori(0, NBLK // 2) as i:
                for b in range(2):
                    act.wait_ge(after[0], after[1] + i * 2 + (b + 1))
                    act.wait_ge(rows_full, NBLK * r + i * 2 + b)
                    nc.scalar.activation(SS[b][:, :], src[:, cols(i, b)], ACT.Copy).then_inc(ss_ready, 1)
                    act_row(act, r, i, b)

        def act_affine(act, m, src, dst=None, ss=None):
            act.wait_ge(bn_coef, m + 1)
            with act.Fori(0, NBLK // 2) as i:
                for b in range(2):
                    if ss is not None:
                        act.wait_ge(rows_full, NBLK * ss + i * 2 + b)
                        act.wait_ge(ss_kept, NBLK * ss + i * 2 + b)
                    ins = nc.scalar.activation(dst[:, cols(i, b)] if ss is None else SS[b][:, :],
                                               src[:, cols(i, b)], ACT.Relu, bias=cf[:, 4:5], scale=cf[:, 3:4])
                    if ss is None:
                        ins.then_inc(aff_done, 1)
                    else:
                        ins.then_inc(ss_ready, 1)
                        act_row(act, ss, i, b)

        def dve_stats(dve, n, s, src):
            with dve.Fori(0, NBLK // 2) as i:
                for b in range(2):
                    dve.wait_ge(lin_taken, NBLK * n + i * 2 + (b + 2))
                    for h, (lo, w) in enumerate(((0, 313), (313, 312))):
                        nc.vector.bn_stats(stats[:, bass.ds(i * 4 + (2 * b + h), 1), :].rearrange("p a s -> p (a s)"),
                                           src[:, bass.ds(i * (2 * BLK) + (b * BLK + lo), w)]
                                           ).then_inc(stats_done, 1)

        def dve_batchnorm(dve, m, gamma, beta):
            dve.wait_ge(stats_done, 2 * NBLK * (m + 1))
            nc.vector.bn_aggr(mv[:, :], stats[:, :, :].rearrange("p a s -> p (a s)")).then_inc(bn_var, 1)
            dve.wait_ge(bn_sd, m + 1)
            link(dve, nc.vector.reciprocal(cf[:, 1:2], cf[:, 0:1]))
            link(dve, nc.vector.tensor_tensor(out=cf[:, 3:4], in0=cf[:, 1:2], in1=vec[gamma], op=ALU.mult))
            link(dve, nc.vector.tensor_tensor(out=cf[:, 2:3], in0=cf[:, 3:4], in1=mv[:, 0:1], op=ALU.mult))
            nc.vector.tensor_tensor(out=cf[:, 4:5], in0=vec[beta], in1=cf[:, 2:3],
                                    op=ALU.subtract).then_inc(bn_coef, 1)

        def act_batchnorm(act, m):
            act.wait_ge(bn_var, m + 1)
            nc.scalar.activation(cf[:, 0:1], mv[:, 1:2], ACT.Sqrt, bias=eps_bn[:, :]).then_inc(bn_sd, 1)

        def pe_rows(pe, r):
            with pe.Fori(0, NBLK // 2) as i:
                for b in range(2):
                    pe.wait_ge(ss_ready, NBLK * r + i * 2 + (b + 1))
                    pe.wait_ge(rows_staged, NBLK * r + i * 2 + b)
                    for j in range(TPB):
                        last = nc.tensor.transpose(row_ps[b][0:TN, j * 128:(j + 1) * 128],
                                                   SS[b][:, j * TN:(j + 1) * TN], ident[:, :])
                    last.then_inc(rows_full, 1)
            pe.wait_ge(rows_staged, NBLK * (r + 1) + 1)

        def act_row(act, r, i, b):
            act.wait_ge(rows_full, NBLK * r + i * 2 + (b + 2))
            act.wait_ge(rows_out[b], 16 * (NBLK // 2) * r + i * 16)
            nc.scalar.activation(ST[b][0:TN, :, :], row_ps[b][0:TN, :].rearrange("p (j f) -> p j f", j=TPB),
                                 ACT.Copy).then_inc(rows_staged, 1)

        def sp_rows(sp, r, where):
            with sp.Fori(0, NBLK // 2) as i:
                for b in range(2):
                    sp.wait_ge(rows_staged, NBLK * r + i * 2 + (b + 2))
                    sp.dma_start(where[cols(i, b), :].rearrange("(j p) f -> p j f", p=TN),
                                 ST[b][0:TN, :, :]).then_inc(rows_out[b], 16)

        def dve_center(dve, n, term, after=None):
            with dve.Fori(0, NBLK // 2) as i:
                for b in range(2):
                    if after is not None:
                        dve.wait_ge(after[0], after[1] + i * 2 + (b + 1))
                    nc.vector.tensor_tensor(out=X[:, cols(i, b)], in0=X[:, cols(i, b)],
                                            in1=term[:, cols(i, b)], op=ALU.add).then_inc(added, 1)
            with dve.Fori(0, NBLK // 2) as i:
                for b in range(2):
                    dve.wait_ge(mean_full, NBLK * n + i * 2 + (b + 1))
                    nc.vector.tensor_tensor(out=X[:, cols(i, b)], in0=X[:, cols(i, b)],
                                            in1=blk_ps[b], op=ALU.subtract).then_inc(centered, 1)

        def pe_center(pe, n):
            with pe.Fori(0, NBLK // 2) as i:
                for b in range(2):
                    pe.wait_ge(added, NBLK * n + i * 2 + (b + 1))
                    pe.wait_ge(centered, NBLK * n + i * 2 + b)
                    block_matmul(blk_ps[b], mean_m[:, :], X, i, b, True, True).then_inc(mean_full, 1)
            pe.wait_ge(centered, NBLK * (n + 1) + 1)

        def act_norm(act, n, src, sq, eps, after, keep=None, rows=None):
            with act.Fori(0, NBLK // 2) as i:
                for b in range(2):
                    act.wait_ge(after[0], after[1] + i * 2 + (b + 1))
                    nc.scalar.activation(sq[:, cols(i, b)], src[:, cols(i, b)], ACT.Square).then_inc(sq_ready, 1)
            with act.Fori(0, NBLK // 2) as i:
                for b in range(2):
                    act.wait_ge(norm_full, NBLK * n + i * 2 + (b + 1))
                    nc.scalar.activation(sq[:, cols(i, b)], blk_ps[b], ACT.Sqrt, bias=eps).then_inc(sd_ready, 1)
            if rows is not None:
                with act.Fori(0, NBLK // 2) as i:
                    for b in range(2):
                        act.wait_ge(ss_ready, NBLK * rows + i * 2 + (b + 1))
                        if keep is not None:
                            nc.scalar.activation(keep[:, cols(i, b)], SS[b][:, :], ACT.Copy).then_inc(ss_kept, 1)
                        act_row(act, rows, i, b)

        def pe_norm(pe, n, sq, left):
            with pe.Fori(0, NBLK // 2) as i:
                for b in range(2):
                    pe.wait_ge(sq_ready, NBLK * n + i * 2 + (b + 1))
                    pe.wait_ge(sd_ready, NBLK * n + i * 2 + b)
                    block_matmul(blk_ps[b], left[:, :], sq, i, b, True, True).then_inc(norm_full, 1)
            pe.wait_ge(sd_ready, NBLK * (n + 1) + 1)

        def dve_norm(dve, n, src, sq, floor=None, relu=False, dst=None, rows=None, kept=None):
            with dve.Fori(0, NBLK // 2) as i:
                for b in range(2):
                    r = sq[:, cols(i, b)]
                    dve.wait_ge(sd_ready, NBLK * n + i * 2 + (b + 2))
                    if floor is not None:
                        nc.vector.tensor_scalar(r, r, floor, None, ALU.max).then_inc(blk_chain, 1)
                    else:
                        dve.sem_inc(blk_chain, 1)
                    dve.wait_ge(blk_chain, 3 * NBLK * n + i * 6 + (3 * b + 1))
                    nc.vector.tensor_copy(tick[:, 3:4], tick[:, 2:3]).then_inc(blk_chain, 1)
                    nc.vector.reciprocal(r, r).then_inc(blk_chain, 1)
                    dve.wait_ge(blk_chain, 3 * NBLK * n + i * 6 + (3 * b + 3))
                    if rows is not None:
                        dve.wait_ge(rows_full, NBLK * rows + i * 2 + b)
                        if kept is not None:
                            dve.wait_ge(ss_kept, kept + i * 2 + b)
                    to = SS[b][:, :] if rows is not None else dst[:, cols(i, b)]
                    if relu:
                        ins = nc.vector.scalar_tensor_tensor(out=to, in0=src[:, cols(i, b)], scalar=0.0, in1=r,
                                                             op0=ALU.max, op1=ALU.mult)
                    else:
                        ins = nc.vector.tensor_tensor(out=to, in0=src[:, cols(i, b)], in1=r, op=ALU.mult)
                    ins.then_inc(ss_ready if rows is not None else scaled, 1)
            if rows is not None:
                dve.wait_ge(ss_ready, NBLK * (rows + 1))

        def dve_times(dve, dst, other, op, tell, after=None):
            with dve.Fori(0, NBLK // 2) as i:
                for b in range(2):
                    if after is not None:
                        dve.wait_ge(after[0], after[1] + i * 2 + (b + 1))
                    nc.vector.tensor_tensor(out=dst[:, cols(i, b)], in0=dst[:, cols(i, b)],
                                            in1=other[:, cols(i, b)], op=op).then_inc(tell, 1)

        def dve_keep(dve, r):
            with dve.Fori(0, NBLK // 2) as i:
                for b in range(2):
                    dve.wait_ge(ss_ready, NBLK * r + i * 2 + (b + 1))
                    nc.vector.tensor_copy(H[:, cols(i, b)], SS[b][:, :]).then_inc(ss_kept, 1)

        chained = [0]

        def link(dve, ins):
            chained[0] += 1
            ins.then_inc(dve_chain, 1)
            dve.wait_ge(dve_chain, chained[0])

        def dve_scatter(dve):
            for b in range(2):
                link(dve, nc.vector.memset(xwin[b][:, D:YW], 1.0))
            for b in range(2):
                nc.vector.tensor_copy(col_slot[b][:, :], src_f[:, b * GT:(b + 1) * GT]).then_inc(col_ready, 1)
            with dve.Fori(0, G // 2) as i:
                for b in range(2):
                    at = lambda k, n: bass.ds(i * (2 * GT) + (b * GT + k), n)
                    dve.wait_ge(m_full, i * 2 + b)
                    build_sel(dve, onehot[b], at).then_inc(hot_ready, 1)
                    dve.wait_ge(kr_full, i * 2 + (b + 1))
                    dve.wait_ge(m_full, i * 2 + (b + 1))
                    nc.vector.tensor_tensor(
                        out=same, in0=keyrow_ps.rearrange("p (k e) -> p k e", k=GT),
                        in1=col_slot[b][:, :].unsqueeze(2).to_broadcast([128, GT, 128]),
                        op=ALU.is_equal).then_inc(same_ready, 1)
                    dve.wait_ge(same_ready, i * 2 + (b + 1))
                    step = lambda j: i * 8 + (4 * b + j)
                    nc.vector.tensor_tensor(out=before, in0=same,
                                            in1=earlier[:, :].unsqueeze(1).to_broadcast([128, GT, 128]),
                                            op=ALU.mult).then_inc(rank_chain, 1)
                    dve.wait_ge(rank_chain, step(1))
                    nc.vector.tensor_reduce(out=rank, in_=before, axis=AX.X, op=ALU.add).then_inc(rank_chain, 1)
                    nc.vector.tensor_scalar(to_row, col_slot[b][:, :], trash[:, :], None, ALU.subtract
                                            ).then_inc(rank_chain, 1)
                    dve.wait_ge(rank_chain, step(3))
                    nc.vector.scalar_tensor_tensor(out=to_row, in0=rank, scalar=0.0, in1=to_row,
                                                   op0=ALU.is_equal, op1=ALU.mult).then_inc(rank_chain, 1)
                    dve.wait_ge(rank_chain, step(4))
                    dve.wait_ge(v_kept, i * 2 + (b + 1))
                    nc.vector.tensor_scalar(idx_slot[b][:, :], to_row, trash[:, :], None, ALU.add
                                            ).then_inc(row_idx, 1)
                    nc.vector.tensor_copy(col_slot[b][:, :], src_f[:, tiles(i, b, 2)]).then_inc(col_ready, 1)

        def pe_scatter(pe):
            def key_rows(b):
                for k in range(GT):
                    last = nc.tensor.matmul(keyrow_ps[:, k * 128:(k + 1) * 128], bc(col_slot[b][:, k:k + 1], 128),
                                            ident[:, :], start=True, stop=True)
                last.then_inc(kr_full, 1)

            pe.wait_ge(col_ready, 1)
            key_rows(0)
            with pe.Fori(0, G // 2) as i:
                for b in range(2):
                    pe.wait_ge(hot_ready, i * 2 + (b + 1))
                    pe.wait_ge(same_ready, i * 2 + (b + 1))
                    pe.wait_ge(m_kept, i * 2 + b)
                    for k in range(GT):
                        last = nc.tensor.matmul(m_ps[:, k * 128:(k + 1) * 128], onehot[b][:, k, :], same[:, k, :],
                                                start=True, stop=True)
                    last.then_inc(m_full, 1)
                    pe.wait_ge(col_ready, i * 2 + (b + 2))
                    key_rows(1 - b)
                    pe.wait_ge(m_kept, i * 2 + (b + 1))
                    pe.wait_ge(xwin_in[b], i * 16 + 16)
                    pe.wait_ge(v_kept, i * 2 + b)
                    for k in range(GT):
                        last = nc.tensor.matmul(v_ps[:, k, 0:YW], mcount[:, k, :], xwin[b], start=True, stop=True)
                    last.then_inc(v_full, 1)
            pe.wait_ge(v_kept, G)

        def act_scatter(act):
            def one_group(i, b):
                act.wait_ge(m_full, i * 2 + (b + 2))
                act.wait_ge(v_full, i * 2 + (b + 1))
                nc.scalar.activation(mcount, m_ps.rearrange("p (k e) -> p k e", k=GT), ACT.Copy).then_inc(m_kept, 1)
                act.wait_ge(v_full, i * 2 + (b + 2))
                if b or not isinstance(i, int):
                    for k in range(GT):
                        act.wait_ge(scattered[k], i * 32 + 16 * (b - 1))
                nc.scalar.activation(summed_rows[b], v_ps[:, :, 0:YW], ACT.Copy).then_inc(v_kept, 1)

            for b in range(2):
                one_group(0, b)
            with act.Fori(1, G // 2) as i:
                for b in range(2):
                    one_group(i, b)

        def pool_scatter(pool):
            with pool.Fori(0, G // 2) as i:
                for b in range(2):
                    pool.wait_ge(v_kept, i * 2 + (b + 1))
                    pool.wait_ge(row_idx, i * 2 + (b + 1))
                    before_g = pool.snap(i * 32 + 16 * b)
                    for k in range(GT):
                        if k % 4 == 0:
                            for j in range(k, k + 4):
                                pool.wait_ge(scattered[j], before_g)
                            pool_stands(pool, 3 * G + i * 4 + (2 * b + k // 4))
                        nc.gpsimd.indirect_dma_start(
                            out=ysum[k], out_offset=bass.IndirectOffsetOnAxis(ap=idx_slot[b][:, k:k + 1], axis=0),
                            in_=summed_rows[b][:, k, :], in_offset=None, compute_op=ALU.add,
                        ).then_inc(scattered[k], 16)

        def sp_scatter(sp):
            with sp.Fori(0, G // 2) as i:
                for b in range(2):
                    base = sp.value_load(base_i[0:1, bass.ds(i * 2 + b, 1)], min_val=0, max_val=N)
                    sp.wait_ge(v_full, i * 2 + b)
                    sp.dma_start(xwin[b][:, 0:D], table[bass.ds(base, W), :]).then_inc(xwin_in[b], 16)

        def sp_readback(sp):
            sp.wait_ge(v_kept, G)
            for k in range(GT):
                sp.wait_ge(scattered[k], 16 * G)
            with sp.Fori(0, NBLK // 2) as i:
                for b in range(2):
                    sp.wait_ge(parts_used, i * 2 + b)
                    for k in range(GT):
                        sp.dma_start(parts[b][:, k * TPB * YW:(k + 1) * TPB * YW].rearrange("p (j f) -> p j f", j=TPB),
                                     ysum[k][cols(i, b), :].rearrange("(j p) f -> p j f", p=TN)
                                     ).then_inc(parts_in[b], 16)

        def dve_readback(dve):
            with dve.Fori(0, NBLK // 2) as i:
                for b in range(2):
                    step = lambda j: i * 6 + (3 * b + j)
                    dve.wait_ge(parts_in[b], i * (16 * GT) + 16 * GT)
                    nc.vector.tensor_reduce(out=ytot[b], in_=parts[b].rearrange("p (k m) -> p m k", k=GT),
                                            axis=AX.X, op=ALU.add).then_inc(parts_used, 1)
                    dve.wait_ge(parts_used, i * 2 + (b + 2))
                    y3 = ytot[b].rearrange("p (j f) -> p j f", j=TPB)
                    nc.vector.tensor_scalar(ydeg[0:TN, b, :], y3[:, :, D], 1.0, None, ALU.max).then_inc(y_chain, 1)
                    dve.wait_ge(y_chain, step(1))
                    nc.vector.reciprocal(ydeg[0:TN, b, :], ydeg[0:TN, b, :]).then_inc(y_chain, 1)
                    dve.wait_ge(y_chain, step(2))
                    dve.wait_ge(yT_full, i * 2 + b)
                    nc.vector.tensor_tensor(out=yrow[b][0:TN, :, :], in0=y3[:, :, 0:D],
                                            in1=ydeg[0:TN, b, :].unsqueeze(2).to_broadcast([TN, TPB, D]),
                                            op=ALU.mult).then_inc(y_chain, 1)

        def pe_readback(pe):
            with pe.Fori(0, NBLK // 2) as i:
                for b in range(2):
                    pe.wait_ge(y_chain, i * 6 + (3 * b + 3))
                    pe.wait_ge(yT_kept, i * 2 + b)
                    for j in range(TPB):
                        last = nc.tensor.transpose(PS[:, 1024 * b + 128 * j:1024 * b + 128 * j + TN],
                                                   yrow[b][0:TN, j, :], ident[0:TN, 0:TN])
                    last.then_inc(yT_full, 1)
            pe.wait_ge(yT_kept, NBLK + 1)

        def act_readback(act):
            with act.Fori(0, NBLK // 2) as i:
                for b in range(2):
                    act.wait_ge(yT_full, i * 2 + (b + 2))
                    nc.scalar.activation(A[:, cols(i, b)].rearrange("p (j n) -> p j n", j=TPB),
                                         PS[:, 1024 * b:1024 * b + 128 * TPB].rearrange("p (j n) -> p j n", j=TPB)
                                         [:, :, 0:TN], ACT.Copy).then_inc(yT_kept, 1)

        @block.sync
        def _(sp):
            for dst, src in ((src_i[:, :], a["src_t"]), (ew[:, :], a["ew_t"]), (X[:, :], a["x_t"]), (weights[:, :, :], a["weights"]),
                             (vectors[:, :], a["vectors"]), (dst_i, a["dst_t"]), (next_i, a["dst_next_t"]),
                             (row_i, a["dst_rows"]), (prev_i, a["dst_prev_rows"])):
                sp.dma_start(dst, src).then_inc(loaded, 16)
            sp.wait_ge(setup_done, 1)
            sp.dma_start(start_penalty, row_pen).then_inc(pen_out, 16)
            sp.dma_start(table[N:NR, :].rearrange("(p r) f -> p (r f)", p=75), H[0:75, 0:2 * D]).then_inc(pen_out, 16)
            for k in range(GT):
                zeroed = ysum[k].rearrange("a b -> (a b)").rearrange("(p c) -> p c", p=128)
                for c in range(5):
                    w = NR * YW // (128 * 5)
                    sp.dma_start(zeroed[:, c * w:(c + 1) * w], H[:, 0:w]).then_inc(ysum_zeroed, 16)
            sp.wait_ge(pen_out, 32)
            sp.wait_ge(ysum_zeroed, 16 * 5 * GT)
            sp_rows(sp, 0, table)
            sp_rows(sp, 1, table)
            sp_rows(sp, 2, table)
            rows_written(sp, 3)
            sp_scatter(sp)
            sp_readback(sp)
            sp_rows(sp, 3, table)
            sp_rows(sp, 4, table)
            sp_rows(sp, 5, table)
            sp_max(sp)
            sp_rows(sp, 6, table)
            sp_rows(sp, 7, out)
            rows_written(sp, 8)

        @block.gpsimd
        def _(pool):
            nc.gpsimd.memset(tick[:, 0:2], 0.0).then_inc(const_ready, 1)
            nc.gpsimd.memset(ident[:, :], 1.0).then_inc(const_ready, 1)
            nc.gpsimd.memset(earlier[:, :], 1.0).then_inc(const_ready, 1)
            nc.gpsimd.iota(iota[:, :], pattern=[[1, W]], base=0, channel_multiplier=0,
                           allow_small_or_imprecise_dtypes=True).then_inc(const_ready, 1)
            nc.gpsimd.iota(trash[:, :], pattern=[[0, 1]], base=NR - 128, channel_multiplier=1,
                           allow_small_or_imprecise_dtypes=True).then_inc(const_ready, 1)
            pool.wait_ge(const_ready, 5)
            nc.gpsimd.affine_select(out=ident[:, :], in_=ident[:, :], compare_op=ALU.is_equal, fill=0.0, base=0,
                                    pattern=[[-1, 128]], channel_multiplier=1).then_inc(const_ready, 1)
            nc.gpsimd.affine_select(out=earlier[:, :], in_=earlier[:, :], compare_op=ALU.is_gt, fill=0.0, base=0,
                                    pattern=[[-1, 128]], channel_multiplier=1).then_inc(const_ready, 1)
            pool_gather(pool, 0, a["x"])
            for q in (1, 2):
                rows_written(pool, q)
                pool_gather(pool, q, table)
            pool.wait_ge(ysum_zeroed, 16 * 5 * GT)
            pool_scatter(pool)
            rows_written(pool, 4)
            pool.wait_ge(yT_kept, NBLK)
            rows_written(pool, 5 - 1)
            pool_gather(pool, 3, table)
            rows_written(pool, 6)
            pool_gather(pool, 4, table)
            rows_written(pool, 7)
            pool_gather(pool, 5, table)

        @block.scalar
        def _(act):
            act.wait_ge(pen_out, 32)
            act.wait_ge(ysum_zeroed, 16 * 5 * GT)
            for m in range(3):
                act_linear(act, 2 * m, ACT.Identity, f"L0_b1_{m}", dst=B)
                act_batchnorm(act, 2 * m)
                act_affine(act, 2 * m, B, dst=A)
                act_linear(act, 2 * m + 1, ACT.Identity, f"L0_b2_{m}", dst=B)
                if m < 2:
                    act_batchnorm(act, 2 * m + 1)
                    act_affine(act, 2 * m + 1, B, ss=m)
            act_norm(act, 0, B, A, zero_c[:, :], (lin_taken, 5 * NBLK + 1))
            act_norm(act, 1, X, A, eps_bn[:, :], (centered, 1), keep=X, rows=2)
            act_scatter(act)
            act_readback(act)
            act_linear(act, 6, ACT.Relu, "L1_b1", dst=B)
            act_linear(act, 7, ACT.Identity, "L1_b2", dst=A)
            act_norm(act, 2, X, B, eps_bn[:, :], (centered, NBLK + 1), keep=X, rows=3)
            act_linear(act, 8, ACT.Identity, "L2_b_l", dst=B)
            act_batchnorm(act, 5)
            act_affine(act, 5, B, dst=A)
            act_norm(act, 3, X, B, eps_bn[:, :], (centered, 2 * NBLK + 1), keep=X, rows=4)
            act_linear(act, 9, ACT.Relu, "L3_b_pool", dst=B)
            act_rows_of(act, 5, B, (lin_taken, 9 * NBLK + 1))
            act_max(act)
            act_linear(act, 10, ACT.Identity, "L3_b1", dst=B)
            act_norm(act, 4, B, A, zero_c[:, :], (lin_taken, 10 * NBLK + 1), keep=B, rows=6)
            act_linear(act, 11, ACT.Relu, "L3_b2", dst=A)
            act_norm(act, 5, X, B, eps_bn[:, :], (centered, 3 * NBLK + 1), rows=7)

        @block.vector
        def _(dve):
            link(dve, nc.vector.memset(tick[:, 2:4], 0.0))
            for c in (summed, placed, msg_full, scanned, lin_taken, rows_full, rows_staged, ss_kept, centered,
                      sd_ready, m_full, v_full, parts_used, yT_full, yT_kept):
                dve.sem_inc(c, 1)
            nc.vector.memset(ones[:, :], 1.0)
            nc.vector.memset(mean_m[:, :], 1.0 / D)
            nc.vector.memset(eps_bn[:, :], BN_EPS)
            nc.vector.memset(zero_c[:, :], 0.0)
            nc.vector.memset(scan[1][:, GE - 1:GE], 0.0)
            nc.vector.memset(keyloc[:, :], -1.0)
            nc.vector.memset(is_end[:, :], 0.0)
            link(dve, nc.vector.memset(H[:, :], 0.0))
            dve.wait_ge(loaded, 16 * 9)
            fill_first(dve)
            nc.vector.tensor_copy(src_f[:, :], src_i[:, :])
            link(dve, nc.vector.tensor_copy(dst_f[:, :], dst_i))
            nc.vector.tensor_copy(next_f, next_i)
            link(dve, nc.vector.tensor_reduce(out=least, in_=dst_f[:, :].rearrange("p (g k) -> p g k", k=GT),
                                              axis=AX.X, op=ALU.min))
            dve.sem_inc(lohi_done, 1)
            nc.vector.tensor_tensor(out=is_end[:, 0:T], in0=dst_f[:, :], in1=next_f, op=ALU.not_equal)
            link(dve, nc.vector.tensor_tensor(out=row_pen, in0=row_i, in1=prev_i, op=ALU.is_equal))
            link(dve, nc.vector.tensor_scalar(row_pen, row_pen, 1.0, BIG, ALU.subtract, ALU.mult))
            dve.sem_inc(setup_done, 1)
            dve.wait_ge(lohi_ps, 1)
            nc.vector.tensor_reduce(out=lohi[0:G, 0:1], in_=PS[0:G, 0:128], axis=AX.X,
                                    op=ALU.min).then_inc(lohi_done, 1)
            dve.wait_ge(base_ps, 1)
            link(dve, nc.vector.tensor_copy(base_i[:, :], PS[0:1, 512:512 + G]))
            link(dve, nc.vector.tensor_tensor(
                out=keyloc[:, 0:T].rearrange("p (g k) -> p g k", k=GT),
                in0=dst_f[:, :].rearrange("p (g k) -> p g k", k=GT),
                in1=PS[:, 512:512 + G].unsqueeze(2).to_broadcast([128, G, GT]), op=ALU.subtract))
            clears = 0
            for m in range(3):
                if m:
                    dve_keep(dve, m - 1)
                    fill_first(dve)
                dve_clear(dve, DEG if m == 0 else None)
                clears += 2 if m == 0 else 1
                dve_sum(dve, m, extra=DEG if m == 0 else None, clears=clears)
                if m == 0:
                    dve.wait_ge(placed, 1 + G)
                    link(dve, nc.vector.tensor_scalar(DEG[:, :], DEG[:, :], 1.0, None, ALU.max))
                    link(dve, nc.vector.reciprocal(DEG[:, :], DEG[:, :]))
                dve.wait_ge(placed, 1 + G * (m + 1))
                dve_times(dve, A, X if m == 0 else H, ALU.add, lin_src)
                dve_stats(dve, 2 * m, 2 * m, B)
                dve_batchnorm(dve, 2 * m, f"L0_g1_{m}", f"L0_be1_{m}")
                if m < 2:
                    dve_stats(dve, 2 * m + 1, 2 * m + 1, B)
                    dve_batchnorm(dve, 2 * m + 1, f"L0_gbn_{m}", f"L0_bbn_{m}")
            dve_norm(dve, 0, B, A, floor=NORM_EPS, dst=B)
            dve_center(dve, 0, B, after=(scaled, 0))
            dve_norm(dve, 1, X, A, rows=2, kept=2 * NBLK)
            dve_scatter(dve)
            dve_readback(dve)
            dve_center(dve, 1, A, after=(lin_taken, 7 * NBLK + 1))
            dve_norm(dve, 2, X, B, rows=3, kept=3 * NBLK)
            fill_first(dve)
            dve_clear(dve, WS)
            clears += 2
            dve_sum(dve, 3, extra=WS, extra_cols=ew, clears=clears)
            dve.wait_ge(placed, 1 + 4 * G)
            dve_times(dve, A, DEG, ALU.mult, lin_src)
            link(dve, nc.vector.tensor_scalar(WS[:, :], WS[:, :], NORM_EPS, None, ALU.max))
            link(dve, nc.vector.reciprocal(WS[:, :], WS[:, :]))
            dve_stats(dve, 8, 5, B)
            dve_batchnorm(dve, 5, "L2_gamma", "L2_beta")
            dve_times(dve, A, X, ALU.add, lin_src, after=(aff_done, 3 * NBLK))
            dve_center(dve, 2, A, after=(lin_src, 4 * NBLK))
            dve_norm(dve, 3, X, B, rows=4, kept=4 * NBLK)
            fill_first(dve)
            dve_clear(dve)
            clears += 1
            dve_max(dve, MAX_PASS, clears)
            dve.wait_ge(placed, 1 + 5 * G)
            dve_times(dve, A, WS, ALU.mult, lin_src)
            dve_norm(dve, 4, B, A, floor=NORM_EPS, relu=True, rows=6, kept=5 * NBLK)
            fill_first(dve)
            dve_clear(dve)
            clears += 1
            dve_sum(dve, 5, scale=ew, clears=clears)
            link(dve, nc.vector.tensor_tensor(out=WS[:, :], in0=WS[:, :], in1=DEG[:, :], op=ALU.mult))
            dve.wait_ge(placed, 1 + 6 * G)
            dve_times(dve, A, WS, ALU.mult, lin_src)
            dve_center(dve, 3, A, after=(lin_taken, 11 * NBLK + 1))
            dve_norm(dve, 5, X, B, rows=7)

        @block.tensor
        def _(pe):
            pe.wait_ge(const_ready, 7)
            pe.wait_ge(loaded, 16 * 9)
            pe.wait_ge(lohi_done, 1)
            nc.tensor.transpose(PS[0:G, 0:128], least, ident[:, :]).then_inc(lohi_ps, 1)
            pe.wait_ge(lohi_done, 2)
            nc.tensor.matmul(PS[:, 512:512 + G], lohi[0:G, 0:1].to_broadcast([G, 128]), ident[0:G, 0:G],
                             start=True, stop=True).then_inc(base_ps, 1)
            for m in range(3):
                pe_sum(pe, m, extra="degree" if m == 0 else None)
                pe_linear(pe, 2 * m, [(f"L0_W1_{m}", A)], after_src=(lin_src, m * NBLK))
                pe_linear(pe, 2 * m + 1, [(f"L0_W2_{m}", A)], after_src=(aff_done, m * NBLK))
                if m < 2:
                    pe_rows(pe, m)
            pe_norm(pe, 0, A, ones)
            pe_center(pe, 0)
            pe_norm(pe, 1, A, mean_m)
            pe_rows(pe, 2)
            pe_scatter(pe)
            pe_readback(pe)
            pe_linear(pe, 6, [("L1_W1", A)], after_src=(yT_kept, 1))
            pe_linear(pe, 7, [("L1_W2", B)], after_src=(lin_taken, 6 * NBLK + 1))
            pe_center(pe, 1)
            pe_norm(pe, 2, B, mean_m)
            pe_rows(pe, 3)
            pe_sum(pe, 3, extra="weight")
            pe_linear(pe, 8, [("L2_W_l", A), ("L2_W_r", X)], after_src=(lin_src, 3 * NBLK))
            pe_center(pe, 2)
            pe_norm(pe, 3, B, mean_m)
            pe_rows(pe, 4)
            pe_linear(pe, 9, [("L3_W_pool", X)], after_src=(ss_kept, 4 * NBLK + 1))
            pe_rows(pe, 5)
            pe_max(pe, MAX_PASS)
            pe_linear(pe, 10, [("L3_W1_self", X), ("L3_W1_neigh", A)], after_src=(lin_src, 5 * NBLK))
            pe_norm(pe, 4, A, ones)
            pe_rows(pe, 6)
            pe_sum(pe, 5)
            pe_linear(pe, 11, [("L3_W2_self", B), ("L3_W2_neigh", A)], after_src=(lin_src, 6 * NBLK))
            pe_center(pe, 3)
            pe_norm(pe, 5, B, mean_m)
            pe_rows(pe, 7)


WEIGHTS = {
    **{f"L0_W1_{m}": ("L0_gnn_W1", m, False) for m in range(3)},
    **{f"L0_W2_{m}": ("L0_gnn_W2", m, False) for m in range(3)},
    "L1_W1": ("L1_gnn_W1", None, True), "L1_W2": ("L1_gnn_W2", None, True),
    "L2_W_l": ("L2_gnn_W_l", None, True), "L2_W_r": ("L2_gnn_W_r", None, True),
    "L3_W_pool": ("L3_gnn_W_pool", None, False),
    "L3_W1_self": ("L3_gnn_W1_self", None, False), "L3_W1_neigh": ("L3_gnn_W1_neigh", None, False),
    "L3_W2_self": ("L3_gnn_W2_self", None, False), "L3_W2_neigh": ("L3_gnn_W2_neigh", None, False),
}
VECTORS = {
    **{f"L0_{v}_{m}": (f"L0_gnn_{v}", m) for v in ("b1", "g1", "be1", "b2") for m in range(3)},
    **{f"L0_{v}_{m}": (f"L0_gnn_{v}", m) for v in ("gbn", "bbn") for m in range(2)},
    "L1_b1": ("L1_gnn_b1", None), "L1_b2": ("L1_gnn_b2", None),
    "L2_b_l": ("L2_gnn_b_l", None), "L2_gamma": ("L2_gnn_gamma", None), "L2_beta": ("L2_gnn_beta", None),
    "L3_b_pool": ("L3_gnn_b_pool", None), "L3_b1": ("L3_gnn_b1", None), "L3_b2": ("L3_gnn_b2", None),
}


def kernel(**inputs):
    import concourse.bacc as bacc
    from concourse.bass_utils import run_bass_kernel_spmd

    def edges(x, tiles, pad):
        flat = np.full(tiles * 128, pad, x.dtype)
        flat[:x.size] = x
        return np.ascontiguousarray(flat.reshape(tiles, 128).T)

    x, dst = np.asarray(inputs["x"]), np.asarray(inputs["dst"])
    padded = np.full(EP + 2, N, dst.dtype)
    padded[0], padded[-1] = -1, -1
    padded[1:E + 1] = dst
    pick = lambda name, m: np.asarray(inputs[name]) if m is None else np.asarray(inputs[name])[m]
    arrays = {
        "x": x,
        "x_t": np.ascontiguousarray(x.T),
        "src_t": edges(np.asarray(inputs["src"]), T + 2 * GT, 0),
        "ew_t": edges(np.asarray(inputs["edge_weight"]), T + GT, 0),
        "dst_t": edges(padded[1:-1], T, N),
        "dst_next_t": edges(padded[2:], T, N),
        "dst_rows": np.ascontiguousarray(padded[1:-1].reshape(G, GE)),
        "dst_prev_rows": np.ascontiguousarray(padded[:-2].reshape(G, GE)),
        "weights": np.ascontiguousarray(np.stack(
            [pick(n, m).T if t else pick(n, m) for n, m, t in WEIGHTS.values()], axis=1)),
        "vectors": np.ascontiguousarray(np.stack([pick(n, m) for n, m in VECTORS.values()], axis=1)),
    }
    nc = bacc.Bacc("TRN2", target_bir_lowering=False, num_devices=1)
    handles = {n: nc.dram_tensor(f"in_{n}", v.shape, mybir.dt.from_np(v.dtype), kind="ExternalInput").ap()
               for n, v in arrays.items()}
    out = nc.dram_tensor("out", (N, D), mybir.dt.float32, kind="ExternalOutput").ap()
    build_program(nc, handles, out)
    return run_bass_kernel_spmd(nc, [{f"in_{n}": v for n, v in arrays.items()}], core_ids=[0]).results[0]["out"]
```

```python
import numpy as np
from contextlib import ExitStack
import concourse.bass as bass
from concourse import mybir

N = 6250
E = 106250
D = 128
GT = 8
G = 2 * -(-E // (2 * 128 * GT))
T = G * GT
EP = T * 128
GE = GT * 128
W = 128
NCOPY = 4
NR = N + 150
BLK = 625
NBLK = N // BLK
TN = 125
TPB = BLK // TN
YW = D + 1
BIG = 3.0e38
MAX_PASS = 4
BN_EPS = 1e-5
NORM_EPS = 1e-12


def build_program(nc, a, out):
    F32, I32, BF16 = mybir.dt.float32, mybir.dt.int32, mybir.dt.bfloat16
    ALU, ACT, AX = mybir.AluOpType, mybir.ActivationFunctionType, mybir.AxisListType
    ctx = ExitStack()
    with ctx:
        def sb(name, shape, dt=F32):
            return ctx.enter_context(nc.sbuf_tensor(name, shape, dt))

        def sem(name):
            return ctx.enter_context(nc.semaphore(name))

        table = nc.dram_tensor("table", [NR, D], F32).ap()
        ysum = [nc.dram_tensor(f"ysum{k}", [NR, YW], F32).ap() for k in range(NCOPY)]
        start_penalty = nc.dram_tensor("start_penalty", [G, GE], F32).ap()

        X = sb("X", [128, N])
        H = sb("H", [128, N + W])
        A = sb("A", [128, N + W])
        B = sb("B", [128, N])
        DEG = sb("DEG", [128, N + W])
        WS = H
        gbuf = [sb(f"gbuf{b}", [128, GT, D]) for b in range(2)]
        sel = [sb(f"sel{b}", [128, GT, W]) for b in range(2)]
        SS = [sb(f"SS{b}", [128, BLK]) for b in range(2)]
        ST = [sb(f"ST{b}", [128, TPB, D]) for b in range(2)]
        src_i = sb("src_i", [128, T + 2 * GT], I32)
        dst_f = sb("dst_f", [128, T])
        src_f = sb("src_f", [128, T + 2 * GT])
        flag_i = sb("flag_i", [1, 1], I32)
        keyloc = sb("keyloc", [128, T + GT])
        ew = sb("ew", [128, T + GT])
        is_end = sb("is_end", [128, T + GT])
        idx_slot = [sb(f"idx_slot{b}", [128, GT], I32) for b in range(2)]
        col_slot = [sb(f"col_slot{b}", [128, GT]) for b in range(2)]
        ident = sb("ident", [128, 128])
        iota = sb("iota", [128, W])
        ones = sb("ones", [128, 128])
        mean_m = sb("mean_m", [128, 128])
        base_i = sb("base_i", [1, G], I32)
        lohi = sb("lohi", [128, 4])
        eps_bn = sb("eps_bn", [128, 1])
        zero_c = sb("zero_c", [128, 1])
        stats = sb("stats", [128, 2 * NBLK, 6])
        mv = sb("mv", [128, 2])
        cf = sb("cf", [128, 5])
        wnames = list(WEIGHTS)
        weights = sb("weights", [128, len(wnames), 128])
        vnames = list(VECTORS)
        vectors = sb("vectors", [128, len(vnames)])
        wt = {n: weights[:, i, :] for i, n in enumerate(wnames)}
        vec = {n: vectors[:, i:i + 1] for i, n in enumerate(vnames)}
        scan = [B[:, b * GE:(b + 1) * GE] for b in range(2)]
        pen = [B[:, (2 + b) * GE:(3 + b) * GE] for b in range(2)]
        scan_rows_flat = B[:, 4 * GE:5 * GE]
        scan_rows = scan_rows_flat.rearrange("p (k f) -> p k f", k=GT)
        diag = B[:, 5 * GE:6 * GE].rearrange("p (k e) -> p k e", k=GT)
        same = A[:, 0:GE // 2].bitcast(BF16).rearrange("p (k e) -> p k e", k=GT)
        onehot = [A[:, (1 + b) * GE // 2:(2 + b) * GE // 2].bitcast(BF16).rearrange("p (k e) -> p k e", k=GT)
                  for b in range(2)]
        before = B[:, 0:GE].rearrange("p (k e) -> p k e", k=GT)
        earlier = sb("earlier", [128, 128])
        mcount = B[:, 2 * GE:3 * GE].rearrange("p (k e) -> p k e", k=GT)
        rank = B[:, 3 * GE:3 * GE + GT]
        to_row = B[:, 3 * GE + 16:3 * GE + 16 + GT]
        trash = sb("trash", [128, 1])
        xwin = [B[:, 3 * GE + 64 + 132 * b:3 * GE + 64 + 132 * b + YW] for b in range(2)]
        summed_rows = [A[:, 3 * GE // 2 + b * GT * YW:3 * GE // 2 + (b + 1) * GT * YW]
                       .rearrange("p (k f) -> p k f", k=GT) for b in range(2)]
        dst_i = B[:, 0:T].bitcast(I32)
        next_i = B[:, T:2 * T].bitcast(I32)
        next_f = B[:, 2 * T:3 * T]
        least = B[:, 3 * T:3 * T + G]
        row_i = A[0:G, 0:GE].bitcast(I32)
        prev_i = A[0:G, GE:2 * GE].bitcast(I32)
        row_pen = B[0:G, 3 * T + 2 * G:3 * T + 2 * G + GE]
        most = B[:, 3 * T + G:3 * T + 2 * G]
        key_i = DEG[:, 0:T + 2 * GT].bitcast(I32)
        parts = [[B, H][b][0:TN, 0:NCOPY * TPB * YW] for b in range(2)]
        ytot = [gbuf[b][0:TN, :, :].rearrange("p k f -> p (k f)")[:, 0:TPB * YW] for b in range(2)]
        ydeg = sb("ydeg", [128, 2, TPB])
        yrow = ST

        PS = ctx.enter_context(nc.psum_tensor("PS", [128, 4096], F32))
        blk_ps = [PS[:, 1024 * b:1024 * b + BLK] for b in range(2)]
        row_ps = [PS[:, 2048 + 1024 * b:2048 + 1024 * b + TPB * 128] for b in range(2)]
        agg_ps = [PS[:, 512 * b:512 * b + W] for b in range(2)]
        extra_ps = [PS[:, 1024 + 512 * b:1024 + 512 * b + W] for b in range(2)]
        msg_ps = [PS[:, 1024:2048], PS[:, 3072:4096]]
        rev_ps = PS[:, 2048:3072]
        keyrow_ps = PS[:, 0:1024]
        m_ps = PS[:, 1024:2048]
        v_ps = PS[:, 2048:4096].rearrange("p (k f) -> p k f", k=GT)

        loaded = sem("loaded")
        dve_chain = sem("dve_chain")
        const_ready = sem("const_ready")
        lohi_ps = sem("lohi_ps")
        lohi_done = sem("lohi_done")
        base_ps = sem("base_ps")
        setup_done = sem("setup_done")
        flag_ps = sem("flag_ps")
        flag_ready = sem("flag_ready")
        general_slots = sem("general_slots")
        general_full = sem("general_full")
        general_used = sem("general_used")
        pen_out = sem("pen_out")
        ysum_zeroed = sem("ysum_zeroed")
        idx_ready = sem("idx_ready")
        gathered = [sem(f"gathered{b}") for b in range(2)]
        sel_ready = sem("sel_ready")
        summed = sem("summed")
        placed = sem("placed")
        pass_clear = sem("pass_clear")
        msg_full = sem("msg_full")
        pen_in = [sem(f"pen_in{b}") for b in range(2)]
        diag_ready = sem("diag_ready")
        scanned = sem("scanned")
        rev_full = sem("rev_full")
        rev_kept = sem("rev_kept")
        lin_src = sem("lin_src")
        lin_full = sem("lin_full")
        lin_taken = sem("lin_taken")
        aff_done = sem("aff_done")
        stats_done = sem("stats_done")
        bn_var = sem("bn_var")
        bn_sd = sem("bn_sd")
        bn_coef = sem("bn_coef")
        ss_ready = sem("ss_ready")
        ss_kept = sem("ss_kept")
        rows_full = sem("rows_full")
        rows_staged = sem("rows_staged")
        rows_out = [sem(f"rows_out{b}") for b in range(2)]
        added = sem("added")
        mean_full = sem("mean_full")
        centered = sem("centered")
        sq_ready = sem("sq_ready")
        norm_full = sem("norm_full")
        sd_ready = sem("sd_ready")
        blk_chain = sem("blk_chain")
        scaled = sem("scaled")
        kr_full = sem("kr_full")
        same_ready = sem("same_ready")
        m_full = sem("m_full")
        m_kept = sem("m_kept")
        v_full = sem("v_full")
        v_kept = sem("v_kept")
        xwin_in = [sem(f"xwin_in{b}") for b in range(2)]
        xwin_ones = sem("xwin_ones")
        row_idx = sem("row_idx")
        col_ready = sem("col_ready")
        hot_ready = sem("hot_ready")
        rank_chain = sem("rank_chain")
        scattered = [sem(f"scattered{k}") for k in range(NCOPY)]
        parts_in = [sem(f"parts_in{b}") for b in range(2)]
        parts_used = sem("parts_used")
        yrow_ready = sem("yrow_ready")
        y_chain = sem("y_chain")
        yT_full = sem("yT_full")
        yT_kept = sem("yT_kept")

        tick = sb("tick", [128, 4])
        block = ctx.enter_context(nc.Block())

        def cols(i, b):
            return bass.ds(i * (2 * BLK) + b * BLK, BLK)

        def tiles(i, b, ahead=0):
            return bass.ds(i * (2 * GT) + (b + ahead) * GT, GT)

        def bc(col, n):
            return col.to_broadcast([128, n])

        def rows_written(eng, n):
            for b in range(2):
                eng.wait_ge(rows_out[b], 16 * (NBLK // 2) * n)

        def pool_gather(pool, q, source):
            group = pool.alloc_register(f"gather_group{q}")
            pool.reg_mov(group, 1)
            with pool.Fori(0, G // 2) as i:
                for b in range(2):
                    g = pool.snap(group, min_val=1, max_val=G)
                    if q == MAX_PASS:
                        pool.wait_ge(msg_full, g)
                    else:
                        pool.wait_ge(summed, g + q * G)
                    pool.wait_ge(idx_ready, g + q * (G + 2))
                    pool.reg_add(group, group, 1)
                    for k in range(GT):
                        nc.gpsimd.indirect_dma_start(
                            out=gbuf[b][:, k, :], out_offset=None, in_=source,
                            in_offset=bass.IndirectOffsetOnAxis(ap=idx_slot[b][:, k:k + 1], axis=0),
                        ).then_inc(gathered[b], 16)

        def q_sel(q):
            return q * (G + 1) - (1 if q > MAX_PASS else 0)

        def gathered_value(q, i):
            return i * (16 * GT) + 16 * GT * (1 + q * (G // 2))

        def pe_sum(pe, q, extra=None):
            with pe.Fori(0, G // 2) as i:
                for b in range(2):
                    pe.wait_ge(gathered[b], gathered_value(q, i))
                    pe.wait_ge(sel_ready, q_sel(q) + i * 2 + (b + 1))
                    pe.wait_ge(placed, q * G + i * 2 + (b + 1))
                    for k in range(GT):
                        last = nc.tensor.matmul(agg_ps[b], gbuf[b][:, k, :], sel[b][:, k, :],
                                                start=(k == 0), stop=(k == GT - 1))
                    if extra is not None:
                        for k in range(GT):
                            left = ones[:, :] if extra == "degree" else bc(col_slot[b][:, k:k + 1], 128)
                            last = nc.tensor.matmul(extra_ps[b], left, sel[b][:, k, :],
                                                    start=(k == 0), stop=(k == GT - 1))
                    last.then_inc(summed, 1)
            pe.wait_ge(placed, G * (q + 1) + 2)

        def pe_max(pe, q):
            def weigh(i, b):
                pe.wait_ge(gathered[b], gathered_value(q, i))
                pe.wait_ge(diag_ready, i * 2 + (b + 1))
                pe.wait_ge(scanned, i * 2 + (b + 1))
                for k in range(GT):
                    last = nc.tensor.matmul(msg_ps[b][:, k * 128:(k + 1) * 128], gbuf[b][:, k, :],
                                            diag[:, k, :], start=True, stop=True)
                last.then_inc(msg_full, 1)

            def ends(i, b):
                pe.wait_ge(scanned, i * 2 + (b + 3))
                pe.wait_ge(rev_kept, i * 2 + (b + 1))
                for k in range(GT):
                    last = nc.tensor.transpose(rev_ps[:, k * 128:(k + 1) * 128],
                                               scan[b][:, k * 128:(k + 1) * 128], ident[:, :])
                last.then_inc(rev_full, 1)
                pe.wait_ge(rev_kept, i * 2 + (b + 2))
                pe.wait_ge(sel_ready, q_sel(q) + i * 2 + (b + 1))
                pe.wait_ge(placed, q * G + i * 2 + (b + 1))
                for k in range(GT):
                    last = nc.tensor.matmul(agg_ps[b], scan_rows[:, k, :], sel[b][:, k, :],
                                            start=(k == 0), stop=(k == GT - 1))
                last.then_inc(summed, 1)

            weigh(0, 0)
            with pe.Fori(0, G // 2 - 1) as i:
                weigh(i, 1)
                ends(i, 0)
                weigh(i + 1, 0)
                ends(i, 1)
            weigh(G // 2 - 1, 1)
            ends(G // 2 - 1, 0)
            ends(G // 2 - 1, 1)
            pe.wait_ge(placed, G * (q + 1) + 2)

        def act_max(act):
            def diagonals(i, b):
                act.wait_ge(msg_full, i * 2 + (b + 2))
                for k in range(GT):
                    last = nc.scalar.activation(diag[:, k, :], ident[:, :], ACT.Copy,
                                                scale=ew[:, bass.ds(i * (2 * GT) + (b * GT + k), 1)])
                last.then_inc(diag_ready, 1)

            def keep(i, b):
                act.wait_ge(rev_full, i * 2 + (b + 1))
                act.wait_ge(summed, MAX_PASS * G + i * 2 + (b + 2))
                nc.scalar.activation(scan_rows_flat, rev_ps, ACT.Copy).then_inc(rev_kept, 1)

            diagonals(0, 0)
            with act.Fori(0, G // 2 - 1) as i:
                diagonals(i, 1)
                keep(i, 0)
                diagonals(i + 1, 0)
                keep(i, 1)
            diagonals(G // 2 - 1, 1)
            keep(G // 2 - 1, 0)
            keep(G // 2 - 1, 1)

        def dve_max(dve, q, clears):
            fill_first(dve)
            dve_clear(dve)
            dve.wait_ge(pass_clear, clears)
            with dve.Fori(0, G // 2) as i:
                for b in range(2):
                    base = dve.value_load(base_i[0:1, bass.ds(i * 2 + b, 1)], min_val=0, max_val=N)
                    at = lambda k, n: bass.ds(i * (2 * GT) + (b * GT + k), n)
                    dve.wait_ge(msg_full, i * 2 + (b + 3))
                    dve.wait_ge(pen_in[b], i * 16 + 16)
                    dve.wait_ge(scanned, i * 2 + (b + 2))
                    nc.vector.tensor_tensor_scan(scan[b], pen[b], msg_ps[b], scan[1 - b][:, GE - 1:GE],
                                                 ALU.add, ALU.max).then_inc(scanned, 1)
                    fill_slots(dve, i, b, 2)
                    build_sel(dve, sel[b], at, is_end).then_inc(sel_ready, 1)
                    dve.wait_ge(summed, q * G + i * 2 + (b + 3))
                    dve.wait_ge(placed, q * G + i * 2 + (b + 2))
                    nc.vector.tensor_tensor(out=A[:, bass.ds(base, W)], in0=A[:, bass.ds(base, W)],
                                            in1=agg_ps[b], op=ALU.add).then_inc(placed, 1)
            dve.wait_ge(placed, 2 + G * (q + 1))

        def sp_max(sp):
            with sp.Fori(0, G // 2) as i:
                for b in range(2):
                    sp.wait_ge(scanned, i * 2 + (b + 1))
                    sp.dma_start(pen[b], start_penalty[bass.ds(i * 2 + b, 1), :].to_broadcast([128, GE])
                                 ).then_inc(pen_in[b], 16)

        def dve_clear(dve, extra=None, start=None):
            if start is None:
                nc.vector.memset(A[:, :], 0.0).then_inc(pass_clear, 1)
            else:
                if start is not A:
                    nc.vector.tensor_copy(A[:, 0:N], start[:, 0:N])
                nc.vector.memset(A[:, N:N + W], 0.0).then_inc(pass_clear, 1)
            if extra is not None:
                nc.vector.memset(extra[:, :], 0.0).then_inc(pass_clear, 1)

        def fill_slots(dve, i, b, ahead):
            nc.vector.tensor_copy(idx_slot[b][:, :], src_i[:, tiles(i, b, ahead)]).then_inc(idx_ready, 1)

        def fill_first(dve):
            for b in range(2):
                nc.vector.tensor_copy(idx_slot[b][:, :], src_i[:, b * GT:(b + 1) * GT]).then_inc(idx_ready, 1)

        def build_sel(dve, where, at, scale=None):
            if scale is None:
                return nc.vector.tensor_tensor(
                    out=where[:, :, :], in0=iota[:, :].unsqueeze(1).to_broadcast([128, GT, W]),
                    in1=keyloc[:, at(0, GT)].unsqueeze(2).to_broadcast([128, GT, W]), op=ALU.is_equal)
            for k in range(GT):
                last = nc.vector.tensor_scalar(where[:, k, :], iota[:, :], keyloc[:, at(k, 1)],
                                               scale[:, at(k, 1)], ALU.is_equal, ALU.mult)
            return last

        def dve_sum(dve, q, extra=None, scale=None, extra_cols=None, clears=0, start=None):
            def one_group(i, b, ahead):
                g = b + ahead
                at = lambda k, n: bass.ds(i * (2 * GT) + (g * GT + k), n)
                if extra_cols is not None:
                    nc.vector.tensor_copy(col_slot[g % 2][:, :], extra_cols[:, at(0, GT)])
                build_sel(dve, sel[g % 2], at, scale).then_inc(sel_ready, 1)
            fill_first(dve)
            dve_clear(dve, extra, start)
            one_group(0, 0, 0)
            dve.wait_ge(pass_clear, clears)
            with dve.Fori(0, G // 2) as i:
                for b in range(2):
                    base = dve.value_load(base_i[0:1, bass.ds(i * 2 + b, 1)], min_val=0, max_val=N)
                    one_group(i, b, 1)
                    dve.wait_ge(summed, q * G + i * 2 + (b + 3))
                    fill_slots(dve, i, b, 2)
                    dve.wait_ge(placed, q * G + i * 2 + (b + 2))
                    last = nc.vector.tensor_tensor(out=A[:, bass.ds(base, W)], in0=A[:, bass.ds(base, W)],
                                                   in1=agg_ps[b], op=ALU.add)
                    if extra is not None:
                        last = nc.vector.tensor_tensor(out=extra[:, bass.ds(base, W)],
                                                       in0=extra[:, bass.ds(base, W)],
                                                       in1=extra_ps[b], op=ALU.add)
                    last.then_inc(placed, 1)
            dve.wait_ge(placed, 2 + G * (q + 1))

        def block_matmul(ps, left, src, i, b, start, stop):
            nc.tensor.matmul(ps[:, 0:512], left, src[:, bass.ds(i * (2 * BLK) + b * BLK, 512)],
                             start=start, stop=stop)
            return nc.tensor.matmul(ps[:, 512:BLK], left,
                                    src[:, bass.ds(i * (2 * BLK) + (b * BLK + 512), BLK - 512)],
                                    start=start, stop=stop)

        def pe_linear(pe, n, terms, after_src=None, free=None):
            with pe.Fori(0, NBLK // 2) as i:
                for b in range(2):
                    if after_src is not None:
                        pe.wait_ge(after_src[0], after_src[1] + i * 2 + (b + 1))
                    if free is not None:
                        pe.wait_ge(free[0], free[1])
                    pe.wait_ge(lin_taken, NBLK * n + i * 2 + (b + 1))
                    for j, (w, src) in enumerate(terms):
                        last = block_matmul(blk_ps[b], wt[w], src, i, b, j == 0, j == len(terms) - 1)
                    last.then_inc(lin_full, 1)
            pe.wait_ge(lin_taken, NBLK * (n + 1) + 2)

        def act_linear(act, n, func, bias, dst):
            with act.Fori(0, NBLK // 2) as i:
                for b in range(2):
                    act.wait_ge(lin_full, NBLK * n + i * 2 + (b + 1))
                    nc.scalar.activation(dst[:, cols(i, b)], blk_ps[b], func, bias=vec[bias]).then_inc(lin_taken, 1)

        def in_pairs(eng, block_of, row_of):
            block_of(0, 0)
            block_of(0, 1)
            row_of(0, 0)
            block_of(1, 0)
            row_of(0, 1)
            with eng.Fori(1, NBLK // 2 - 1) as i:
                block_of(i, 1)
                row_of(i, 0)
                block_of(i + 1, 0)
                row_of(i, 1)
            block_of(NBLK // 2 - 1, 1)
            row_of(NBLK // 2 - 1, 0)
            row_of(NBLK // 2 - 1, 1)

        def act_linear_rows(act, n, r, func, bias):
            def block_of(i, b):
                act.wait_ge(lin_full, NBLK * n + i * 2 + (b + 1))
                act.wait_ge(rows_full, NBLK * r + i * 2 + (b + 1))
                nc.scalar.activation(SS[b][:, :], blk_ps[b], func, bias=vec[bias]).then_inc(ss_ready, 1)
            in_pairs(act, block_of, lambda i, b: act_row(act, r, i, b))
            act.sem_inc(lin_taken, NBLK)

        def pe_linear_rows(pe, n, r, w, src):
            def block_of(i, b):
                pe.wait_ge(ss_ready, NBLK * r - 1 + i * 2 + b)
                block_matmul(blk_ps[b], wt[w], src, i, b, True, True).then_inc(lin_full, 1)

            def row_of(i, b):
                pe_row(pe, r, i, b)

            in_pairs(pe, block_of, row_of)
            pe.wait_ge(rows_staged, NBLK * (r + 1) + 2)

        def act_affine(act, m, src, dst=None, ss=None):
            act.wait_ge(bn_coef, m + 1)
            if ss is None:
                with act.Fori(0, NBLK // 2) as i:
                    for b in range(2):
                        nc.scalar.activation(dst[:, cols(i, b)], src[:, cols(i, b)], ACT.Relu, bias=cf[:, 4:5],
                                             scale=cf[:, 3:4]).then_inc(aff_done, 1)
                return

            def block_of(i, b):
                act.wait_ge(rows_full, NBLK * ss + i * 2 + (b + 1))
                act.wait_ge(ss_kept, NBLK * ss + i * 2 + (b + 1))
                nc.scalar.activation(SS[b][:, :], src[:, cols(i, b)], ACT.Relu, bias=cf[:, 4:5],
                                     scale=cf[:, 3:4]).then_inc(ss_ready, 1)
            in_pairs(act, block_of, lambda i, b: act_row(act, ss, i, b))

        def dve_stats(dve, n, s, src):
            with dve.Fori(0, NBLK // 2) as i:
                for b in range(2):
                    dve.wait_ge(lin_taken, NBLK * n + i * 2 + (b + 3))
                    for h, (lo, w) in enumerate(((0, 313), (313, 312))):
                        nc.vector.bn_stats(stats[:, bass.ds(i * 4 + (2 * b + h), 1), :].rearrange("p a s -> p (a s)"),
                                           src[:, bass.ds(i * (2 * BLK) + (b * BLK + lo), w)]
                                           ).then_inc(stats_done, 1)

        def dve_batchnorm(dve, m, gamma, beta):
            dve.wait_ge(stats_done, 2 * NBLK * (m + 1))
            nc.vector.bn_aggr(mv[:, :], stats[:, :, :].rearrange("p a s -> p (a s)")).then_inc(bn_var, 1)
            dve.wait_ge(bn_sd, m + 1)
            link(dve, nc.vector.reciprocal(cf[:, 1:2], cf[:, 0:1]))
            link(dve, nc.vector.tensor_tensor(out=cf[:, 3:4], in0=cf[:, 1:2], in1=vec[gamma], op=ALU.mult))
            link(dve, nc.vector.tensor_tensor(out=cf[:, 2:3], in0=cf[:, 3:4], in1=mv[:, 0:1], op=ALU.mult))
            nc.vector.tensor_tensor(out=cf[:, 4:5], in0=vec[beta], in1=cf[:, 2:3],
                                    op=ALU.subtract).then_inc(bn_coef, 1)

        def act_batchnorm(act, m):
            act.wait_ge(bn_var, m + 1)
            nc.scalar.activation(cf[:, 0:1], mv[:, 1:2], ACT.Sqrt, bias=eps_bn[:, :]).then_inc(bn_sd, 1)

        def pe_row(pe, r, i, b):
            pe.wait_ge(ss_ready, NBLK * r + i * 2 + (b + 1))
            pe.wait_ge(rows_staged, NBLK * r + i * 2 + (b + 1))
            for j in range(TPB):
                last = nc.tensor.transpose(row_ps[b][0:TN, j * 128:(j + 1) * 128],
                                           SS[b][:, j * TN:(j + 1) * TN], ident[:, :])
            last.then_inc(rows_full, 1)

        def pe_rows(pe, r):
            with pe.Fori(0, NBLK // 2) as i:
                for b in range(2):
                    pe_row(pe, r, i, b)
            pe.wait_ge(rows_staged, NBLK * (r + 1) + 2)

        def act_row(act, r, i, b):
            act.wait_ge(rows_full, NBLK * r + i * 2 + (b + 3))
            if r or not isinstance(i, int) or i:
                act.wait_ge(rows_out[b], 16 * (NBLK // 2) * r + i * 16)
            nc.scalar.activation(ST[b][0:TN, :, :], row_ps[b][0:TN, :].rearrange("p (j f) -> p j f", j=TPB),
                                 ACT.Copy).then_inc(rows_staged, 1)

        def sp_rows(sp, r, where):
            with sp.Fori(0, NBLK // 2) as i:
                for b in range(2):
                    sp.wait_ge(rows_staged, NBLK * r + i * 2 + (b + 3))
                    sp.dma_start(where[cols(i, b), :].rearrange("(j p) f -> p j f", p=TN),
                                 ST[b][0:TN, :, :]).then_inc(rows_out[b], 16)

        def dve_center(dve, n, term, after=None):
            with dve.Fori(0, NBLK // 2) as i:
                for b in range(2):
                    if after is not None:
                        dve.wait_ge(after[0], after[1] + i * 2 + (b + 1))
                    nc.vector.tensor_tensor(out=X[:, cols(i, b)], in0=X[:, cols(i, b)],
                                            in1=term[:, cols(i, b)], op=ALU.add).then_inc(added, 1)
            with dve.Fori(0, NBLK // 2) as i:
                for b in range(2):
                    dve.wait_ge(mean_full, NBLK * n + i * 2 + (b + 1))
                    nc.vector.tensor_tensor(out=X[:, cols(i, b)], in0=X[:, cols(i, b)],
                                            in1=blk_ps[b], op=ALU.subtract).then_inc(centered, 1)

        def pe_center(pe, n):
            with pe.Fori(0, NBLK // 2) as i:
                for b in range(2):
                    pe.wait_ge(added, NBLK * n + i * 2 + (b + 1))
                    pe.wait_ge(centered, NBLK * n + i * 2 + (b + 1))
                    block_matmul(blk_ps[b], mean_m[:, :], X, i, b, True, True).then_inc(mean_full, 1)
            pe.wait_ge(centered, NBLK * (n + 1) + 2)

        def act_norm(act, n, src, sq, eps, after, keep=None, rows=None):
            with act.Fori(0, NBLK // 2) as i:
                for b in range(2):
                    act.wait_ge(after[0], after[1] + i * 2 + (b + 1))
                    nc.scalar.activation(sq[:, cols(i, b)], src[:, cols(i, b)], ACT.Square).then_inc(sq_ready, 1)
            with act.Fori(0, NBLK // 2) as i:
                for b in range(2):
                    act.wait_ge(norm_full, NBLK * n + i * 2 + (b + 1))
                    nc.scalar.activation(sq[:, cols(i, b)], blk_ps[b], ACT.Sqrt, bias=eps).then_inc(sd_ready, 1)
            if rows is not None:
                with act.Fori(0, NBLK // 2) as i:
                    for b in range(2):
                        act.wait_ge(ss_ready, NBLK * rows + i * 2 + (b + 1))
                        if keep is not None:
                            nc.scalar.activation(keep[:, cols(i, b)], SS[b][:, :], ACT.Copy).then_inc(ss_kept, 1)
                        act_row(act, rows, i, b)

        def pe_norm(pe, n, sq, left):
            with pe.Fori(0, NBLK // 2) as i:
                for b in range(2):
                    pe.wait_ge(sq_ready, NBLK * n + i * 2 + (b + 1))
                    pe.wait_ge(sd_ready, NBLK * n + i * 2 + (b + 1))
                    block_matmul(blk_ps[b], left[:, :], sq, i, b, True, True).then_inc(norm_full, 1)
            pe.wait_ge(sd_ready, NBLK * (n + 1) + 2)

        def dve_norm(dve, n, src, sq, floor=None, relu=False, dst=None, rows=None, kept=None):
            with dve.Fori(0, NBLK // 2) as i:
                for b in range(2):
                    r = sq[:, cols(i, b)]
                    dve.wait_ge(sd_ready, NBLK * n + i * 2 + (b + 3))
                    if floor is not None:
                        nc.vector.tensor_scalar(r, r, floor, None, ALU.max).then_inc(blk_chain, 1)
                    else:
                        dve.sem_inc(blk_chain, 1)
                    dve.wait_ge(blk_chain, 3 * NBLK * n + i * 6 + (3 * b + 1))
                    nc.vector.tensor_copy(tick[:, 3:4], tick[:, 2:3]).then_inc(blk_chain, 1)
                    nc.vector.reciprocal(r, r).then_inc(blk_chain, 1)
                    dve.wait_ge(blk_chain, 3 * NBLK * n + i * 6 + (3 * b + 3))
                    if rows is not None:
                        dve.wait_ge(rows_full, NBLK * rows + i * 2 + (b + 1))
                        if kept is not None:
                            dve.wait_ge(ss_kept, kept + i * 2 + (b + 1))
                    to = SS[b][:, :] if rows is not None else dst[:, cols(i, b)]
                    if relu:
                        ins = nc.vector.scalar_tensor_tensor(out=to, in0=src[:, cols(i, b)], scalar=0.0, in1=r,
                                                             op0=ALU.max, op1=ALU.mult)
                    else:
                        ins = nc.vector.tensor_tensor(out=to, in0=src[:, cols(i, b)], in1=r, op=ALU.mult)
                    ins.then_inc(ss_ready if rows is not None else scaled, 1)
            if rows is not None:
                dve.wait_ge(ss_ready, NBLK * (rows + 1))

        def dve_times(dve, dst, other, op, tell, after=None):
            with dve.Fori(0, NBLK // 2) as i:
                for b in range(2):
                    if after is not None:
                        dve.wait_ge(after[0], after[1] + i * 2 + (b + 1))
                    nc.vector.tensor_tensor(out=dst[:, cols(i, b)], in0=dst[:, cols(i, b)],
                                            in1=other[:, cols(i, b)], op=op).then_inc(tell, 1)

        def dve_keep(dve, r):
            with dve.Fori(0, NBLK // 2) as i:
                for b in range(2):
                    dve.wait_ge(ss_ready, NBLK * r + i * 2 + (b + 1))
                    nc.vector.tensor_copy(A[:, cols(i, b)], SS[b][:, :]).then_inc(ss_kept, 1)
            dve.wait_ge(ss_kept, NBLK * (r + 1) + 2)

        chained = [0]

        def link(dve, ins):
            chained[0] += 1
            ins.then_inc(dve_chain, 1)
            dve.wait_ge(dve_chain, chained[0])

        def dve_scatter(dve):
            for b in range(2):
                nc.vector.memset(xwin[b][:, D:YW], 1.0).then_inc(xwin_ones, 1)
            for b in range(2):
                nc.vector.tensor_copy(col_slot[b][:, :], src_f[:, b * GT:(b + 1) * GT]).then_inc(col_ready, 1)
            with dve.Fori(0, G // 2) as i:
                for b in range(2):
                    at = lambda k, n: bass.ds(i * (2 * GT) + (b * GT + k), n)
                    dve.wait_ge(m_full, i * 2 + (b + 1))
                    build_sel(dve, onehot[b], at).then_inc(hot_ready, 1)
                    dve.wait_ge(kr_full, i * 2 + (b + 1))
                    dve.wait_ge(m_full, i * 2 + (b + 2))
                    nc.vector.tensor_tensor(
                        out=same, in0=keyrow_ps.rearrange("p (k e) -> p k e", k=GT),
                        in1=col_slot[b][:, :].unsqueeze(2).to_broadcast([128, GT, 128]),
                        op=ALU.is_equal).then_inc(same_ready, 1)
                    dve.wait_ge(same_ready, i * 2 + (b + 1))
                    step = lambda j: i * 8 + (4 * b + j)
                    nc.vector.tensor_tensor(out=before, in0=same,
                                            in1=earlier[:, :].unsqueeze(1).to_broadcast([128, GT, 128]),
                                            op=ALU.mult).then_inc(rank_chain, 1)
                    dve.wait_ge(rank_chain, step(1))
                    nc.vector.tensor_reduce(out=rank, in_=before, axis=AX.X, op=ALU.add).then_inc(rank_chain, 1)
                    nc.vector.tensor_scalar(to_row, col_slot[b][:, :], trash[:, :], None, ALU.subtract
                                            ).then_inc(rank_chain, 1)
                    dve.wait_ge(rank_chain, step(3))
                    nc.vector.scalar_tensor_tensor(out=to_row, in0=rank, scalar=0.0, in1=to_row,
                                                   op0=ALU.is_equal, op1=ALU.mult).then_inc(rank_chain, 1)
                    dve.wait_ge(rank_chain, step(4))
                    dve.wait_ge(v_kept, i * 2 + (b + 2))
                    nc.vector.tensor_scalar(idx_slot[b][:, :], to_row, trash[:, :], None, ALU.add
                                            ).then_inc(row_idx, 1)
                    nc.vector.tensor_copy(col_slot[b][:, :], src_f[:, tiles(i, b, 2)]).then_inc(col_ready, 1)

        def pe_scatter(pe):
            def key_rows(b):
                for k in range(GT):
                    last = nc.tensor.matmul(keyrow_ps[:, k * 128:(k + 1) * 128], bc(col_slot[b][:, k:k + 1], 128),
                                            ident[:, :], start=True, stop=True)
                last.then_inc(kr_full, 1)

            pe.wait_ge(xwin_ones, 2)
            pe.wait_ge(col_ready, 1)
            key_rows(0)
            with pe.Fori(0, G // 2) as i:
                for b in range(2):
                    pe.wait_ge(hot_ready, i * 2 + (b + 1))
                    pe.wait_ge(same_ready, i * 2 + (b + 1))
                    pe.wait_ge(m_kept, i * 2 + (b + 1))
                    for k in range(GT):
                        last = nc.tensor.matmul(m_ps[:, k * 128:(k + 1) * 128], onehot[b][:, k, :], same[:, k, :],
                                                start=True, stop=True)
                    last.then_inc(m_full, 1)
                    pe.wait_ge(col_ready, i * 2 + (b + 2))
                    key_rows(1 - b)
                    pe.wait_ge(m_kept, i * 2 + (b + 2))
                    pe.wait_ge(xwin_in[b], i * 16 + 16)
                    pe.wait_ge(v_kept, i * 2 + (b + 1))
                    for k in range(GT):
                        last = nc.tensor.matmul(v_ps[:, k, 0:YW], mcount[:, k, :], xwin[b], start=True, stop=True)
                    last.then_inc(v_full, 1)
            pe.wait_ge(v_kept, G + 1)

        def act_scatter(act):
            PER_COPY = 16 * GT // NCOPY

            def one_group(i, b):
                act.wait_ge(m_full, i * 2 + (b + 3))
                act.wait_ge(v_full, i * 2 + (b + 2))
                nc.scalar.activation(mcount, m_ps.rearrange("p (k e) -> p k e", k=GT), ACT.Copy).then_inc(m_kept, 1)
                act.wait_ge(v_full, i * 2 + (b + 3))
                if not isinstance(i, int):
                    for c in range(NCOPY):
                        act.wait_ge(scattered[c], i * (2 * PER_COPY) + PER_COPY * (b - 1))
                nc.scalar.activation(summed_rows[b], v_ps[:, :, 0:YW], ACT.Copy).then_inc(v_kept, 1)

            for b in range(2):
                one_group(0, b)
            with act.Fori(1, G // 2) as i:
                for b in range(2):
                    one_group(i, b)

        def pool_scatter(pool):
            added_to = [pool.alloc_register(f"added_to{c}") for c in range(NCOPY)]
            for c in range(NCOPY):
                pool.reg_mov(added_to[c], 16)

            def one_group(i, b):
                first = pool.snap(added_to[0], min_val=16, max_val=16 * T)
                pool.wait_ge(row_idx, i * 2 + (b + 1))
                pool.wait_ge(v_kept, i * 2 + (b + 2))
                for k in range(GT):
                    c = k % NCOPY
                    if k >= NCOPY or b or not isinstance(i, int):
                        pool.wait_ge(scattered[c], pool.snap(added_to[c], min_val=16, max_val=16 * T)
                                     if k else first)
                        pool.reg_add(added_to[c], added_to[c], 16)
                    nc.gpsimd.indirect_dma_start(
                        out=ysum[c], out_offset=bass.IndirectOffsetOnAxis(ap=idx_slot[b][:, k:k + 1], axis=0),
                        in_=summed_rows[b][:, k, :], in_offset=None, compute_op=ALU.add,
                    ).then_inc(scattered[c], 16)

            for b in range(2):
                one_group(0, b)
            with pool.Fori(1, G // 2) as i:
                for b in range(2):
                    one_group(i, b)

        def sp_scatter(sp):
            with sp.Fori(0, G // 2) as i:
                for b in range(2):
                    base = sp.value_load(base_i[0:1, bass.ds(i * 2 + b, 1)], min_val=0, max_val=N)
                    sp.wait_ge(v_full, i * 2 + (b + 1))
                    sp.dma_start(xwin[b][:, 0:D], table[bass.ds(base, W), :]).then_inc(xwin_in[b], 16)

        def sp_readback(sp):
            sp.wait_ge(v_kept, G + 1)
            for c in range(NCOPY):
                sp.wait_ge(scattered[c], 16 * T // NCOPY)
            with sp.Fori(0, NBLK // 2) as i:
                for b in range(2):
                    sp.wait_ge(parts_used, i * 2 + (b + 1))
                    for k in range(NCOPY):
                        sp.dma_start(parts[b][:, k * TPB * YW:(k + 1) * TPB * YW].rearrange("p (j f) -> p j f", j=TPB),
                                     ysum[k][cols(i, b), :].rearrange("(j p) f -> p j f", p=TN)
                                     ).then_inc(parts_in[b], 16)

        def dve_readback(dve):
            with dve.Fori(0, NBLK // 2) as i:
                for b in range(2):
                    step = lambda j: i * 6 + (3 * b + j)
                    dve.wait_ge(parts_in[b], i * (16 * NCOPY) + 16 * NCOPY)
                    nc.vector.tensor_reduce(out=ytot[b], in_=parts[b].rearrange("p (k m) -> p m k", k=NCOPY),
                                            axis=AX.X, op=ALU.add).then_inc(parts_used, 1)
                    dve.wait_ge(parts_used, i * 2 + (b + 3))
                    y3 = ytot[b].rearrange("p (j f) -> p j f", j=TPB)
                    nc.vector.tensor_scalar(ydeg[0:TN, b, :], y3[:, :, D], 1.0, None, ALU.max).then_inc(y_chain, 1)
                    dve.wait_ge(y_chain, step(1))
                    nc.vector.reciprocal(ydeg[0:TN, b, :], ydeg[0:TN, b, :]).then_inc(y_chain, 1)
                    dve.wait_ge(y_chain, step(2))
                    dve.wait_ge(yT_full, i * 2 + (b + 1))
                    nc.vector.tensor_tensor(out=yrow[b][0:TN, :, :], in0=y3[:, :, 0:D],
                                            in1=ydeg[0:TN, b, :].unsqueeze(2).to_broadcast([TN, TPB, D]),
                                            op=ALU.mult).then_inc(y_chain, 1)

        def pe_readback(pe):
            with pe.Fori(0, NBLK // 2) as i:
                for b in range(2):
                    pe.wait_ge(y_chain, i * 6 + (3 * b + 3))
                    pe.wait_ge(yT_kept, i * 2 + (b + 1))
                    for j in range(TPB):
                        last = nc.tensor.transpose(PS[:, 1024 * b + 128 * j:1024 * b + 128 * j + TN],
                                                   yrow[b][0:TN, j, :], ident[0:TN, 0:TN])
                    last.then_inc(yT_full, 1)
            pe.wait_ge(yT_kept, NBLK + 2)

        def act_readback(act):
            with act.Fori(0, NBLK // 2) as i:
                for b in range(2):
                    act.wait_ge(yT_full, i * 2 + (b + 3))
                    nc.scalar.activation(A[:, cols(i, b)].rearrange("p (j n) -> p j n", j=TPB),
                                         PS[:, 1024 * b:1024 * b + 128 * TPB].rearrange("p (j n) -> p j n", j=TPB)
                                         [:, :, 0:TN], ACT.Copy).then_inc(yT_kept, 1)

        def pool_general(pool, n, source):
            slots = pool.alloc_register(f"general_slots{n}")
            pool.reg_mov(slots, 3 * T * n + 3)
            with pool.Fori(0, T // 2) as i:
                for b in range(2):
                    pool.wait_ge(general_slots, pool.snap(slots, min_val=3, max_val=21 * T))
                    pool.reg_add(slots, slots, 3)
                    nc.gpsimd.indirect_dma_start(
                        out=gbuf[b][:, 0, :], out_offset=None, in_=source,
                        in_offset=bass.IndirectOffsetOnAxis(ap=idx_slot[b][:, 0:1], axis=0),
                    ).then_inc(gathered[b], 16)

        def pe_general(pe, n):
            with pe.Fori(0, T // 2) as i:
                for b in range(2):
                    pe.wait_ge(gathered[b], 16 * (T // 2) * n + i * 16 + 16)
                    nc.tensor.matmul(agg_ps[b], gbuf[b][:, 0, :], sel[b][:, 0, :], start=True, stop=True)
                    nc.tensor.matmul(extra_ps[b], bc(col_slot[b][:, 0:1], 128), ident[:, :],
                                     start=True, stop=True).then_inc(general_full, 1)
            pe.wait_ge(general_used, T * (n + 1))

        def dve_general(dve, n, keys, index, scale=None, extra=None, extra_cols=None, maximum=False,
                        start=None):
            nc.vector.memset(A[:, N if start is A else 0:N + W], -BIG if maximum else 0.0)
            if start is not None and start is not A:
                dve.drain()
                nc.vector.tensor_copy(A[:, 0:N], start[:, 0:N])
            if extra is not None:
                nc.vector.memset(extra[:, :], 0.0)
            dve.drain()
            with dve.Fori(0, T // 2) as i:
                for b in range(2):
                    t = bass.ds(i * 2 + b, 1)
                    nc.vector.tensor_copy(idx_slot[b][:, 0:1], index[:, t]).then_inc(general_slots, 1)
                    nc.vector.tensor_scalar(sel[b][:, 0, :], ident[:, :], ones[:, 0:1] if scale is None
                                            else scale[:, t], None, ALU.mult).then_inc(general_slots, 1)
                    nc.vector.tensor_copy(col_slot[b][:, 0:1], ones[:, 0:1] if extra_cols is None
                                          else extra_cols[:, t]).then_inc(general_slots, 1)
                    dve.wait_ge(general_full, T * n + i * 2 + (b + 1))
                    nc.vector.tensor_copy(tick[:, 3:4], tick[:, 2:3])
                    with dve.Fori(0, 128) as e:
                        key = dve.value_load(keys[0:1, bass.ds(i * 256 + e + b * 128, 1)], min_val=0, max_val=N)
                        col = bass.ds(key, 1)
                        nc.vector.tensor_tensor(out=A[:, col], in0=A[:, col], in1=agg_ps[b][:, bass.ds(e, 1)],
                                                op=ALU.max if maximum else ALU.add)
                        if extra is not None:
                            nc.vector.tensor_tensor(out=extra[:, col], in0=extra[:, col],
                                                    in1=extra_ps[b][:, bass.ds(e, 1)], op=ALU.add)
                        dve.drain()
                    dve.sem_inc(general_used, 1)
            if maximum:
                nc.vector.scalar_tensor_tensor(out=A[:, :], in0=A[:, :], scalar=-0.9 * BIG, in1=A[:, :],
                                               op0=ALU.is_gt, op1=ALU.mult)
                dve.drain()

        def either(eng, usual, general):
            with eng.If(flag[eng] == 0):
                usual()
            with eng.Else():
                general()

        def load_flag(eng):
            eng.wait_ge(flag_ready, 1)
            flag[eng] = eng.snap(eng.value_load(flag_i[0:1, 0:1], min_val=0, max_val=1))

        flag = {}

        @block.sync
        def _(sp):
            for dst, src in ((src_i[:, :], a["src_t"]), (ew[:, :], a["ew_t"]), (X[:, :], a["x_t"]), (weights[:, :, :], a["weights"]),
                             (vectors[:, :], a["vectors"]), (dst_i, a["dst_t"]), (next_i, a["dst_next_t"]),
                             (row_i, a["dst_rows"]), (prev_i, a["dst_prev_rows"]),
                             (key_i, a["src_key_t"])):
                sp.dma_start(dst, src).then_inc(loaded, 16)
            sp.wait_ge(setup_done, 1)
            sp.dma_start(start_penalty, row_pen).then_inc(pen_out, 16)
            sp.dma_start(table[N:NR, :].rearrange("(p r) f -> p (r f)", p=75), H[0:75, 0:2 * D]).then_inc(pen_out, 16)
            for k in range(NCOPY):
                zeroed = ysum[k].rearrange("a b -> (a b)").rearrange("(p c) -> p c", p=128)
                for c in range(5):
                    w = NR * YW // (128 * 5)
                    sp.dma_start(zeroed[:, c * w:(c + 1) * w], H[:, 0:w]).then_inc(ysum_zeroed, 16)
            sp.wait_ge(pen_out, 32)
            sp.wait_ge(ysum_zeroed, 16 * 5 * NCOPY)
            load_flag(sp)
            sp_rows(sp, 0, table)
            sp_rows(sp, 1, table)
            sp_rows(sp, 2, table)
            rows_written(sp, 3)
            with sp.If(flag[sp] == 0):
                sp_scatter(sp)
                sp_readback(sp)
            sp_rows(sp, 3, table)
            sp_rows(sp, 4, table)
            sp_rows(sp, 5, table)
            with sp.If(flag[sp] == 0):
                sp_max(sp)
            sp_rows(sp, 6, table)
            sp_rows(sp, 7, out)
            rows_written(sp, 8)

        @block.gpsimd
        def _(pool):
            nc.gpsimd.memset(ident[:, :], 1.0).then_inc(const_ready, 1)
            nc.gpsimd.memset(earlier[:, :], 1.0).then_inc(const_ready, 1)
            nc.gpsimd.iota(iota[:, :], pattern=[[1, W]], base=0, channel_multiplier=0,
                           allow_small_or_imprecise_dtypes=True).then_inc(const_ready, 1)
            nc.gpsimd.iota(trash[:, :], pattern=[[0, 1]], base=NR - 128, channel_multiplier=1,
                           allow_small_or_imprecise_dtypes=True).then_inc(const_ready, 1)
            pool.wait_ge(const_ready, 4)
            nc.gpsimd.affine_select(out=ident[:, :], in_=ident[:, :], compare_op=ALU.is_equal, fill=0.0, base=0,
                                    pattern=[[-1, 128]], channel_multiplier=1).then_inc(const_ready, 1)
            nc.gpsimd.affine_select(out=earlier[:, :], in_=earlier[:, :], compare_op=ALU.is_gt, fill=0.0, base=0,
                                    pattern=[[-1, 128]], channel_multiplier=1).then_inc(const_ready, 1)
            load_flag(pool)
            either(pool, lambda: pool_gather(pool, 0, a["x"]), lambda: pool_general(pool, 0, a["x"]))
            for q in (1, 2):
                rows_written(pool, q)
                either(pool, lambda: pool_gather(pool, q, table), lambda: pool_general(pool, q, table))
            rows_written(pool, 3)
            pool.wait_ge(ysum_zeroed, 16 * 5 * NCOPY)
            either(pool, lambda: pool_scatter(pool), lambda: pool_general(pool, 3, table))
            for q, r in ((3, 4), (4, 6), (5, 7)):
                rows_written(pool, r)
                either(pool, lambda: pool_gather(pool, q, table), lambda: pool_general(pool, q + 1, table))

        @block.scalar
        def _(act):
            act.wait_ge(pen_out, 32)
            load_flag(act)
            for m in range(3):
                act_linear(act, 2 * m, ACT.Identity, f"L0_b1_{m}", dst=B)
                act_batchnorm(act, 2 * m)
                act_affine(act, 2 * m, B, dst=A)
                act_linear(act, 2 * m + 1, ACT.Identity, f"L0_b2_{m}", dst=B)
                if m < 2:
                    act_batchnorm(act, 2 * m + 1)
                    act_affine(act, 2 * m + 1, B, ss=m)
            act_norm(act, 0, B, A, zero_c[:, :], (lin_taken, 5 * NBLK + 2))
            act_norm(act, 1, X, A, eps_bn[:, :], (centered, 2), keep=X, rows=2)
            with act.If(flag[act] == 0):
                act_scatter(act)
                act_readback(act)
            act_linear(act, 6, ACT.Relu, "L1_b1", dst=B)
            act_linear(act, 7, ACT.Identity, "L1_b2", dst=A)
            act_norm(act, 2, X, B, eps_bn[:, :], (centered, NBLK + 2), keep=X, rows=3)
            act_linear(act, 8, ACT.Identity, "L2_b_l", dst=B)
            act_batchnorm(act, 5)
            act_affine(act, 5, B, dst=A)
            act_norm(act, 3, X, B, eps_bn[:, :], (centered, 2 * NBLK + 2), keep=X, rows=4)
            act_linear_rows(act, 9, 5, ACT.Relu, "L3_b_pool")
            with act.If(flag[act] == 0):
                act_max(act)
            act_linear(act, 10, ACT.Identity, "L3_b1", dst=B)
            act_norm(act, 4, B, A, zero_c[:, :], (lin_taken, 10 * NBLK + 2), keep=B, rows=6)
            act_linear(act, 11, ACT.Relu, "L3_b2", dst=A)
            act_norm(act, 5, X, B, eps_bn[:, :], (centered, 3 * NBLK + 2), rows=7)

        @block.vector
        def _(dve):
            link(dve, nc.vector.memset(tick[:, 2:4], 0.0))
            for c in (summed, placed, msg_full, scanned, lin_taken, rows_full, rows_staged, ss_kept, centered,
                      sd_ready, m_full, v_full, parts_used, yT_full, yT_kept):
                dve.sem_inc(c, 2)
            for c in (rev_kept, m_kept, v_kept):
                dve.sem_inc(c, 1)
            nc.vector.memset(ones[:, :], 1.0)
            nc.vector.memset(mean_m[:, :], 1.0 / D)
            nc.vector.memset(eps_bn[:, :], BN_EPS)
            nc.vector.memset(zero_c[:, :], 0.0)
            nc.vector.memset(scan[1][:, GE - 1:GE], 0.0)
            nc.vector.memset(keyloc[:, :], -1.0)
            nc.vector.memset(is_end[:, :], 0.0)
            link(dve, nc.vector.memset(H[:, :], 0.0))
            dve.wait_ge(loaded, 16 * 10)
            nc.vector.tensor_copy(src_f[:, :], key_i)
            link(dve, nc.vector.tensor_copy(dst_f[:, :], dst_i))
            nc.vector.tensor_copy(next_f, next_i)
            link(dve, nc.vector.tensor_reduce(out=least, in_=dst_f[:, :].rearrange("p (g k) -> p g k", k=GT),
                                              axis=AX.X, op=ALU.min))
            link(dve, nc.vector.tensor_reduce(out=most, in_=dst_f[:, :].rearrange("p (g k) -> p g k", k=GT),
                                              axis=AX.X, op=ALU.max))
            dve.sem_inc(lohi_done, 1)
            nc.vector.tensor_tensor(out=is_end[:, 0:T], in0=dst_f[:, :], in1=next_f, op=ALU.not_equal)
            link(dve, nc.vector.tensor_tensor(out=row_pen, in0=row_i, in1=prev_i, op=ALU.is_lt))
            link(dve, nc.vector.tensor_reduce(out=lohi[0:G, 2:3], in_=row_pen, axis=AX.X, op=ALU.add))
            link(dve, nc.vector.tensor_tensor(out=row_pen, in0=row_i, in1=prev_i, op=ALU.is_equal))
            link(dve, nc.vector.tensor_scalar(row_pen, row_pen, 1.0, BIG, ALU.subtract, ALU.mult))
            dve.sem_inc(setup_done, 1)
            dve.wait_ge(lohi_ps, 1)
            link(dve, nc.vector.tensor_reduce(out=lohi[0:G, 1:2], in_=PS[0:G, 128:256], axis=AX.X, op=ALU.max))
            link(dve, nc.vector.tensor_reduce(out=lohi[0:G, 0:1], in_=PS[0:G, 0:128], axis=AX.X, op=ALU.min))
            dve.sem_inc(lohi_done, 1)
            link(dve, nc.vector.tensor_tensor(out=lohi[0:G, 3:4], in0=lohi[0:G, 1:2], in1=lohi[0:G, 0:1],
                                              op=ALU.subtract))
            link(dve, nc.vector.tensor_scalar(lohi[0:G, 3:4], lohi[0:G, 3:4], float(W), lohi[0:G, 2:3],
                                              ALU.is_ge, ALU.add))
            dve.sem_inc(lohi_done, 1)
            dve.wait_ge(flag_ps, 1)
            link(dve, nc.vector.tensor_scalar(flag_i[:, :], PS[0:1, 1024:1025], 1.0, None, ALU.min))
            dve.sem_inc(flag_ready, 1)
            load_flag(dve)
            dve.wait_ge(base_ps, 1)
            link(dve, nc.vector.tensor_copy(base_i[:, :], PS[0:1, 512:512 + G]))
            link(dve, nc.vector.tensor_tensor(
                out=keyloc[:, 0:T].rearrange("p (g k) -> p g k", k=GT),
                in0=dst_f[:, :].rearrange("p (g k) -> p g k", k=GT),
                in1=PS[:, 512:512 + G].unsqueeze(2).to_broadcast([128, G, GT]), op=ALU.subtract))
            clears = 0
            for m in range(3):
                if m:
                    dve_keep(dve, m - 1)
                extra = DEG if m == 0 else None
                clears += 2 if m == 0 else 1
                h = A if m else X
                either(dve, lambda: dve_sum(dve, m, extra=extra, clears=clears, start=h),
                       lambda: dve_general(dve, m, a["dst_flat"], src_i, extra=extra, start=h))
                if m == 0:
                    link(dve, nc.vector.tensor_scalar(DEG[:, :], DEG[:, :], 1.0, None, ALU.max))
                    link(dve, nc.vector.reciprocal(DEG[:, :], DEG[:, :]))
                dve.sem_inc(lin_src, NBLK)
                dve_stats(dve, 2 * m, 2 * m, B)
                dve_batchnorm(dve, 2 * m, f"L0_g1_{m}", f"L0_be1_{m}")
                if m < 2:
                    dve_stats(dve, 2 * m + 1, 2 * m + 1, B)
                    dve_batchnorm(dve, 2 * m + 1, f"L0_gbn_{m}", f"L0_bbn_{m}")
            dve_norm(dve, 0, B, A, floor=NORM_EPS, dst=B)
            dve_center(dve, 0, B, after=(scaled, 0))
            dve_norm(dve, 1, X, A, rows=2, kept=2 * NBLK)
            with dve.If(flag[dve] == 0):
                dve_scatter(dve)
                dve_readback(dve)
            with dve.Else():
                dve_general(dve, 3, a["src_flat"], dst_f, extra=H)
                nc.vector.tensor_scalar(H[:, :], H[:, :], 1.0, None, ALU.max)
                dve.drain()
                nc.vector.reciprocal(H[:, :], H[:, :])
                dve.drain()
                nc.vector.tensor_tensor(out=A[:, :], in0=A[:, :], in1=H[:, :], op=ALU.mult)
                dve.drain()
                dve.sem_inc(yT_kept, NBLK)
            dve_center(dve, 1, A, after=(lin_taken, 7 * NBLK + 2))
            dve_norm(dve, 2, X, B, rows=3, kept=3 * NBLK)
            clears += 2
            either(dve, lambda: dve_sum(dve, 3, extra=WS, extra_cols=ew, clears=clears),
                   lambda: dve_general(dve, 4, a["dst_flat"], src_i, extra=WS, extra_cols=ew))
            dve_times(dve, A, DEG, ALU.mult, lin_src)
            link(dve, nc.vector.tensor_scalar(WS[:, :], WS[:, :], NORM_EPS, None, ALU.max))
            link(dve, nc.vector.reciprocal(WS[:, :], WS[:, :]))
            dve_stats(dve, 8, 5, B)
            dve_batchnorm(dve, 5, "L2_gamma", "L2_beta")
            dve_times(dve, A, X, ALU.add, lin_src, after=(aff_done, 3 * NBLK))
            dve_center(dve, 2, A, after=(lin_src, 4 * NBLK))
            dve_norm(dve, 3, X, B, rows=4, kept=4 * NBLK)
            clears += 1
            either(dve, lambda: dve_max(dve, MAX_PASS, clears),
                   lambda: dve_general(dve, 5, a["dst_flat"], src_i, scale=ew, maximum=True))
            dve_times(dve, A, WS, ALU.mult, lin_src)
            dve_norm(dve, 4, B, A, floor=NORM_EPS, relu=True, rows=6, kept=5 * NBLK)
            clears += 1
            either(dve, lambda: dve_sum(dve, 5, scale=ew, clears=clears),
                   lambda: dve_general(dve, 6, a["dst_flat"], src_i, scale=ew))
            link(dve, nc.vector.tensor_tensor(out=WS[:, :], in0=WS[:, :], in1=DEG[:, :], op=ALU.mult))
            dve_times(dve, A, WS, ALU.mult, lin_src)
            dve_center(dve, 3, A, after=(lin_taken, 11 * NBLK + 2))
            dve_norm(dve, 5, X, B, rows=7)

        @block.tensor
        def _(pe):
            pe.wait_ge(const_ready, 6)
            pe.wait_ge(loaded, 16 * 10)
            pe.wait_ge(lohi_done, 1)
            nc.tensor.transpose(PS[0:G, 0:128], least, ident[:, :])
            nc.tensor.transpose(PS[0:G, 128:256], most, ident[:, :]).then_inc(lohi_ps, 1)
            pe.wait_ge(lohi_done, 2)
            nc.tensor.matmul(PS[:, 512:512 + G], lohi[0:G, 0:1].to_broadcast([G, 128]), ident[0:G, 0:G],
                             start=True, stop=True).then_inc(base_ps, 1)
            pe.wait_ge(lohi_done, 3)
            nc.tensor.matmul(PS[0:1, 1024:1025], lohi[0:G, 3:4], ones[0:G, 0:1],
                             start=True, stop=True).then_inc(flag_ps, 1)
            load_flag(pe)
            for m in range(3):
                either(pe, lambda: pe_sum(pe, m, extra="degree" if m == 0 else None), lambda: pe_general(pe, m))
                pe_linear(pe, 2 * m, [(f"L0_W1_{m}", A)], after_src=(lin_src, m * NBLK))
                pe_linear(pe, 2 * m + 1, [(f"L0_W2_{m}", A)], after_src=(aff_done, m * NBLK))
                if m < 2:
                    pe_rows(pe, m)
            pe_norm(pe, 0, A, ones)
            pe_center(pe, 0)
            pe_norm(pe, 1, A, mean_m)
            pe_rows(pe, 2)
            with pe.If(flag[pe] == 0):
                pe_scatter(pe)
                pe_readback(pe)
            with pe.Else():
                pe_general(pe, 3)
            pe_linear(pe, 6, [("L1_W1", A)], after_src=(yT_kept, 2))
            pe_linear(pe, 7, [("L1_W2", B)], after_src=(lin_taken, 6 * NBLK + 2))
            pe_center(pe, 1)
            pe_norm(pe, 2, B, mean_m)
            pe_rows(pe, 3)
            either(pe, lambda: pe_sum(pe, 3, extra="weight"), lambda: pe_general(pe, 4))
            pe_linear(pe, 8, [("L2_W_l", A), ("L2_W_r", X)], after_src=(lin_src, 3 * NBLK))
            pe_center(pe, 2)
            pe_norm(pe, 3, B, mean_m)
            pe_rows(pe, 4)
            pe.wait_ge(ss_kept, 5 * NBLK + 2)
            pe_linear_rows(pe, 9, 5, "L3_W_pool", X)
            either(pe, lambda: pe_max(pe, MAX_PASS), lambda: pe_general(pe, 5))
            pe_linear(pe, 10, [("L3_W1_self", X), ("L3_W1_neigh", A)], after_src=(lin_src, 5 * NBLK))
            pe_norm(pe, 4, A, ones)
            pe_rows(pe, 6)
            either(pe, lambda: pe_sum(pe, 5), lambda: pe_general(pe, 6))
            pe_linear(pe, 11, [("L3_W2_self", B), ("L3_W2_neigh", A)], after_src=(lin_src, 6 * NBLK))
            pe_center(pe, 3)
            pe_norm(pe, 5, B, mean_m)
            pe_rows(pe, 7)


WEIGHTS = {
    **{f"L0_W1_{m}": ("L0_gnn_W1", m, False) for m in range(3)},
    **{f"L0_W2_{m}": ("L0_gnn_W2", m, False) for m in range(3)},
    "L1_W1": ("L1_gnn_W1", None, True), "L1_W2": ("L1_gnn_W2", None, True),
    "L2_W_l": ("L2_gnn_W_l", None, True), "L2_W_r": ("L2_gnn_W_r", None, True),
    "L3_W_pool": ("L3_gnn_W_pool", None, False),
    "L3_W1_self": ("L3_gnn_W1_self", None, False), "L3_W1_neigh": ("L3_gnn_W1_neigh", None, False),
    "L3_W2_self": ("L3_gnn_W2_self", None, False), "L3_W2_neigh": ("L3_gnn_W2_neigh", None, False),
}
VECTORS = {
    **{f"L0_{v}_{m}": (f"L0_gnn_{v}", m) for v in ("b1", "g1", "be1", "b2") for m in range(3)},
    **{f"L0_{v}_{m}": (f"L0_gnn_{v}", m) for v in ("gbn", "bbn") for m in range(2)},
    "L1_b1": ("L1_gnn_b1", None), "L1_b2": ("L1_gnn_b2", None),
    "L2_b_l": ("L2_gnn_b_l", None), "L2_gamma": ("L2_gnn_gamma", None), "L2_beta": ("L2_gnn_beta", None),
    "L3_b_pool": ("L3_gnn_b_pool", None), "L3_b1": ("L3_gnn_b1", None), "L3_b2": ("L3_gnn_b2", None),
}


def kernel(**inputs):
    import concourse.bacc as bacc
    from concourse.bass_utils import run_bass_kernel_spmd

    def edges(x, tiles, pad):
        flat = np.full(tiles * 128, pad, x.dtype)
        flat[:x.size] = x
        return np.ascontiguousarray(flat.reshape(tiles, 128).T)

    x, dst = np.asarray(inputs["x"]), np.asarray(inputs["dst"])
    padded = np.full(EP + 2, N, dst.dtype)
    padded[0], padded[-1] = -1, -1
    padded[1:E + 1] = dst
    pick = lambda name, m: np.asarray(inputs[name]) if m is None else np.asarray(inputs[name])[m]
    arrays = {
        "x": x,
        "x_t": np.ascontiguousarray(x.T),
        "src_t": edges(np.asarray(inputs["src"]), T + 2 * GT, 0),
        "src_key_t": edges(np.asarray(inputs["src"]), T + 2 * GT, N),
        "src_flat": edges(np.asarray(inputs["src"]), T, N).T.reshape(1, EP).copy(),
        "dst_flat": padded[1:-1].reshape(1, EP).copy(),
        "ew_t": edges(np.asarray(inputs["edge_weight"]), T + GT, 0),
        "dst_t": edges(padded[1:-1], T, N),
        "dst_next_t": edges(padded[2:], T, N),
        "dst_rows": np.ascontiguousarray(padded[1:-1].reshape(G, GE)),
        "dst_prev_rows": np.ascontiguousarray(padded[:-2].reshape(G, GE)),
        "weights": np.ascontiguousarray(np.stack(
            [pick(n, m).T if t else pick(n, m) for n, m, t in WEIGHTS.values()], axis=1)),
        "vectors": np.ascontiguousarray(np.stack([pick(n, m) for n, m in VECTORS.values()], axis=1)),
    }
    nc = bacc.Bacc("TRN2", target_bir_lowering=False, num_devices=1)
    handles = {n: nc.dram_tensor(f"in_{n}", v.shape, mybir.dt.from_np(v.dtype), kind="ExternalInput").ap()
               for n, v in arrays.items()}
    out = nc.dram_tensor("out", (N, D), mybir.dt.float32, kind="ExternalOutput").ap()
    build_program(nc, handles, out)
    return run_bass_kernel_spmd(nc, [{f"in_{n}": v for n, v in arrays.items()}], core_ids=[0]).results[0]["out"]
```

```python
import numpy as np
from contextlib import ExitStack
import concourse.bass as bass
from concourse import mybir

N = 6250
E = 106250
D = 128
GT = 8
G = 2 * -(-E // (2 * 128 * GT))
T = G * GT
EP = T * 128
GE = GT * 128
W = 128
NCOPY = 4
NR = N + 150
BLK = 625
NBLK = N // BLK
TN = 125
TPB = BLK // TN
YW = D + 1
BIG = 3.0e38
CHUNK = -(-N // (G // 2))
MAX_PASS = 4
BN_EPS = 1e-5
NORM_EPS = 1e-12


def build_program(nc, a, out):
    F32, I32, BF16 = mybir.dt.float32, mybir.dt.int32, mybir.dt.bfloat16
    ALU, ACT, AX = mybir.AluOpType, mybir.ActivationFunctionType, mybir.AxisListType
    ctx = ExitStack()
    with ctx:
        def sb(name, shape, dt=F32):
            return ctx.enter_context(nc.sbuf_tensor(name, shape, dt))

        def sem(name):
            return ctx.enter_context(nc.semaphore(name))

        table = nc.dram_tensor("table", [NR, D], F32).ap()
        ysum = [nc.dram_tensor(f"ysum{k}", [NR, YW], F32).ap() for k in range(NCOPY)]
        start_penalty = nc.dram_tensor("start_penalty", [G, GE], F32).ap()

        X = sb("X", [128, N])
        H = sb("H", [128, N + W])
        A = sb("A", [128, N + W])
        B = sb("B", [128, N])
        DEG = sb("DEG", [128, N + W])
        WS = H
        gbuf = [sb(f"gbuf{b}", [128, GT, D]) for b in range(2)]
        sel = [sb(f"sel{b}", [128, GT, W]) for b in range(2)]
        SS = [sb(f"SS{b}", [128, BLK]) for b in range(2)]
        ST = [sb(f"ST{b}", [128, TPB, D]) for b in range(2)]
        src_i = sb("src_i", [128, T + 2 * GT], I32)
        dst_f = sb("dst_f", [128, T])
        src_f = sb("src_f", [128, T + 2 * GT])
        flag_i = sb("flag_i", [1, 1], I32)
        keyloc = sb("keyloc", [128, T + GT])
        ew = sb("ew", [128, T + GT])
        is_end = sb("is_end", [128, T + GT])
        idx_slot = [sb(f"idx_slot{b}", [128, GT], I32) for b in range(2)]
        col_slot = [sb(f"col_slot{b}", [128, GT]) for b in range(2)]
        ident = sb("ident", [128, 128])
        iota = sb("iota", [128, W])
        ones = sb("ones", [128, 128])
        base_i = sb("base_i", [1, G], I32)
        lohi = sb("lohi", [128, 4])
        eps_bn = sb("eps_bn", [128, 1])
        zero_c = sb("zero_c", [128, 1])
        stats = sb("stats", [128, 2 * NBLK, 6])
        mv = sb("mv", [128, 2])
        row_stats = sb("row_stats", [128, 2, TPB, 6])
        row_mv = sb("row_mv", [128, 2, TPB, 2])
        row_sd = sb("row_sd", [128, 2, TPB])
        cf = sb("cf", [128, 5])
        wnames = list(WEIGHTS)
        weights = sb("weights", [128, len(wnames), 128])
        vnames = list(VECTORS)
        vectors = sb("vectors", [128, len(vnames)])
        wt = {n: weights[:, i, :] for i, n in enumerate(wnames)}
        vec = {n: vectors[:, i:i + 1] for i, n in enumerate(vnames)}
        scan = [B[:, b * GE:(b + 1) * GE] for b in range(2)]
        pen = [B[:, (2 + b) * GE:(3 + b) * GE] for b in range(2)]
        scan_rows_flat = B[:, 4 * GE:5 * GE]
        scan_rows = scan_rows_flat.rearrange("p (k f) -> p k f", k=GT)
        diag = B[:, 5 * GE:6 * GE].rearrange("p (k e) -> p k e", k=GT)
        same = A[:, 0:GE // 2].bitcast(BF16).rearrange("p (k e) -> p k e", k=GT)
        onehot = [A[:, (1 + b) * GE // 2:(2 + b) * GE // 2].bitcast(BF16).rearrange("p (k e) -> p k e", k=GT)
                  for b in range(2)]
        before = B[:, 0:GE].rearrange("p (k e) -> p k e", k=GT)
        earlier = sb("earlier", [128, 128])
        mcount = B[:, 2 * GE:3 * GE].rearrange("p (k e) -> p k e", k=GT)
        rank = B[:, 3 * GE:3 * GE + GT]
        to_row = B[:, 3 * GE + 16:3 * GE + 16 + GT]
        trash = sb("trash", [128, 1])
        xwin = [B[:, 3 * GE + 64 + 132 * b:3 * GE + 64 + 132 * b + YW] for b in range(2)]
        summed_rows = [A[:, 3 * GE // 2 + b * GT * YW:3 * GE // 2 + (b + 1) * GT * YW]
                       .rearrange("p (k f) -> p k f", k=GT) for b in range(2)]
        dst_i = B[:, 0:T].bitcast(I32)
        next_i = B[:, T:2 * T].bitcast(I32)
        next_f = B[:, 2 * T:3 * T]
        least = B[:, 3 * T:3 * T + G]
        row_i = A[0:G, 0:GE].bitcast(I32)
        prev_i = A[0:G, GE:2 * GE].bitcast(I32)
        row_pen = B[0:G, 3 * T + 2 * G:3 * T + 2 * G + GE]
        most = B[:, 3 * T + G:3 * T + 2 * G]
        key_i = DEG[:, 0:T + 2 * GT].bitcast(I32)
        parts = [[B, H][b][0:TN, 0:NCOPY * TPB * YW] for b in range(2)]
        ytot = [gbuf[b][0:TN, :, :].rearrange("p k f -> p (k f)")[:, 0:TPB * YW] for b in range(2)]
        ydeg = sb("ydeg", [128, 2, TPB])
        yrow = ST

        PS = ctx.enter_context(nc.psum_tensor("PS", [128, 4096], F32))
        blk_ps = [PS[:, 1024 * b:1024 * b + BLK] for b in range(2)]
        row_ps = [PS[:, 2048 + 1024 * b:2048 + 1024 * b + TPB * 128] for b in range(2)]
        back_ps = [PS[:, 1024 * b:1024 * b + TPB * 128].rearrange("p (j n) -> p j n", j=TPB)[:, :, 0:TN]
                   for b in range(2)]
        agg_ps = [PS[:, 512 * b:512 * b + W] for b in range(2)]
        extra_ps = [PS[:, 1024 + 512 * b:1024 + 512 * b + W] for b in range(2)]
        msg_ps = [PS[:, 1024:2048], PS[:, 3072:4096]]
        rev_ps = PS[:, 2048:3072]
        keyrow_ps = PS[:, 0:1024]
        m_ps = PS[:, 1024:2048]
        v_ps = PS[:, 2048:4096].rearrange("p (k f) -> p k f", k=GT)

        loaded = sem("loaded")
        dve_chain = sem("dve_chain")
        const_ready = sem("const_ready")
        lohi_ps = sem("lohi_ps")
        lohi_done = sem("lohi_done")
        base_ps = sem("base_ps")
        setup_done = sem("setup_done")
        flag_ps = sem("flag_ps")
        flag_ready = sem("flag_ready")
        general_slots = sem("general_slots")
        general_full = sem("general_full")
        general_used = sem("general_used")
        pen_out = sem("pen_out")
        ysum_zeroed = sem("ysum_zeroed")
        idx_ready = sem("idx_ready")
        gathered = [sem(f"gathered{b}") for b in range(2)]
        sel_ready = sem("sel_ready")
        summed = sem("summed")
        floored = sem("floored")
        placed = sem("placed")
        pass_clear = sem("pass_clear")
        msg_full = sem("msg_full")
        pen_in = [sem(f"pen_in{b}") for b in range(2)]
        diag_ready = sem("diag_ready")
        scanned = sem("scanned")
        rev_full = sem("rev_full")
        rev_kept = sem("rev_kept")
        lin_src = sem("lin_src")
        lin_full = sem("lin_full")
        lin_taken = sem("lin_taken")
        aff_done = sem("aff_done")
        stats_done = sem("stats_done")
        bn_var = sem("bn_var")
        bn_sd = sem("bn_sd")
        bn_coef = sem("bn_coef")
        ss_ready = sem("ss_ready")
        ss_kept = sem("ss_kept")
        rows_full = sem("rows_full")
        rows_staged = sem("rows_staged")
        rows_out = [sem(f"rows_out{b}") for b in range(2)]
        row_measured = sem("row_measured")
        row_var = sem("row_var")
        row_rooted = sem("row_rooted")
        row_inverse = sem("row_inverse")
        row_chain = sem("row_chain")
        back_full = sem("back_full")
        sq_ready = sem("sq_ready")
        norm_full = sem("norm_full")
        unit_chain = sem("unit_chain")
        sd_ready = sem("sd_ready")
        scaled = sem("scaled")
        kr_full = sem("kr_full")
        same_ready = sem("same_ready")
        m_full = sem("m_full")
        m_kept = sem("m_kept")
        v_full = sem("v_full")
        v_kept = sem("v_kept")
        xwin_in = [sem(f"xwin_in{b}") for b in range(2)]
        xwin_ones = sem("xwin_ones")
        row_idx = sem("row_idx")
        col_ready = sem("col_ready")
        hot_ready = sem("hot_ready")
        rank_chain = sem("rank_chain")
        scattered = [sem(f"scattered{k}") for k in range(NCOPY)]
        parts_in = [sem(f"parts_in{b}") for b in range(2)]
        parts_used = sem("parts_used")
        y_chain = sem("y_chain")
        yT_full = sem("yT_full")
        yT_kept = sem("yT_kept")

        tick = sb("tick", [128, 4])
        block = ctx.enter_context(nc.Block())

        def cols(i, b):
            return bass.ds(i * (2 * BLK) + b * BLK, BLK)

        def tiles(i, b, ahead=0):
            return bass.ds(i * (2 * GT) + (b + ahead) * GT, GT)

        def bc(col, n):
            return col.to_broadcast([128, n])

        def rows_written(eng, n):
            for b in range(2):
                eng.wait_ge(rows_out[b], 16 * (NBLK // 2) * n)

        def pool_gather(pool, q, source):
            group = pool.alloc_register(f"gather_group{q}")
            pool.reg_mov(group, 1)
            with pool.Fori(0, G // 2) as i:
                for b in range(2):
                    g = pool.snap(group, min_val=1, max_val=G)
                    if q == MAX_PASS:
                        pool.wait_ge(msg_full, g)
                    else:
                        pool.wait_ge(summed, g + q * G)
                    pool.wait_ge(idx_ready, g + q * (G + 2))
                    pool.reg_add(group, group, 1)
                    for k in range(GT):
                        nc.gpsimd.indirect_dma_start(
                            out=gbuf[b][:, k, :], out_offset=None, in_=source,
                            in_offset=bass.IndirectOffsetOnAxis(ap=idx_slot[b][:, k:k + 1], axis=0),
                        ).then_inc(gathered[b], 16)

        def q_sel(q):
            return q * (G + 1) - (1 if q > MAX_PASS else 0)

        def gathered_value(q, i):
            return i * (16 * GT) + 16 * GT * (1 + q * (G // 2))

        def pe_sum(pe, q, extra=None):
            with pe.Fori(0, G // 2) as i:
                for b in range(2):
                    pe.wait_ge(gathered[b], gathered_value(q, i))
                    pe.wait_ge(sel_ready, q_sel(q) + i * 2 + (b + 1))
                    pe.wait_ge(placed, q * G + i * 2 + (b + 1))
                    for k in range(GT):
                        last = nc.tensor.matmul(agg_ps[b], gbuf[b][:, k, :], sel[b][:, k, :],
                                                start=(k == 0), stop=(k == GT - 1))
                    if extra is not None:
                        for k in range(GT):
                            left = ones[:, :] if extra == "degree" else bc(col_slot[b][:, k:k + 1], 128)
                            last = nc.tensor.matmul(extra_ps[b], left, sel[b][:, k, :],
                                                    start=(k == 0), stop=(k == GT - 1))
                    last.then_inc(summed, 1)
            pe.wait_ge(placed, G * (q + 1) + 2)

        def pe_max(pe, q):
            def weigh(i, b):
                pe.wait_ge(gathered[b], gathered_value(q, i))
                pe.wait_ge(diag_ready, i * 2 + (b + 1))
                pe.wait_ge(scanned, i * 2 + (b + 1))
                for k in range(GT):
                    last = nc.tensor.matmul(msg_ps[b][:, k * 128:(k + 1) * 128], gbuf[b][:, k, :],
                                            diag[:, k, :], start=True, stop=True)
                last.then_inc(msg_full, 1)

            def ends(i, b):
                pe.wait_ge(scanned, i * 2 + (b + 3))
                pe.wait_ge(rev_kept, i * 2 + (b + 1))
                for k in range(GT):
                    last = nc.tensor.transpose(rev_ps[:, k * 128:(k + 1) * 128],
                                               scan[b][:, k * 128:(k + 1) * 128], ident[:, :])
                last.then_inc(rev_full, 1)
                pe.wait_ge(rev_kept, i * 2 + (b + 2))
                pe.wait_ge(sel_ready, q_sel(q) + i * 2 + (b + 1))
                pe.wait_ge(placed, q * G + i * 2 + (b + 1))
                for k in range(GT):
                    last = nc.tensor.matmul(agg_ps[b], scan_rows[:, k, :], sel[b][:, k, :],
                                            start=(k == 0), stop=(k == GT - 1))
                last.then_inc(summed, 1)

            weigh(0, 0)
            with pe.Fori(0, G // 2 - 1) as i:
                weigh(i, 1)
                ends(i, 0)
                weigh(i + 1, 0)
                ends(i, 1)
            weigh(G // 2 - 1, 1)
            ends(G // 2 - 1, 0)
            ends(G // 2 - 1, 1)
            pe.wait_ge(placed, G * (q + 1) + 2)

        def act_max(act):
            def diagonals(i, b):
                act.wait_ge(msg_full, i * 2 + (b + 2))
                for k in range(GT):
                    last = nc.scalar.activation(diag[:, k, :], ident[:, :], ACT.Copy,
                                                scale=ew[:, bass.ds(i * (2 * GT) + (b * GT + k), 1)])
                last.then_inc(diag_ready, 1)

            def keep(i, b):
                act.wait_ge(rev_full, i * 2 + (b + 1))
                act.wait_ge(summed, MAX_PASS * G + i * 2 + (b + 2))
                nc.scalar.activation(scan_rows_flat, rev_ps, ACT.Copy).then_inc(rev_kept, 1)

            diagonals(0, 0)
            with act.Fori(0, G // 2 - 1) as i:
                diagonals(i, 1)
                keep(i, 0)
                diagonals(i + 1, 0)
                keep(i, 1)
            diagonals(G // 2 - 1, 1)
            keep(G // 2 - 1, 0)
            keep(G // 2 - 1, 1)

        def invert(dve, array, floor, n, i=None):
            part = array[:, :] if i is None else array[:, bass.ds(i * CHUNK, CHUNK)]
            ins = nc.vector.tensor_scalar(part, part, floor, None, ALU.max)
            if i is None:
                dve.drain()
            else:
                ins.then_inc(floored, 1)
                dve.wait_ge(floored, n * (G // 2) + i + 1)
                nc.vector.tensor_copy(tick[:, 3:4], tick[:, 2:3])
            nc.vector.reciprocal(part, part)
            if i is None:
                dve.drain()

        def times_degree(dve, i=None):
            at = slice(0, N) if i is None else bass.ds(i * CHUNK, CHUNK)
            nc.vector.tensor_tensor(out=WS[:, at], in0=WS[:, at], in1=DEG[:, at], op=ALU.mult)
            if i is None:
                dve.drain()

        def dve_max(dve, q, clears, beside):
            fill_first(dve)
            dve_clear(dve)
            dve.wait_ge(pass_clear, clears)
            with dve.Fori(0, G // 2) as i:
                for b in range(2):
                    base = dve.value_load(base_i[0:1, bass.ds(i * 2 + b, 1)], min_val=0, max_val=N)
                    at = lambda k, n: bass.ds(i * (2 * GT) + (b * GT + k), n)
                    dve.wait_ge(msg_full, i * 2 + (b + 3))
                    dve.wait_ge(pen_in[b], i * 16 + 16)
                    dve.wait_ge(scanned, i * 2 + (b + 2))
                    nc.vector.tensor_tensor_scan(scan[b], pen[b], msg_ps[b], scan[1 - b][:, GE - 1:GE],
                                                 ALU.add, ALU.max).then_inc(scanned, 1)
                    fill_slots(dve, i, b, 2)
                    build_sel(dve, sel[b], at, is_end).then_inc(sel_ready, 1)
                    dve.wait_ge(summed, q * G + i * 2 + (b + 3))
                    dve.wait_ge(placed, q * G + i * 2 + (b + 2))
                    nc.vector.tensor_tensor(out=A[:, bass.ds(base, W)], in0=A[:, bass.ds(base, W)],
                                            in1=agg_ps[b], op=ALU.add).then_inc(placed, 1)
                    if b == 0:
                        beside(i)
            dve.wait_ge(placed, 2 + G * (q + 1))

        def sp_max(sp):
            with sp.Fori(0, G // 2) as i:
                for b in range(2):
                    sp.wait_ge(scanned, i * 2 + (b + 1))
                    sp.dma_start(pen[b], start_penalty[bass.ds(i * 2 + b, 1), :].to_broadcast([128, GE])
                                 ).then_inc(pen_in[b], 16)

        def dve_clear(dve, extra=None, start=None):
            if start is None:
                nc.vector.memset(A[:, :], 0.0).then_inc(pass_clear, 1)
            else:
                if start is not A:
                    nc.vector.tensor_copy(A[:, 0:N], start[:, 0:N])
                nc.vector.memset(A[:, N:N + W], 0.0).then_inc(pass_clear, 1)
            if extra is not None:
                nc.vector.memset(extra[:, :], 0.0).then_inc(pass_clear, 1)

        def fill_slots(dve, i, b, ahead):
            nc.vector.tensor_copy(idx_slot[b][:, :], src_i[:, tiles(i, b, ahead)]).then_inc(idx_ready, 1)

        def fill_first(dve):
            for b in range(2):
                nc.vector.tensor_copy(idx_slot[b][:, :], src_i[:, b * GT:(b + 1) * GT]).then_inc(idx_ready, 1)

        def build_sel(dve, where, at, scale=None):
            if scale is None:
                return nc.vector.tensor_tensor(
                    out=where[:, :, :], in0=iota[:, :].unsqueeze(1).to_broadcast([128, GT, W]),
                    in1=keyloc[:, at(0, GT)].unsqueeze(2).to_broadcast([128, GT, W]), op=ALU.is_equal)
            for k in range(GT):
                last = nc.vector.tensor_scalar(where[:, k, :], iota[:, :], keyloc[:, at(k, 1)],
                                               scale[:, at(k, 1)], ALU.is_equal, ALU.mult)
            return last

        def dve_sum(dve, q, extra=None, scale=None, extra_cols=None, clears=0, start=None, beside=None):
            def one_group(i, b, ahead):
                g = b + ahead
                at = lambda k, n: bass.ds(i * (2 * GT) + (g * GT + k), n)
                if extra_cols is not None:
                    nc.vector.tensor_copy(col_slot[g % 2][:, :], extra_cols[:, at(0, GT)])
                build_sel(dve, sel[g % 2], at, scale).then_inc(sel_ready, 1)
            fill_first(dve)
            dve_clear(dve, extra, start)
            one_group(0, 0, 0)
            dve.wait_ge(pass_clear, clears)
            with dve.Fori(0, G // 2) as i:
                for b in range(2):
                    base = dve.value_load(base_i[0:1, bass.ds(i * 2 + b, 1)], min_val=0, max_val=N)
                    one_group(i, b, 1)
                    dve.wait_ge(summed, q * G + i * 2 + (b + 3))
                    fill_slots(dve, i, b, 2)
                    dve.wait_ge(placed, q * G + i * 2 + (b + 2))
                    last = nc.vector.tensor_tensor(out=A[:, bass.ds(base, W)], in0=A[:, bass.ds(base, W)],
                                                   in1=agg_ps[b], op=ALU.add)
                    if extra is not None:
                        last = nc.vector.tensor_tensor(out=extra[:, bass.ds(base, W)],
                                                       in0=extra[:, bass.ds(base, W)],
                                                       in1=extra_ps[b], op=ALU.add)
                    last.then_inc(placed, 1)
                    if beside is not None and b == 0:
                        beside(i)
            dve.wait_ge(placed, 2 + G * (q + 1))

        def block_matmul(ps, left, src, i, b, start, stop):
            nc.tensor.matmul(ps[:, 0:512], left, src[:, bass.ds(i * (2 * BLK) + b * BLK, 512)],
                             start=start, stop=stop)
            return nc.tensor.matmul(ps[:, 512:BLK], left,
                                    src[:, bass.ds(i * (2 * BLK) + (b * BLK + 512), BLK - 512)],
                                    start=start, stop=stop)

        def pe_linear(pe, n, terms, after_src=None, free=None):
            with pe.Fori(0, NBLK // 2) as i:
                for b in range(2):
                    if after_src is not None:
                        pe.wait_ge(after_src[0], after_src[1] + i * 2 + (b + 1))
                    if free is not None:
                        pe.wait_ge(free[0], free[1])
                    pe.wait_ge(lin_taken, NBLK * n + i * 2 + (b + 1))
                    for j, (w, src) in enumerate(terms):
                        last = block_matmul(blk_ps[b], wt[w], src, i, b, j == 0, j == len(terms) - 1)
                    last.then_inc(lin_full, 1)
            pe.wait_ge(lin_taken, NBLK * (n + 1) + 2)

        def act_linear(act, n, func, bias, dst):
            with act.Fori(0, NBLK // 2) as i:
                for b in range(2):
                    act.wait_ge(lin_full, NBLK * n + i * 2 + (b + 1))
                    nc.scalar.activation(dst[:, cols(i, b)], blk_ps[b], func, bias=vec[bias]).then_inc(lin_taken, 1)

        def in_pairs(eng, block_of, row_of):
            block_of(0, 0)
            block_of(0, 1)
            row_of(0, 0)
            block_of(1, 0)
            row_of(0, 1)
            with eng.Fori(1, NBLK // 2 - 1) as i:
                block_of(i, 1)
                row_of(i, 0)
                block_of(i + 1, 0)
                row_of(i, 1)
            block_of(NBLK // 2 - 1, 1)
            row_of(NBLK // 2 - 1, 0)
            row_of(NBLK // 2 - 1, 1)

        def act_linear_rows(act, n, r, func, bias):
            def block_of(i, b):
                act.wait_ge(lin_full, NBLK * n + i * 2 + (b + 1))
                act.wait_ge(rows_full, NBLK * r + i * 2 + (b + 1))
                nc.scalar.activation(SS[b][:, :], blk_ps[b], func, bias=vec[bias]).then_inc(ss_ready, 1)
            in_pairs(act, block_of, lambda i, b: act_row(act, r, i, b))
            act.sem_inc(lin_taken, NBLK)

        def pe_linear_rows(pe, n, r, w, src):
            def block_of(i, b):
                pe.wait_ge(ss_ready, NBLK * r - 1 + i * 2 + b)
                block_matmul(blk_ps[b], wt[w], src, i, b, True, True).then_inc(lin_full, 1)

            def row_of(i, b):
                pe_row(pe, r, i, b)

            in_pairs(pe, block_of, row_of)
            pe.wait_ge(rows_staged, NBLK * (r + 1) + 2)

        def act_affine(act, m, src, dst=None, ss=None):
            act.wait_ge(bn_coef, m + 1)
            if ss is None:
                with act.Fori(0, NBLK // 2) as i:
                    for b in range(2):
                        nc.scalar.activation(dst[:, cols(i, b)], src[:, cols(i, b)], ACT.Relu, bias=cf[:, 4:5],
                                             scale=cf[:, 3:4]).then_inc(aff_done, 1)
                return

            def block_of(i, b):
                act.wait_ge(rows_full, NBLK * ss + i * 2 + (b + 1))
                act.wait_ge(ss_kept, NBLK * ss + i * 2 + (b + 1))
                nc.scalar.activation(SS[b][:, :], src[:, cols(i, b)], ACT.Relu, bias=cf[:, 4:5],
                                     scale=cf[:, 3:4]).then_inc(ss_ready, 1)
            in_pairs(act, block_of, lambda i, b: act_row(act, ss, i, b))

        def dve_stats(dve, n, s, src):
            with dve.Fori(0, NBLK // 2) as i:
                for b in range(2):
                    dve.wait_ge(lin_taken, NBLK * n + i * 2 + (b + 3))
                    for h, (lo, w) in enumerate(((0, 313), (313, 312))):
                        nc.vector.bn_stats(stats[:, bass.ds(i * 4 + (2 * b + h), 1), :].rearrange("p a s -> p (a s)"),
                                           src[:, bass.ds(i * (2 * BLK) + (b * BLK + lo), w)]
                                           ).then_inc(stats_done, 1)

        def dve_batchnorm(dve, m, gamma, beta):
            dve.wait_ge(stats_done, 2 * NBLK * (m + 1))
            nc.vector.bn_aggr(mv[:, :], stats[:, :, :].rearrange("p a s -> p (a s)")).then_inc(bn_var, 1)
            dve.wait_ge(bn_sd, m + 1)
            link(dve, nc.vector.reciprocal(cf[:, 1:2], cf[:, 0:1]))
            link(dve, nc.vector.tensor_tensor(out=cf[:, 3:4], in0=cf[:, 1:2], in1=vec[gamma], op=ALU.mult))
            link(dve, nc.vector.tensor_tensor(out=cf[:, 2:3], in0=cf[:, 3:4], in1=mv[:, 0:1], op=ALU.mult))
            nc.vector.tensor_tensor(out=cf[:, 4:5], in0=vec[beta], in1=cf[:, 2:3],
                                    op=ALU.subtract).then_inc(bn_coef, 1)

        def act_batchnorm(act, m):
            act.wait_ge(bn_var, m + 1)
            nc.scalar.activation(cf[:, 0:1], mv[:, 1:2], ACT.Sqrt, bias=eps_bn[:, :]).then_inc(bn_sd, 1)

        def pe_row(pe, r, i, b):
            pe.wait_ge(ss_ready, NBLK * r + i * 2 + (b + 1))
            pe.wait_ge(rows_staged, NBLK * r + i * 2 + (b + 1))
            for j in range(TPB):
                last = nc.tensor.transpose(row_ps[b][0:TN, j * 128:(j + 1) * 128],
                                           SS[b][:, j * TN:(j + 1) * TN], ident[:, :])
            last.then_inc(rows_full, 1)

        def pe_rows(pe, r):
            with pe.Fori(0, NBLK // 2) as i:
                for b in range(2):
                    pe_row(pe, r, i, b)
            pe.wait_ge(rows_staged, NBLK * (r + 1) + 2)

        def act_row(act, r, i, b):
            act.wait_ge(rows_full, NBLK * r + i * 2 + (b + 3))
            if r or not isinstance(i, int) or i:
                act.wait_ge(rows_out[b], 16 * (NBLK // 2) * r + i * 16)
            nc.scalar.activation(ST[b][0:TN, :, :], row_ps[b][0:TN, :].rearrange("p (j f) -> p j f", j=TPB),
                                 ACT.Copy).then_inc(rows_staged, 1)

        def sp_rows(sp, r, where):
            with sp.Fori(0, NBLK // 2) as i:
                for b in range(2):
                    sp.wait_ge(rows_staged, NBLK * r + i * 2 + (b + 3))
                    sp.dma_start(where[cols(i, b), :].rearrange("(j p) f -> p j f", p=TN),
                                 ST[b][0:TN, :, :]).then_inc(rows_out[b], 16)

        def dve_rownorm(dve, k, r, term, after, twice=False, by_length=False):
            def add(i, b):
                dve.wait_ge(after[0], after[1] + i * 2 + (b + 1))
                dve.wait_ge(rows_full, NBLK * r + i * 2 + (b + 1))
                if by_length:
                    ins = nc.vector.tensor_copy(SS[b][:, :], term[:, cols(i, b)])
                elif twice:
                    ins = nc.vector.scalar_tensor_tensor(out=SS[b][:, :], in0=X[:, cols(i, b)], scalar=2.0,
                                                         in1=term[:, cols(i, b)], op0=ALU.mult, op1=ALU.add)
                else:
                    ins = nc.vector.tensor_tensor(out=SS[b][:, :], in0=X[:, cols(i, b)],
                                                  in1=term[:, cols(i, b)], op=ALU.add)
                ins.then_inc(ss_ready, 1)

            def normalize(i, b):
                dve.wait_ge(rows_full, NBLK * r + i * 2 + (b + 3))
                for j in range(TPB):
                    last = nc.vector.bn_stats(row_stats[0:TN, b, j, :], row_ps[b][0:TN, j * 128:(j + 1) * 128])
                last.then_inc(row_measured, 1)
                dve.wait_ge(row_measured, NBLK * k + i * 2 + (b + 1))
                nc.vector.tensor_copy(tick[:, 3:4], tick[:, 2:3])
                for j in range(TPB):
                    last = nc.vector.bn_aggr(row_mv[0:TN, b, j, :], row_stats[0:TN, b, j, :])
                if by_length:
                    mean, var = row_mv[0:TN, b, :, 0], row_mv[0:TN, b, :, 1]
                    last.then_inc(row_chain, 1)
                    dve.wait_ge(row_chain, i * 6 + (3 * b + 1))
                    nc.vector.tensor_tensor(out=mean, in0=mean, in1=mean, op=ALU.mult).then_inc(row_chain, 1)
                    dve.wait_ge(row_chain, i * 6 + (3 * b + 2))
                    last = nc.vector.tensor_tensor(out=var, in0=var, in1=mean, op=ALU.add)
                last.then_inc(row_var, 1)
                dve.wait_ge(row_rooted, NBLK * k + i * 2 + (b + 1))
                nc.vector.tensor_copy(tick[:, 3:4], tick[:, 2:3])
                if by_length:
                    nc.vector.tensor_scalar(row_sd[0:TN, b, :], row_sd[0:TN, b, :], NORM_EPS, None,
                                            ALU.max).then_inc(row_chain, 1)
                    dve.wait_ge(row_chain, i * 6 + (3 * b + 3))
                    nc.vector.tensor_copy(tick[:, 3:4], tick[:, 2:3])
                nc.vector.reciprocal(row_sd[0:TN, b, :], row_sd[0:TN, b, :]).then_inc(row_inverse, 1)
                dve.wait_ge(row_inverse, NBLK * k + i * 2 + (b + 1))
                dve.wait_ge(rows_out[b], 16 * (NBLK // 2) * r + i * 16)
                if r < 7:
                    dve.wait_ge(back_full, NBLK * k + i * 2 + (b + 1))
                for j in range(TPB):
                    row = row_ps[b][0:TN, j * 128:(j + 1) * 128]
                    if by_length:
                        last = nc.vector.tensor_scalar(ST[b][0:TN, j, :], row, row_sd[0:TN, b, j:j + 1], 0.0,
                                                       ALU.mult, ALU.max)
                    else:
                        last = nc.vector.tensor_scalar(ST[b][0:TN, j, :], row, row_mv[0:TN, b, j, 0:1],
                                                       row_sd[0:TN, b, j:j + 1], ALU.subtract, ALU.mult)
                last.then_inc(rows_staged, 1)
            in_pairs(dve, add, normalize)

        def act_rownorm(act, k, r, into=None, by_length=False):
            def root(i, b):
                act.wait_ge(row_var, NBLK * k + i * 2 + (b + 1))
                nc.scalar.activation(row_sd[0:TN, b, :], row_mv[0:TN, b, :, 1], ACT.Sqrt,
                                     bias=zero_c[0:TN, :] if by_length else eps_bn[0:TN, :],
                                     scale=float(D) if by_length else 1.0).then_inc(row_rooted, 1)

            def keep(i, b):
                act.wait_ge(back_full, NBLK * k + i * 2 + (b + 3))
                nc.scalar.activation(into[:, cols(i, b)].rearrange("p (j n) -> p j n", j=TPB), back_ps[b],
                                     ACT.Copy).then_inc(ss_kept, 1)
            in_pairs(act, root, keep if r < 7 else lambda i, b: None)

        def pe_rownorm(pe, k, r, kept=0):
            def back(i, b):
                pe.wait_ge(rows_staged, NBLK * r + i * 2 + (b + 3))
                pe.wait_ge(ss_kept, NBLK * kept + i * 2 + (b + 1))
                for j in range(TPB):
                    last = nc.tensor.transpose(back_ps[b][:, j, :], ST[b][0:TN, j, :], ident[0:TN, 0:TN])
                last.then_inc(back_full, 1)
            in_pairs(pe, lambda i, b: pe_row(pe, r, i, b), back if r < 7 else lambda i, b: None)
            if r < 7:
                pe.wait_ge(ss_kept, NBLK * (kept + 1) + 2)

        def act_squares(act):
            with act.Fori(0, NBLK // 2) as i:
                for b in range(2):
                    act.wait_ge(lin_taken, 5 * NBLK + i * 2 + (b + 3))
                    nc.scalar.activation(A[:, cols(i, b)], B[:, cols(i, b)], ACT.Square).then_inc(sq_ready, 1)
            with act.Fori(0, NBLK // 2) as i:
                for b in range(2):
                    act.wait_ge(norm_full, i * 2 + (b + 1))
                    act.wait_ge(scaled, i * 2 + (b + 1))
                    nc.scalar.activation(SS[b][:, :], blk_ps[b], ACT.Sqrt, bias=zero_c[:, :]).then_inc(sd_ready, 1)

        def pe_squares(pe):
            with pe.Fori(0, NBLK // 2) as i:
                for b in range(2):
                    pe.wait_ge(sq_ready, i * 2 + (b + 1))
                    pe.wait_ge(sd_ready, i * 2 + (b + 1))
                    block_matmul(blk_ps[b], ones[:, :], A, i, b, True, True).then_inc(norm_full, 1)
            pe.wait_ge(sd_ready, NBLK + 2)

        def dve_unit(dve):
            with dve.Fori(0, NBLK // 2) as i:
                for b in range(2):
                    dve.wait_ge(sd_ready, i * 2 + (b + 3))
                    nc.vector.tensor_scalar(SS[b][:, :], SS[b][:, :], NORM_EPS, None,
                                            ALU.max).then_inc(unit_chain, 1)
                    dve.wait_ge(unit_chain, i * 4 + (2 * b + 1))
                    nc.vector.tensor_copy(tick[:, 3:4], tick[:, 2:3])
                    nc.vector.reciprocal(SS[b][:, :], SS[b][:, :]).then_inc(unit_chain, 1)
                    dve.wait_ge(unit_chain, i * 4 + (2 * b + 2))
                    nc.vector.tensor_tensor(out=B[:, cols(i, b)], in0=B[:, cols(i, b)], in1=SS[b][:, :],
                                            op=ALU.mult).then_inc(scaled, 1)
            dve.wait_ge(scaled, NBLK + 2)

        def dve_times(dve, dst, other, op, tell, after=None):
            with dve.Fori(0, NBLK // 2) as i:
                for b in range(2):
                    if after is not None:
                        dve.wait_ge(after[0], after[1] + i * 2 + (b + 1))
                    nc.vector.tensor_tensor(out=dst[:, cols(i, b)], in0=dst[:, cols(i, b)],
                                            in1=other[:, cols(i, b)], op=op).then_inc(tell, 1)

        def dve_keep(dve, r):
            with dve.Fori(0, NBLK // 2) as i:
                for b in range(2):
                    dve.wait_ge(ss_ready, NBLK * r + i * 2 + (b + 1))
                    nc.vector.tensor_copy(A[:, cols(i, b)], SS[b][:, :]).then_inc(ss_kept, 1)
            dve.wait_ge(ss_kept, NBLK * (r + 1) + 2)

        chained = [0]

        def link(dve, ins):
            chained[0] += 1
            ins.then_inc(dve_chain, 1)
            dve.wait_ge(dve_chain, chained[0])

        def dve_scatter(dve):
            for b in range(2):
                nc.vector.memset(xwin[b][:, D:YW], 1.0).then_inc(xwin_ones, 1)
            for b in range(2):
                nc.vector.tensor_copy(col_slot[b][:, :], src_f[:, b * GT:(b + 1) * GT]).then_inc(col_ready, 1)
            with dve.Fori(0, G // 2) as i:
                for b in range(2):
                    at = lambda k, n: bass.ds(i * (2 * GT) + (b * GT + k), n)
                    dve.wait_ge(m_full, i * 2 + (b + 1))
                    build_sel(dve, onehot[b], at).then_inc(hot_ready, 1)
                    dve.wait_ge(kr_full, i * 2 + (b + 1))
                    dve.wait_ge(m_full, i * 2 + (b + 2))
                    nc.vector.tensor_tensor(
                        out=same, in0=keyrow_ps.rearrange("p (k e) -> p k e", k=GT),
                        in1=col_slot[b][:, :].unsqueeze(2).to_broadcast([128, GT, 128]),
                        op=ALU.is_equal).then_inc(same_ready, 1)
                    dve.wait_ge(same_ready, i * 2 + (b + 1))
                    step = lambda j: i * 8 + (4 * b + j)
                    nc.vector.tensor_tensor(out=before, in0=same,
                                            in1=earlier[:, :].unsqueeze(1).to_broadcast([128, GT, 128]),
                                            op=ALU.mult).then_inc(rank_chain, 1)
                    dve.wait_ge(rank_chain, step(1))
                    nc.vector.tensor_reduce(out=rank, in_=before, axis=AX.X, op=ALU.add).then_inc(rank_chain, 1)
                    nc.vector.tensor_scalar(to_row, col_slot[b][:, :], trash[:, :], None, ALU.subtract
                                            ).then_inc(rank_chain, 1)
                    dve.wait_ge(rank_chain, step(3))
                    nc.vector.scalar_tensor_tensor(out=to_row, in0=rank, scalar=0.0, in1=to_row,
                                                   op0=ALU.is_equal, op1=ALU.mult).then_inc(rank_chain, 1)
                    dve.wait_ge(rank_chain, step(4))
                    dve.wait_ge(v_kept, i * 2 + (b + 2))
                    nc.vector.tensor_scalar(idx_slot[b][:, :], to_row, trash[:, :], None, ALU.add
                                            ).then_inc(row_idx, 1)
                    nc.vector.tensor_copy(col_slot[b][:, :], src_f[:, tiles(i, b, 2)]).then_inc(col_ready, 1)

        def pe_scatter(pe):
            def key_rows(b):
                for k in range(GT):
                    last = nc.tensor.matmul(keyrow_ps[:, k * 128:(k + 1) * 128], bc(col_slot[b][:, k:k + 1], 128),
                                            ident[:, :], start=True, stop=True)
                last.then_inc(kr_full, 1)

            pe.wait_ge(xwin_ones, 2)
            pe.wait_ge(col_ready, 1)
            key_rows(0)
            with pe.Fori(0, G // 2) as i:
                for b in range(2):
                    pe.wait_ge(hot_ready, i * 2 + (b + 1))
                    pe.wait_ge(same_ready, i * 2 + (b + 1))
                    pe.wait_ge(m_kept, i * 2 + (b + 1))
                    for k in range(GT):
                        last = nc.tensor.matmul(m_ps[:, k * 128:(k + 1) * 128], onehot[b][:, k, :], same[:, k, :],
                                                start=True, stop=True)
                    last.then_inc(m_full, 1)
                    pe.wait_ge(col_ready, i * 2 + (b + 2))
                    key_rows(1 - b)
                    pe.wait_ge(m_kept, i * 2 + (b + 2))
                    pe.wait_ge(xwin_in[b], i * 16 + 16)
                    pe.wait_ge(v_kept, i * 2 + (b + 1))
                    for k in range(GT):
                        last = nc.tensor.matmul(v_ps[:, k, 0:YW], mcount[:, k, :], xwin[b], start=True, stop=True)
                    last.then_inc(v_full, 1)
            pe.wait_ge(v_kept, G + 1)

        def act_scatter(act):
            PER_COPY = 16 * GT // NCOPY

            def one_group(i, b):
                act.wait_ge(m_full, i * 2 + (b + 3))
                act.wait_ge(v_full, i * 2 + (b + 2))
                nc.scalar.activation(mcount, m_ps.rearrange("p (k e) -> p k e", k=GT), ACT.Copy).then_inc(m_kept, 1)
                act.wait_ge(v_full, i * 2 + (b + 3))
                if not isinstance(i, int):
                    for c in range(NCOPY):
                        act.wait_ge(scattered[c], i * (2 * PER_COPY) + PER_COPY * (b - 1))
                nc.scalar.activation(summed_rows[b], v_ps[:, :, 0:YW], ACT.Copy).then_inc(v_kept, 1)

            for b in range(2):
                one_group(0, b)
            with act.Fori(1, G // 2) as i:
                for b in range(2):
                    one_group(i, b)

        def pool_scatter(pool):
            added_to = [pool.alloc_register(f"added_to{c}") for c in range(NCOPY)]
            for c in range(NCOPY):
                pool.reg_mov(added_to[c], 16)

            def one_group(i, b):
                first = pool.snap(added_to[0], min_val=16, max_val=16 * T)
                pool.wait_ge(row_idx, i * 2 + (b + 1))
                pool.wait_ge(v_kept, i * 2 + (b + 2))
                for k in range(GT):
                    c = k % NCOPY
                    if k >= NCOPY or b or not isinstance(i, int):
                        pool.wait_ge(scattered[c], pool.snap(added_to[c], min_val=16, max_val=16 * T)
                                     if k else first)
                        pool.reg_add(added_to[c], added_to[c], 16)
                    nc.gpsimd.indirect_dma_start(
                        out=ysum[c], out_offset=bass.IndirectOffsetOnAxis(ap=idx_slot[b][:, k:k + 1], axis=0),
                        in_=summed_rows[b][:, k, :], in_offset=None, compute_op=ALU.add,
                    ).then_inc(scattered[c], 16)

            for b in range(2):
                one_group(0, b)
            with pool.Fori(1, G // 2) as i:
                for b in range(2):
                    one_group(i, b)

        def sp_scatter(sp):
            with sp.Fori(0, G // 2) as i:
                for b in range(2):
                    base = sp.value_load(base_i[0:1, bass.ds(i * 2 + b, 1)], min_val=0, max_val=N)
                    sp.wait_ge(v_full, i * 2 + (b + 1))
                    sp.dma_start(xwin[b][:, 0:D], table[bass.ds(base, W), :]).then_inc(xwin_in[b], 16)

        def sp_readback(sp):
            sp.wait_ge(v_kept, G + 1)
            for c in range(NCOPY):
                sp.wait_ge(scattered[c], 16 * T // NCOPY)
            with sp.Fori(0, NBLK // 2) as i:
                for b in range(2):
                    sp.wait_ge(parts_used, i * 2 + (b + 1))
                    for k in range(NCOPY):
                        sp.dma_start(parts[b][:, k * TPB * YW:(k + 1) * TPB * YW].rearrange("p (j f) -> p j f", j=TPB),
                                     ysum[k][cols(i, b), :].rearrange("(j p) f -> p j f", p=TN)
                                     ).then_inc(parts_in[b], 16)

        def dve_readback(dve):
            with dve.Fori(0, NBLK // 2) as i:
                for b in range(2):
                    step = lambda j: i * 6 + (3 * b + j)
                    dve.wait_ge(parts_in[b], i * (16 * NCOPY) + 16 * NCOPY)
                    nc.vector.tensor_reduce(out=ytot[b], in_=parts[b].rearrange("p (k m) -> p m k", k=NCOPY),
                                            axis=AX.X, op=ALU.add).then_inc(parts_used, 1)
                    dve.wait_ge(parts_used, i * 2 + (b + 3))
                    y3 = ytot[b].rearrange("p (j f) -> p j f", j=TPB)
                    nc.vector.tensor_scalar(ydeg[0:TN, b, :], y3[:, :, D], 1.0, None, ALU.max).then_inc(y_chain, 1)
                    dve.wait_ge(y_chain, step(1))
                    nc.vector.reciprocal(ydeg[0:TN, b, :], ydeg[0:TN, b, :]).then_inc(y_chain, 1)
                    dve.wait_ge(y_chain, step(2))
                    dve.wait_ge(yT_full, i * 2 + (b + 1))
                    nc.vector.tensor_tensor(out=yrow[b][0:TN, :, :], in0=y3[:, :, 0:D],
                                            in1=ydeg[0:TN, b, :].unsqueeze(2).to_broadcast([TN, TPB, D]),
                                            op=ALU.mult).then_inc(y_chain, 1)

        def pe_readback(pe):
            with pe.Fori(0, NBLK // 2) as i:
                for b in range(2):
                    pe.wait_ge(y_chain, i * 6 + (3 * b + 3))
                    pe.wait_ge(yT_kept, i * 2 + (b + 1))
                    for j in range(TPB):
                        last = nc.tensor.transpose(PS[:, 1024 * b + 128 * j:1024 * b + 128 * j + TN],
                                                   yrow[b][0:TN, j, :], ident[0:TN, 0:TN])
                    last.then_inc(yT_full, 1)
            pe.wait_ge(yT_kept, NBLK + 2)

        def act_readback(act):
            with act.Fori(0, NBLK // 2) as i:
                for b in range(2):
                    act.wait_ge(yT_full, i * 2 + (b + 3))
                    nc.scalar.activation(A[:, cols(i, b)].rearrange("p (j n) -> p j n", j=TPB),
                                         PS[:, 1024 * b:1024 * b + 128 * TPB].rearrange("p (j n) -> p j n", j=TPB)
                                         [:, :, 0:TN], ACT.Copy).then_inc(yT_kept, 1)

        def pool_general(pool, n, source):
            slots = pool.alloc_register(f"general_slots{n}")
            pool.reg_mov(slots, 3 * T * n + 3)
            with pool.Fori(0, T // 2) as i:
                for b in range(2):
                    pool.wait_ge(general_slots, pool.snap(slots, min_val=3, max_val=21 * T))
                    pool.reg_add(slots, slots, 3)
                    nc.gpsimd.indirect_dma_start(
                        out=gbuf[b][:, 0, :], out_offset=None, in_=source,
                        in_offset=bass.IndirectOffsetOnAxis(ap=idx_slot[b][:, 0:1], axis=0),
                    ).then_inc(gathered[b], 16)

        def pe_general(pe, n):
            with pe.Fori(0, T // 2) as i:
                for b in range(2):
                    pe.wait_ge(gathered[b], 16 * (T // 2) * n + i * 16 + 16)
                    nc.tensor.matmul(agg_ps[b], gbuf[b][:, 0, :], sel[b][:, 0, :], start=True, stop=True)
                    nc.tensor.matmul(extra_ps[b], bc(col_slot[b][:, 0:1], 128), ident[:, :],
                                     start=True, stop=True).then_inc(general_full, 1)
            pe.wait_ge(general_used, T * (n + 1))

        def dve_general(dve, n, keys, index, scale=None, extra=None, extra_cols=None, maximum=False,
                        start=None):
            nc.vector.memset(A[:, N if start is A else 0:N + W], -BIG if maximum else 0.0)
            if start is not None and start is not A:
                dve.drain()
                nc.vector.tensor_copy(A[:, 0:N], start[:, 0:N])
            if extra is not None:
                nc.vector.memset(extra[:, :], 0.0)
            dve.drain()
            with dve.Fori(0, T // 2) as i:
                for b in range(2):
                    t = bass.ds(i * 2 + b, 1)
                    nc.vector.tensor_copy(idx_slot[b][:, 0:1], index[:, t]).then_inc(general_slots, 1)
                    nc.vector.tensor_scalar(sel[b][:, 0, :], ident[:, :], ones[:, 0:1] if scale is None
                                            else scale[:, t], None, ALU.mult).then_inc(general_slots, 1)
                    nc.vector.tensor_copy(col_slot[b][:, 0:1], ones[:, 0:1] if extra_cols is None
                                          else extra_cols[:, t]).then_inc(general_slots, 1)
                    dve.wait_ge(general_full, T * n + i * 2 + (b + 1))
                    nc.vector.tensor_copy(tick[:, 3:4], tick[:, 2:3])
                    with dve.Fori(0, 128) as e:
                        key = dve.value_load(keys[0:1, bass.ds(i * 256 + e + b * 128, 1)], min_val=0, max_val=N)
                        col = bass.ds(key, 1)
                        nc.vector.tensor_tensor(out=A[:, col], in0=A[:, col], in1=agg_ps[b][:, bass.ds(e, 1)],
                                                op=ALU.max if maximum else ALU.add)
                        if extra is not None:
                            nc.vector.tensor_tensor(out=extra[:, col], in0=extra[:, col],
                                                    in1=extra_ps[b][:, bass.ds(e, 1)], op=ALU.add)
                        dve.drain()
                    dve.sem_inc(general_used, 1)
            if maximum:
                nc.vector.scalar_tensor_tensor(out=A[:, :], in0=A[:, :], scalar=-0.9 * BIG, in1=A[:, :],
                                               op0=ALU.is_gt, op1=ALU.mult)
                dve.drain()

        def either(eng, usual, general):
            with eng.If(flag[eng] == 0):
                usual()
            with eng.Else():
                general()

        def load_flag(eng):
            eng.wait_ge(flag_ready, 1)
            flag[eng] = eng.snap(eng.value_load(flag_i[0:1, 0:1], min_val=0, max_val=1))

        flag = {}

        @block.sync
        def _(sp):
            for dst, src in ((src_i[:, :], a["src_t"]), (ew[:, :], a["ew_t"]), (X[:, :], a["x_t"]), (weights[:, :, :], a["weights"]),
                             (vectors[:, :], a["vectors"]), (dst_i, a["dst_t"]), (next_i, a["dst_next_t"]),
                             (row_i, a["dst_rows"]), (prev_i, a["dst_prev_rows"]),
                             (key_i, a["src_key_t"])):
                sp.dma_start(dst, src).then_inc(loaded, 16)
            sp.wait_ge(setup_done, 1)
            sp.dma_start(start_penalty, row_pen).then_inc(pen_out, 16)
            sp.dma_start(table[N:NR, :].rearrange("(p r) f -> p (r f)", p=75), H[0:75, 0:2 * D]).then_inc(pen_out, 16)
            for k in range(NCOPY):
                zeroed = ysum[k].rearrange("a b -> (a b)").rearrange("(p c) -> p c", p=128)
                for c in range(5):
                    w = NR * YW // (128 * 5)
                    sp.dma_start(zeroed[:, c * w:(c + 1) * w], H[:, 0:w]).then_inc(ysum_zeroed, 16)
            sp.wait_ge(pen_out, 32)
            sp.wait_ge(ysum_zeroed, 16 * 5 * NCOPY)
            load_flag(sp)
            sp_rows(sp, 0, table)
            sp_rows(sp, 1, table)
            sp_rows(sp, 2, table)
            rows_written(sp, 3)
            with sp.If(flag[sp] == 0):
                sp_scatter(sp)
                sp_readback(sp)
            sp_rows(sp, 3, table)
            sp_rows(sp, 4, table)
            sp_rows(sp, 5, table)
            with sp.If(flag[sp] == 0):
                sp_max(sp)
            sp_rows(sp, 6, table)
            sp_rows(sp, 7, out)
            rows_written(sp, 8)

        @block.gpsimd
        def _(pool):
            nc.gpsimd.memset(ident[:, :], 1.0).then_inc(const_ready, 1)
            nc.gpsimd.memset(earlier[:, :], 1.0).then_inc(const_ready, 1)
            nc.gpsimd.iota(iota[:, :], pattern=[[1, W]], base=0, channel_multiplier=0,
                           allow_small_or_imprecise_dtypes=True).then_inc(const_ready, 1)
            nc.gpsimd.iota(trash[:, :], pattern=[[0, 1]], base=NR - 128, channel_multiplier=1,
                           allow_small_or_imprecise_dtypes=True).then_inc(const_ready, 1)
            pool.wait_ge(const_ready, 4)
            nc.gpsimd.affine_select(out=ident[:, :], in_=ident[:, :], compare_op=ALU.is_equal, fill=0.0, base=0,
                                    pattern=[[-1, 128]], channel_multiplier=1).then_inc(const_ready, 1)
            nc.gpsimd.affine_select(out=earlier[:, :], in_=earlier[:, :], compare_op=ALU.is_gt, fill=0.0, base=0,
                                    pattern=[[-1, 128]], channel_multiplier=1).then_inc(const_ready, 1)
            load_flag(pool)
            either(pool, lambda: pool_gather(pool, 0, a["x"]), lambda: pool_general(pool, 0, a["x"]))
            for q in (1, 2):
                rows_written(pool, q)
                either(pool, lambda: pool_gather(pool, q, table), lambda: pool_general(pool, q, table))
            rows_written(pool, 3)
            pool.wait_ge(ysum_zeroed, 16 * 5 * NCOPY)
            either(pool, lambda: pool_scatter(pool), lambda: pool_general(pool, 3, table))
            for q, r in ((3, 4), (4, 6), (5, 7)):
                rows_written(pool, r)
                either(pool, lambda: pool_gather(pool, q, table), lambda: pool_general(pool, q + 1, table))

        @block.scalar
        def _(act):
            act.wait_ge(pen_out, 32)
            load_flag(act)
            for m in range(3):
                act_linear(act, 2 * m, ACT.Identity, f"L0_b1_{m}", dst=B)
                act_batchnorm(act, 2 * m)
                act_affine(act, 2 * m, B, dst=A)
                act_linear(act, 2 * m + 1, ACT.Identity, f"L0_b2_{m}", dst=B)
                if m < 2:
                    act_batchnorm(act, 2 * m + 1)
                    act_affine(act, 2 * m + 1, B, ss=m)
            act_squares(act)
            act_rownorm(act, 0, 2, into=X)
            with act.If(flag[act] == 0):
                act_scatter(act)
                act_readback(act)
            act_linear(act, 6, ACT.Relu, "L1_b1", dst=B)
            act_linear(act, 7, ACT.Identity, "L1_b2", dst=A)
            act_rownorm(act, 1, 3, into=X)
            act_linear(act, 8, ACT.Identity, "L2_b_l", dst=B)
            act_batchnorm(act, 5)
            act_affine(act, 5, B, dst=A)
            act_rownorm(act, 2, 4, into=X)
            act_linear_rows(act, 9, 5, ACT.Relu, "L3_b_pool")
            with act.If(flag[act] == 0):
                act_max(act)
            act_linear(act, 10, ACT.Identity, "L3_b1", dst=B)
            act_rownorm(act, 3, 6, into=B, by_length=True)
            act_linear(act, 11, ACT.Relu, "L3_b2", dst=A)
            act_rownorm(act, 4, 7)

        @block.vector
        def _(dve):
            link(dve, nc.vector.memset(tick[:, 2:4], 0.0))
            for c in (summed, placed, msg_full, scanned, lin_taken, rows_full, rows_staged, ss_kept, back_full,
                      sd_ready, scaled, m_full, v_full, parts_used, yT_full, yT_kept):
                dve.sem_inc(c, 2)
            for c in (rev_kept, m_kept, v_kept):
                dve.sem_inc(c, 1)
            nc.vector.memset(ones[:, :], 1.0)
            nc.vector.memset(eps_bn[:, :], BN_EPS)
            nc.vector.memset(zero_c[:, :], 0.0)
            nc.vector.memset(scan[1][:, GE - 1:GE], 0.0)
            nc.vector.memset(keyloc[:, :], -1.0)
            nc.vector.memset(is_end[:, :], 0.0)
            link(dve, nc.vector.memset(H[:, :], 0.0))
            dve.wait_ge(loaded, 16 * 10)
            nc.vector.tensor_copy(src_f[:, :], key_i)
            link(dve, nc.vector.tensor_copy(dst_f[:, :], dst_i))
            nc.vector.tensor_copy(next_f, next_i)
            link(dve, nc.vector.tensor_reduce(out=least, in_=dst_f[:, :].rearrange("p (g k) -> p g k", k=GT),
                                              axis=AX.X, op=ALU.min))
            link(dve, nc.vector.tensor_reduce(out=most, in_=dst_f[:, :].rearrange("p (g k) -> p g k", k=GT),
                                              axis=AX.X, op=ALU.max))
            dve.sem_inc(lohi_done, 1)
            nc.vector.tensor_tensor(out=is_end[:, 0:T], in0=dst_f[:, :], in1=next_f, op=ALU.not_equal)
            link(dve, nc.vector.tensor_tensor(out=row_pen, in0=row_i, in1=prev_i, op=ALU.is_lt))
            link(dve, nc.vector.tensor_reduce(out=lohi[0:G, 2:3], in_=row_pen, axis=AX.X, op=ALU.add))
            link(dve, nc.vector.tensor_tensor(out=row_pen, in0=row_i, in1=prev_i, op=ALU.is_equal))
            link(dve, nc.vector.tensor_scalar(row_pen, row_pen, 1.0, BIG, ALU.subtract, ALU.mult))
            dve.sem_inc(setup_done, 1)
            dve.wait_ge(lohi_ps, 1)
            link(dve, nc.vector.tensor_reduce(out=lohi[0:G, 1:2], in_=PS[0:G, 128:256], axis=AX.X, op=ALU.max))
            link(dve, nc.vector.tensor_reduce(out=lohi[0:G, 0:1], in_=PS[0:G, 0:128], axis=AX.X, op=ALU.min))
            dve.sem_inc(lohi_done, 1)
            link(dve, nc.vector.tensor_tensor(out=lohi[0:G, 3:4], in0=lohi[0:G, 1:2], in1=lohi[0:G, 0:1],
                                              op=ALU.subtract))
            link(dve, nc.vector.tensor_scalar(lohi[0:G, 3:4], lohi[0:G, 3:4], float(W), lohi[0:G, 2:3],
                                              ALU.is_ge, ALU.add))
            dve.sem_inc(lohi_done, 1)
            dve.wait_ge(flag_ps, 1)
            link(dve, nc.vector.tensor_scalar(flag_i[:, :], PS[0:1, 1024:1025], 1.0, None, ALU.min))
            dve.sem_inc(flag_ready, 1)
            load_flag(dve)
            dve.wait_ge(base_ps, 1)
            link(dve, nc.vector.tensor_copy(base_i[:, :], PS[0:1, 512:512 + G]))
            link(dve, nc.vector.tensor_tensor(
                out=keyloc[:, 0:T].rearrange("p (g k) -> p g k", k=GT),
                in0=dst_f[:, :].rearrange("p (g k) -> p g k", k=GT),
                in1=PS[:, 512:512 + G].unsqueeze(2).to_broadcast([128, G, GT]), op=ALU.subtract))
            clears = 0
            for m in range(3):
                if m:
                    dve_keep(dve, m - 1)
                extra = DEG if m == 0 else None
                clears += 2 if m == 0 else 1
                h = A if m else X
                beside = (lambda i: invert(dve, DEG, 1.0, 0, i)) if m == 1 else None

                def general_sum():
                    dve_general(dve, m, a["dst_flat"], src_i, extra=extra, start=h)
                    if m == 1:
                        invert(dve, DEG, 1.0, 0)
                either(dve, lambda: dve_sum(dve, m, extra=extra, clears=clears, start=h, beside=beside),
                       general_sum)
                dve.sem_inc(lin_src, NBLK)
                dve_stats(dve, 2 * m, 2 * m, B)
                dve_batchnorm(dve, 2 * m, f"L0_g1_{m}", f"L0_be1_{m}")
                if m < 2:
                    dve_stats(dve, 2 * m + 1, 2 * m + 1, B)
                    dve_batchnorm(dve, 2 * m + 1, f"L0_gbn_{m}", f"L0_bbn_{m}")
            dve_unit(dve)
            dve_rownorm(dve, 0, 2, B, after=(scaled, 2))
            with dve.If(flag[dve] == 0):
                dve_scatter(dve)
                dve_readback(dve)
            with dve.Else():
                dve_general(dve, 3, a["src_flat"], dst_f, extra=H)
                nc.vector.tensor_scalar(H[:, :], H[:, :], 1.0, None, ALU.max)
                dve.drain()
                nc.vector.reciprocal(H[:, :], H[:, :])
                dve.drain()
                nc.vector.tensor_tensor(out=A[:, :], in0=A[:, :], in1=H[:, :], op=ALU.mult)
                dve.drain()
                dve.sem_inc(yT_kept, NBLK)
            dve.wait_ge(ss_kept, 3 * NBLK + 2)
            dve_rownorm(dve, 1, 3, A, after=(lin_taken, 7 * NBLK + 2))
            clears += 2
            either(dve, lambda: dve_sum(dve, 3, extra=WS, extra_cols=ew, clears=clears),
                   lambda: dve_general(dve, 4, a["dst_flat"], src_i, extra=WS, extra_cols=ew))
            dve_times(dve, A, DEG, ALU.mult, lin_src)
            dve_stats(dve, 8, 5, B)
            dve_batchnorm(dve, 5, "L2_gamma", "L2_beta")
            dve.wait_ge(ss_kept, 4 * NBLK + 2)
            dve_rownorm(dve, 2, 4, A, after=(aff_done, 3 * NBLK), twice=True)
            clears += 1
            def general_max():
                dve_general(dve, 5, a["dst_flat"], src_i, scale=ew, maximum=True)
                invert(dve, WS, NORM_EPS, 1)
            either(dve, lambda: dve_max(dve, MAX_PASS, clears, lambda i: invert(dve, WS, NORM_EPS, 1, i)),
                   general_max)
            dve_times(dve, A, WS, ALU.mult, lin_src)
            dve_rownorm(dve, 3, 6, B, after=(lin_taken, 10 * NBLK + 2), by_length=True)
            clears += 1
            def general_weighted():
                dve_general(dve, 6, a["dst_flat"], src_i, scale=ew)
                times_degree(dve)
            either(dve, lambda: dve_sum(dve, 5, scale=ew, clears=clears, beside=lambda i: times_degree(dve, i)),
                   general_weighted)
            dve_times(dve, A, WS, ALU.mult, lin_src)
            dve.wait_ge(ss_kept, 5 * NBLK + 2)
            dve_rownorm(dve, 4, 7, A, after=(lin_taken, 11 * NBLK + 2))

        @block.tensor
        def _(pe):
            pe.wait_ge(const_ready, 6)
            pe.wait_ge(loaded, 16 * 10)
            pe.wait_ge(lohi_done, 1)
            nc.tensor.transpose(PS[0:G, 0:128], least, ident[:, :])
            nc.tensor.transpose(PS[0:G, 128:256], most, ident[:, :]).then_inc(lohi_ps, 1)
            pe.wait_ge(lohi_done, 2)
            nc.tensor.matmul(PS[:, 512:512 + G], lohi[0:G, 0:1].to_broadcast([G, 128]), ident[0:G, 0:G],
                             start=True, stop=True).then_inc(base_ps, 1)
            pe.wait_ge(lohi_done, 3)
            nc.tensor.matmul(PS[0:1, 1024:1025], lohi[0:G, 3:4], ones[0:G, 0:1],
                             start=True, stop=True).then_inc(flag_ps, 1)
            load_flag(pe)
            for m in range(3):
                either(pe, lambda: pe_sum(pe, m, extra="degree" if m == 0 else None), lambda: pe_general(pe, m))
                pe_linear(pe, 2 * m, [(f"L0_W1_{m}", A)], after_src=(lin_src, m * NBLK))
                pe_linear(pe, 2 * m + 1, [(f"L0_W2_{m}", A)], after_src=(aff_done, m * NBLK))
                if m < 2:
                    pe_rows(pe, m)
            pe_squares(pe)
            pe_rownorm(pe, 0, 2, kept=2)
            with pe.If(flag[pe] == 0):
                pe_scatter(pe)
                pe_readback(pe)
            with pe.Else():
                pe_general(pe, 3)
            pe_linear(pe, 6, [("L1_W1", A)], after_src=(yT_kept, 2))
            pe_linear(pe, 7, [("L1_W2", B)], after_src=(lin_taken, 6 * NBLK + 2))
            pe_rownorm(pe, 1, 3, kept=3)
            either(pe, lambda: pe_sum(pe, 3, extra="weight"), lambda: pe_general(pe, 4))
            pe_linear(pe, 8, [("L2_W_l", A), ("L2_W_r", X)], after_src=(lin_src, 3 * NBLK))
            pe_rownorm(pe, 2, 4, kept=4)
            pe_linear_rows(pe, 9, 5, "L3_W_pool", X)
            either(pe, lambda: pe_max(pe, MAX_PASS), lambda: pe_general(pe, 5))
            pe_linear(pe, 10, [("L3_W1_self", X), ("L3_W1_neigh", A)], after_src=(lin_src, 4 * NBLK))
            pe_rownorm(pe, 3, 6, kept=5)
            either(pe, lambda: pe_sum(pe, 5), lambda: pe_general(pe, 6))
            pe_linear(pe, 11, [("L3_W2_self", B), ("L3_W2_neigh", A)], after_src=(lin_src, 5 * NBLK))
            pe_rownorm(pe, 4, 7)


WEIGHTS = {
    **{f"L0_W1_{m}": ("L0_gnn_W1", m, False) for m in range(3)},
    **{f"L0_W2_{m}": ("L0_gnn_W2", m, False) for m in range(3)},
    "L1_W1": ("L1_gnn_W1", None, True), "L1_W2": ("L1_gnn_W2", None, True),
    "L2_W_l": ("L2_gnn_W_l", None, True), "L2_W_r": ("L2_gnn_W_r", None, True),
    "L3_W_pool": ("L3_gnn_W_pool", None, False),
    "L3_W1_self": ("L3_gnn_W1_self", None, False), "L3_W1_neigh": ("L3_gnn_W1_neigh", None, False),
    "L3_W2_self": ("L3_gnn_W2_self", None, False), "L3_W2_neigh": ("L3_gnn_W2_neigh", None, False),
}
VECTORS = {
    **{f"L0_{v}_{m}": (f"L0_gnn_{v}", m) for v in ("b1", "g1", "be1", "b2") for m in range(3)},
    **{f"L0_{v}_{m}": (f"L0_gnn_{v}", m) for v in ("gbn", "bbn") for m in range(2)},
    "L1_b1": ("L1_gnn_b1", None), "L1_b2": ("L1_gnn_b2", None),
    "L2_b_l": ("L2_gnn_b_l", None), "L2_gamma": ("L2_gnn_gamma", None), "L2_beta": ("L2_gnn_beta", None),
    "L3_b_pool": ("L3_gnn_b_pool", None), "L3_b1": ("L3_gnn_b1", None), "L3_b2": ("L3_gnn_b2", None),
}


def kernel(**inputs):
    import concourse.bacc as bacc
    from concourse.bass_utils import run_bass_kernel_spmd

    def edges(x, tiles, pad):
        flat = np.full(tiles * 128, pad, x.dtype)
        flat[:x.size] = x
        return np.ascontiguousarray(flat.reshape(tiles, 128).T)

    x, dst = np.asarray(inputs["x"]), np.asarray(inputs["dst"])
    padded = np.full(EP + 2, N, dst.dtype)
    padded[0], padded[-1] = -1, -1
    padded[1:E + 1] = dst
    pick = lambda name, m: np.asarray(inputs[name]) if m is None else np.asarray(inputs[name])[m]
    arrays = {
        "x": x,
        "x_t": np.ascontiguousarray(x.T),
        "src_t": edges(np.asarray(inputs["src"]), T + 2 * GT, 0),
        "src_key_t": edges(np.asarray(inputs["src"]), T + 2 * GT, N),
        "src_flat": edges(np.asarray(inputs["src"]), T, N).T.reshape(1, EP).copy(),
        "dst_flat": padded[1:-1].reshape(1, EP).copy(),
        "ew_t": edges(np.asarray(inputs["edge_weight"]), T + GT, 0),
        "dst_t": edges(padded[1:-1], T, N),
        "dst_next_t": edges(padded[2:], T, N),
        "dst_rows": np.ascontiguousarray(padded[1:-1].reshape(G, GE)),
        "dst_prev_rows": np.ascontiguousarray(padded[:-2].reshape(G, GE)),
        "weights": np.ascontiguousarray(np.stack(
            [pick(n, m).T if t else pick(n, m) for n, m, t in WEIGHTS.values()], axis=1)),
        "vectors": np.ascontiguousarray(np.stack([pick(n, m) for n, m in VECTORS.values()], axis=1)),
    }
    nc = bacc.Bacc("TRN2", target_bir_lowering=False, num_devices=1)
    handles = {n: nc.dram_tensor(f"in_{n}", v.shape, mybir.dt.from_np(v.dtype), kind="ExternalInput").ap()
               for n, v in arrays.items()}
    out = nc.dram_tensor("out", (N, D), mybir.dt.float32, kind="ExternalOutput").ap()
    build_program(nc, handles, out)
    return run_bass_kernel_spmd(nc, [{f"in_{n}": v for n, v in arrays.items()}], core_ids=[0]).results[0]["out"]
```
